# Optimizing a Trainium2 kernel written in Bass

```python
import numpy as np
import jax
import jax.numpy as jnp

def _softmax(x, axis=-1):
    return jax.nn.softmax(x, axis=axis)

def _gelu(x):
    return jax.nn.gelu(x, approximate=True)

def _silu(x):
    return jax.nn.silu(x)

def _sigmoid(x):
    return jax.nn.sigmoid(x)

def _layernorm(x, axis=-1, eps=1e-05):
    m = jnp.mean(x, axis=axis, keepdims=True)
    v = jnp.var(x, axis=axis, keepdims=True)
    return (x - m) / jnp.sqrt(v + eps)

def _scatter_add(tgt, idx, src, axis=0):
    return tgt.at[idx].add(src)

def _segment_sum(src, seg, n):
    return jax.ops.segment_sum(src, seg, n)
kernel_name = 'mk_vit_tower_postln_d2_tok_img512_r4_1fc5e0'

def setup_inputs(seed: int=0):
    np.random.seed(seed)
    _w = jnp.asarray

    def _rec_inputs():
        import jax
        import jax.numpy as jnp
        _rk = jax.random.key(seed)
        x = -0.000356955 + 1 * jax.random.normal(jax.random.fold_in(_rk, 1), (32, 3, 96, 96), jnp.float32)
        return x
    x = _rec_inputs()

    def _L0_tok_setup():
        import jax, jax.numpy as jnp
        import numpy as np
        P = 16
        SHIFT = P // 2
        EPS = 1e-05

        def _shift2d(img, dy, dx):
            H, W = (img.shape[2], img.shape[3])
            pad = ((0, 0), (0, 0), (max(dy, 0), max(-dy, 0)), (max(dx, 0), max(-dx, 0)))
            z = jnp.pad(img, pad)
            return z[:, :, max(-dy, 0):max(-dy, 0) + H, max(-dx, 0):max(-dx, 0) + W]

        def _patchify(img):
            B, C, H, W = img.shape
            nH, nW = (H // P, W // P)
            t = img.reshape(B, C, nH, P, nW, P).transpose(0, 2, 4, 1, 3, 5)
            return t.reshape(B, nH * nW, C * P * P)
        key = jax.random.key(seed)
        ks = jax.random.split(key, 8)
        B, C, H, Wd = (128, 3, 224, 224)
        embed_dim = 128
        d_main = embed_dim // 2
        d_shift = embed_dim // 8
        fan_in = C * P * P
        std = 0.02
        x = jax.random.normal(ks[0], (B, C, H, Wd), dtype=jnp.float32)
        W_main = jax.random.normal(ks[1], (d_main, fan_in), dtype=jnp.float32) * std
        b_main = jnp.zeros((d_main,), dtype=jnp.float32)
        W_sx = jax.random.normal(ks[2], (d_shift, fan_in), dtype=jnp.float32) * std
        b_sx = jnp.zeros((d_shift,), dtype=jnp.float32)
        W_sy = jax.random.normal(ks[3], (d_shift, fan_in), dtype=jnp.float32) * std
        b_sy = jnp.zeros((d_shift,), dtype=jnp.float32)
        ln_g = jnp.ones((embed_dim,), dtype=jnp.float32)
        ln_b = jnp.zeros((embed_dim,), dtype=jnp.float32)
        return {'x': x, 'W_main': W_main, 'b_main': b_main, 'W_sx': W_sx, 'b_sx': b_sx, 'W_sy': W_sy, 'b_sy': b_sy, 'ln_g': ln_g, 'ln_b': ln_b}
    _L0_tok_all = _L0_tok_setup()
    _L0_tok_in = {k: v for k, v in _L0_tok_all.items() if k in ('W_main', 'b_main', 'W_sx', 'b_sx', 'W_sy', 'b_sy', 'ln_g', 'ln_b')}
    del _L0_tok_all

    def _L0_attn_setup():
        import jax, jax.numpy as jnp
        import numpy as np
        import math
        B, L, D, K = (1, 512, 128, 64)
        key = jax.random.key(seed)
        ks = jax.random.split(key, 12)
        w = lambda k, shape: jax.random.normal(k, shape, jnp.float32) * 0.02
        return {'x': jax.random.normal(ks[0], (B, L, D), jnp.float32), 'ke_w1': w(ks[1], (D, D)), 'ke_b1': jnp.zeros((D,), jnp.float32), 'ke_w2': w(ks[2], (D, K)), 'ke_b2': jnp.zeros((K,), jnp.float32), 'qe_w1': w(ks[3], (D, D)), 'qe_b1': jnp.zeros((D,), jnp.float32), 'qe_w2': w(ks[4], (D, K)), 'qe_b2': jnp.zeros((K,), jnp.float32), 'amp_w': w(ks[5], (D, K)), 'amp_b': jnp.zeros((K,), jnp.float32), 'v_w': w(ks[6], (D, D)), 'v_b': jnp.zeros((D,), jnp.float32), 'ln_g': jnp.ones((D,), jnp.float32), 'ln_b': jnp.zeros((D,), jnp.float32), 'out_w': w(ks[7], (D, D)), 'out_b': jnp.zeros((D,), jnp.float32)}
    _L0_attn_all = _L0_attn_setup()
    _L0_attn_in = {k: v for k, v in _L0_attn_all.items() if k in ('ke_w1', 'ke_b1', 'ke_w2', 'ke_b2', 'qe_w1', 'qe_b1', 'qe_w2', 'qe_b2', 'amp_w', 'amp_b', 'v_w', 'v_b', 'ln_g', 'ln_b', 'out_w', 'out_b')}
    del _L0_attn_all

    def _L0_ffn_setup():
        import jax, jax.numpy as jnp
        import numpy as np
        NUM_TILES = 64
        TPC = 8
        GRID = 16
        EPS = 1e-05
        key = jax.random.key(seed)
        ks = jax.random.split(key, 6)
        B, S, D, T, DH, G = (2, 256, 128, NUM_TILES, 128, GRID)
        x = jax.random.normal(ks[0], (B, S, D), dtype=jnp.float32)
        gamma = jnp.ones((D,), jnp.float32)
        beta = jnp.zeros((D,), jnp.float32)
        Wd = jax.random.normal(ks[1], (T, DH, D), dtype=jnp.float32) * 0.02
        spline_bases = jax.random.normal(ks[2], (T, DH, G), dtype=jnp.float32) * 0.1
        spline_slopes = jax.random.normal(ks[3], (T, DH, G), dtype=jnp.float32) * 0.1
        Wu = jax.random.normal(ks[4], (T, D, DH), dtype=jnp.float32) * 0.02
        scale = jnp.full((T,), 0.1, jnp.float32)
        return {'x': x, 'gamma': gamma, 'beta': beta, 'Wd': Wd, 'spline_bases': spline_bases, 'spline_slopes': spline_slopes, 'Wu': Wu, 'scale': scale}
    _L0_ffn_all = _L0_ffn_setup()
    _L0_ffn_in = {k: v for k, v in _L0_ffn_all.items() if k in ('gamma', 'beta', 'Wd', 'spline_bases', 'spline_slopes', 'Wu', 'scale')}
    del _L0_ffn_all

    def _L1_attn_setup():
        import jax, jax.numpy as jnp
        import numpy as np
        N_HEAD = 8
        D_MODEL = 128
        D_HEAD = 64
        N_ROLL = 2
        SLEN = 512
        BSZ = 8
        EPS = 1e-05
        SCALE = D_HEAD ** (-0.5)

        def _dpfp(x):
            x = jnp.concatenate([jax.nn.relu(x), jax.nn.relu(-x)], axis=-1)
            x = jnp.concatenate([x * jnp.roll(x, i, axis=-1) for i in range(1, N_ROLL + 1)], axis=-1)
            return x / x.sum(-1, keepdims=True)
        key = jax.random.key(seed)
        k1, k2, k3 = jax.random.split(key, 3)
        h = jax.random.normal(k1, (SLEN, BSZ, D_MODEL), dtype=jnp.float32)
        W_qkvb = jax.random.normal(k2, (N_HEAD * (3 * D_HEAD + 1), D_MODEL), dtype=jnp.float32) * 0.02
        W_o = jax.random.normal(k3, (D_MODEL, N_HEAD * D_HEAD), dtype=jnp.float32) * 0.02
        ln_g = jnp.ones((D_MODEL,), dtype=jnp.float32)
        ln_b = jnp.zeros((D_MODEL,), dtype=jnp.float32)
        return {'h': h, 'W_qkvb': W_qkvb, 'W_o': W_o, 'ln_g': ln_g, 'ln_b': ln_b}
    _L1_attn_all = _L1_attn_setup()
    _L1_attn_in = {k: v for k, v in _L1_attn_all.items() if k in ('W_qkvb', 'W_o', 'ln_g', 'ln_b')}
    del _L1_attn_all

    def _L1_ffn_setup():
        import jax, jax.numpy as jnp
        import numpy as np
        E = 8
        K = 1
        D = 128
        I = 512
        B, T = (2, 512)
        key = jax.random.key(seed)
        ks = jax.random.split(key, 7)
        s = 0.02
        x = jax.random.normal(ks[0], (B, T, D), jnp.float32)
        gate_w = jax.random.normal(ks[1], (E, D), jnp.float32) * s
        w1 = jax.random.normal(ks[2], (E, I, D), jnp.float32) * s
        w2 = jax.random.normal(ks[3], (E, D, I), jnp.float32) * s
        w3 = jax.random.normal(ks[4], (E, I, D), jnp.float32) * s
        sw1 = jax.random.normal(ks[5], (I, D), jnp.float32) * s
        sw2 = jax.random.normal(ks[6], (D, I), jnp.float32) * s
        return {'x': x, 'gate_w': gate_w, 'w1': w1, 'w2': w2, 'w3': w3, 'sw1': sw1, 'sw2': sw2}
    _L1_ffn_all = _L1_ffn_setup()
    _L1_ffn_in = {k: v for k, v in _L1_ffn_all.items() if k in ('gate_w', 'w1', 'w2', 'w3', 'sw1', 'sw2')}
    del _L1_ffn_all
    return {'x': x, 'L0_tok_W_main': _L0_tok_in['W_main'], 'L0_tok_b_main': _L0_tok_in['b_main'], 'L0_tok_W_sx': _L0_tok_in['W_sx'], 'L0_tok_b_sx': _L0_tok_in['b_sx'], 'L0_tok_W_sy': _L0_tok_in['W_sy'], 'L0_tok_b_sy': _L0_tok_in['b_sy'], 'L0_tok_ln_g': _L0_tok_in['ln_g'], 'L0_tok_ln_b': _L0_tok_in['ln_b'], 'L0_attn_ke_w1': _L0_attn_in['ke_w1'], 'L0_attn_ke_b1': _L0_attn_in['ke_b1'], 'L0_attn_ke_w2': _L0_attn_in['ke_w2'], 'L0_attn_ke_b2': _L0_attn_in['ke_b2'], 'L0_attn_qe_w1': _L0_attn_in['qe_w1'], 'L0_attn_qe_b1': _L0_attn_in['qe_b1'], 'L0_attn_qe_w2': _L0_attn_in['qe_w2'], 'L0_attn_qe_b2': _L0_attn_in['qe_b2'], 'L0_attn_amp_w': _L0_attn_in['amp_w'], 'L0_attn_amp_b': _L0_attn_in['amp_b'], 'L0_attn_v_w': _L0_attn_in['v_w'], 'L0_attn_v_b': _L0_attn_in['v_b'], 'L0_attn_ln_g': _L0_attn_in['ln_g'], 'L0_attn_ln_b': _L0_attn_in['ln_b'], 'L0_attn_out_w': _L0_attn_in['out_w'], 'L0_attn_out_b': _L0_attn_in['out_b'], 'L0_ffn_gamma': _L0_ffn_in['gamma'], 'L0_ffn_beta': _L0_ffn_in['beta'], 'L0_ffn_Wd': _L0_ffn_in['Wd'], 'L0_ffn_spline_bases': _L0_ffn_in['spline_bases'], 'L0_ffn_spline_slopes': _L0_ffn_in['spline_slopes'], 'L0_ffn_Wu': _L0_ffn_in['Wu'], 'L0_ffn_scale': _L0_ffn_in['scale'], 'L1_attn_W_qkvb': _L1_attn_in['W_qkvb'], 'L1_attn_W_o': _L1_attn_in['W_o'], 'L1_attn_ln_g': _L1_attn_in['ln_g'], 'L1_attn_ln_b': _L1_attn_in['ln_b'], 'L1_ffn_gate_w': _L1_ffn_in['gate_w'], 'L1_ffn_w1': _L1_ffn_in['w1'], 'L1_ffn_w2': _L1_ffn_in['w2'], 'L1_ffn_w3': _L1_ffn_in['w3'], 'L1_ffn_sw1': _L1_ffn_in['sw1'], 'L1_ffn_sw2': _L1_ffn_in['sw2']}

def reference(x, L0_tok_W_main, L0_tok_b_main, L0_tok_W_sx, L0_tok_b_sx, L0_tok_W_sy, L0_tok_b_sy, L0_tok_ln_g, L0_tok_ln_b, L0_attn_ke_w1, L0_attn_ke_b1, L0_attn_ke_w2, L0_attn_ke_b2, L0_attn_qe_w1, L0_attn_qe_b1, L0_attn_qe_w2, L0_attn_qe_b2, L0_attn_amp_w, L0_attn_amp_b, L0_attn_v_w, L0_attn_v_b, L0_attn_ln_g, L0_attn_ln_b, L0_attn_out_w, L0_attn_out_b, L0_ffn_gamma, L0_ffn_beta, L0_ffn_Wd, L0_ffn_spline_bases, L0_ffn_spline_slopes, L0_ffn_Wu, L0_ffn_scale, L1_attn_W_qkvb, L1_attn_W_o, L1_attn_ln_g, L1_attn_ln_b, L1_ffn_gate_w, L1_ffn_w1, L1_ffn_w2, L1_ffn_w3, L1_ffn_sw1, L1_ffn_sw2):
    import jax
    import jax.numpy as jnp

    def _L0_tok_ref(x, W_main, b_main, W_sx, b_sx, W_sy, b_sy, ln_g, ln_b):
        import jax, jax.numpy as jnp
        import numpy as np
        P = 16
        SHIFT = P // 2
        EPS = 1e-05

        def _shift2d(img, dy, dx):
            H, W = (img.shape[2], img.shape[3])
            pad = ((0, 0), (0, 0), (max(dy, 0), max(-dy, 0)), (max(dx, 0), max(-dx, 0)))
            z = jnp.pad(img, pad)
            return z[:, :, max(-dy, 0):max(-dy, 0) + H, max(-dx, 0):max(-dx, 0) + W]

        def _patchify(img):
            B, C, H, W = img.shape
            nH, nW = (H // P, W // P)
            t = img.reshape(B, C, nH, P, nW, P).transpose(0, 2, 4, 1, 3, 5)
            return t.reshape(B, nH * nW, C * P * P)

        def proj(img, W, b):
            return jnp.einsum('bnf,of->bno', _patchify(img), W) + b
        main = proj(x, W_main, b_main)
        xl = proj(_shift2d(x, 0, -SHIFT), W_sx, b_sx)
        xr = proj(_shift2d(x, 0, SHIFT), W_sx, b_sx)
        yu = proj(_shift2d(x, -SHIFT, 0), W_sy, b_sy)
        yd = proj(_shift2d(x, SHIFT, 0), W_sy, b_sy)
        tok = jnp.concatenate([main, xl, xr, yu, yd], axis=-1)
        mu = jnp.mean(tok, axis=-1, keepdims=True)
        var = jnp.mean(jnp.square(tok - mu), axis=-1, keepdims=True)
        return (tok - mu) * jax.lax.rsqrt(var + EPS) * ln_g + ln_b

    def _L0_attn_ref(x, ke_w1, ke_b1, ke_w2, ke_b2, qe_w1, qe_b1, qe_w2, qe_b2, amp_w, amp_b, v_w, v_b, ln_g, ln_b, out_w, out_b):
        import jax, jax.numpy as jnp
        import numpy as np
        import math
        B, L, D, K = (1, 512, 128, 64)
        Bx, Lx, Dx = x.shape
        Kx = amp_w.shape[1]
        gelu = lambda t: jax.nn.gelu(t, approximate=False)
        key_phase = jnp.tanh(gelu(x @ ke_w1 + ke_b1) @ ke_w2 + ke_b2) * math.pi
        query_phase = jnp.tanh(gelu(x @ qe_w1 + qe_b1) @ qe_w2 + qe_b2) * math.pi
        amp = jax.nn.softplus(x @ amp_w + amp_b) + 0.1
        V = x @ v_w + v_b
        kr = amp * jnp.cos(key_phase)
        ki = amp * jnp.sin(key_phase)
        qr = amp * jnp.cos(query_phase)
        qi = amp * jnp.sin(query_phase)
        mem_r = jnp.cumsum(kr[..., None] * V[..., None, :], axis=1)
        mem_i = jnp.cumsum(ki[..., None] * V[..., None, :], axis=1)
        retrieved = jnp.einsum('blkd,blk->bld', mem_r, qr) + jnp.einsum('blkd,blk->bld', mem_i, qi)
        positions = jnp.arange(1, Lx + 1, dtype=jnp.float32)
        norm = jnp.sqrt(positions * Kx)[None, :, None]
        retrieved = retrieved / norm
        mu = retrieved.mean(-1, keepdims=True)
        var = ((retrieved - mu) ** 2).mean(-1, keepdims=True)
        rn = (retrieved - mu) / jnp.sqrt(var + 1e-05) * ln_g + ln_b
        return x + rn @ out_w + out_b

    def _L0_ffn_ref(x, gamma, beta, Wd, spline_bases, spline_slopes, Wu, scale):
        import jax, jax.numpy as jnp
        import numpy as np
        NUM_TILES = 64
        TPC = 8
        GRID = 16
        EPS = 1e-05
        B, S, D = x.shape
        T, DH, _ = Wd.shape
        C = T // TPC
        N = B * S
        mu = x.mean(-1, keepdims=True)
        var = ((x - mu) ** 2).mean(-1, keepdims=True)
        xn = (x - mu) * jax.lax.rsqrt(var + EPS) * gamma + beta
        xf = xn.reshape(N, D)
        tile_sigs = jnp.sign(Wd.mean(axis=1))
        cluster_sigs = jnp.sign(tile_sigs.reshape(C, TPC, D).mean(1))
        in_sigs = jnp.sign(xf)
        best_c = jnp.argmax(in_sigs @ cluster_sigs.T, axis=-1)
        tile_scores = (in_sigs @ tile_sigs.T).reshape(N, C, TPC)
        sc = jnp.take_along_axis(tile_scores, best_c[:, None, None], axis=1)[:, 0, :]
        local_best = jnp.argmax(sc, axis=-1)
        tidx = best_c * TPC + local_best
        h = jnp.einsum('nd,nhd->nh', xf, Wd[tidx])
        hn = jax.nn.sigmoid(h)
        idx = jnp.clip((hn * GRID).astype(jnp.int32), 0, GRID - 1)
        base = jnp.take_along_axis(spline_bases[tidx], idx[..., None], axis=-1)[..., 0]
        slope = jnp.take_along_axis(spline_slopes[tidx], idx[..., None], axis=-1)[..., 0]
        local_pos = hn * GRID - idx.astype(h.dtype)
        hs = base + slope * local_pos
        y = jnp.einsum('nh,ndh->nd', hs, Wu[tidx]) * scale[tidx][:, None]
        return x + y.reshape(B, S, D)

    def _L1_attn_ref(h, W_qkvb, W_o, ln_g, ln_b):
        import jax, jax.numpy as jnp
        import numpy as np
        N_HEAD = 8
        D_MODEL = 128
        D_HEAD = 64
        N_ROLL = 2
        SLEN = 512
        BSZ = 8
        EPS = 1e-05
        SCALE = D_HEAD ** (-0.5)

        def _dpfp(x):
            x = jnp.concatenate([jax.nn.relu(x), jax.nn.relu(-x)], axis=-1)
            x = jnp.concatenate([x * jnp.roll(x, i, axis=-1) for i in range(1, N_ROLL + 1)], axis=-1)
            return x / x.sum(-1, keepdims=True)
        slen, bsz, _ = h.shape
        qkvb = jnp.einsum('lbd,ed->lbe', h, W_qkvb).reshape(slen, bsz, N_HEAD, 3 * D_HEAD + 1)
        q, k, v, beta = jnp.split(qkvb, [D_HEAD, 2 * D_HEAD, 3 * D_HEAD], axis=-1)
        beta = jax.nn.sigmoid(beta)
        q = _dpfp(q)
        k = _dpfp(k)
        denom_acc = jnp.cumsum(k, axis=0)
        denominator = jnp.einsum('lbhd,lbhd->lbh', denom_acc, q)[..., None]
        dk = 2 * N_ROLL * D_HEAD
        W0 = jnp.zeros((bsz, N_HEAD, dk, D_HEAD), dtype=h.dtype)

        def step(W, inp):
            qt, kt, vt, bt = inp
            v_old = jnp.einsum('bhd,bhde->bhe', kt, W)
            delta = bt * (vt - v_old)
            W = W + jnp.einsum('bhd,bhe->bhde', kt, delta)
            out = jnp.einsum('bhd,bhde->bhe', qt, W)
            return (W, out)
        _, out = jax.lax.scan(step, W0, (q, k, v, beta))
        out = SCALE * out / (denominator + EPS)
        out = out.reshape(slen, bsz, N_HEAD * D_HEAD)
        attn_out = jnp.einsum('lbe,de->lbd', out, W_o)
        x = h + attn_out
        mu = x.mean(-1, keepdims=True)
        var = x.var(-1, keepdims=True)
        return (x - mu) * jax.lax.rsqrt(var + EPS) * ln_g + ln_b

    def _L1_ffn_ref(x, gate_w, w1, w2, w3, sw1, sw2):
        import jax, jax.numpy as jnp
        import numpy as np
        E = 8
        K = 1
        D = 128
        I = 512
        B, T = (2, 512)
        xf = x.reshape(-1, D)
        logits = xf @ gate_w.T
        wts, idx = jax.lax.top_k(logits, K)
        wts = jax.nn.softmax(wts, axis=-1)
        comb = jnp.einsum('nke,nk->ne', jax.nn.one_hot(idx, E, dtype=xf.dtype), wts)
        h = jax.nn.silu(jnp.einsum('nd,eid->nei', xf, w1)) * jnp.einsum('nd,eid->nei', xf, w3)
        y = jnp.einsum('nei,edi->nd', h * comb[:, :, None], w2)
        y = y + jax.nn.gelu(xf @ sw1.T, approximate=False) @ sw2.T
        return y.reshape(x.shape)
    h = _L0_tok_ref(x, L0_tok_W_main, L0_tok_b_main, L0_tok_W_sx, L0_tok_b_sx, L0_tok_W_sy, L0_tok_b_sy, L0_tok_ln_g, L0_tok_ln_b)
    h = _layernorm(h + _L0_attn_ref(h, L0_attn_ke_w1, L0_attn_ke_b1, L0_attn_ke_w2, L0_attn_ke_b2, L0_attn_qe_w1, L0_attn_qe_b1, L0_attn_qe_w2, L0_attn_qe_b2, L0_attn_amp_w, L0_attn_amp_b, L0_attn_v_w, L0_attn_v_b, L0_attn_ln_g, L0_attn_ln_b, L0_attn_out_w, L0_attn_out_b), axis=-1)
    h = _layernorm(h + _L0_ffn_ref(h, L0_ffn_gamma, L0_ffn_beta, L0_ffn_Wd, L0_ffn_spline_bases, L0_ffn_spline_slopes, L0_ffn_Wu, L0_ffn_scale), axis=-1)
    h = _layernorm(h + _L1_attn_ref(h, L1_attn_W_qkvb, L1_attn_W_o, L1_attn_ln_g, L1_attn_ln_b), axis=-1)
    h = _layernorm(h + _L1_ffn_ref(h, L1_ffn_gate_w, L1_ffn_w1, L1_ffn_w2, L1_ffn_w3, L1_ffn_sw1, L1_ffn_sw2), axis=-1)
    return h

_drawn_inputs = setup_inputs


def setup_inputs(seed=0):
    import zlib

    import numpy as np

    out = dict(_drawn_inputs(seed))
    spreads = {'L0_tok_b_main': (0.0, 0.1),
     'L0_tok_b_sx': (0.0, 0.1),
     'L0_tok_b_sy': (0.0, 0.1),
     'L0_tok_ln_g': (1.0, 0.2),
     'L0_tok_ln_b': (0.0, 0.1),
     'L0_attn_ke_b1': (0.0, 0.8),
     'L0_attn_ke_b2': (0.0, 0.8),
     'L0_attn_qe_b1': (0.0, 0.8),
     'L0_attn_qe_b2': (0.0, 0.8),
     'L0_attn_amp_b': (0.0, 0.8),
     'L0_attn_v_b': (0.0, 0.1),
     'L0_attn_ln_g': (1.0, 0.6),
     'L0_attn_ln_b': (0.0, 0.712),
     'L0_attn_out_b': (0.0, 0.1),
     'L0_ffn_gamma': (1.0, 0.6),
     'L0_ffn_beta': (0.0, 0.8),
     'L0_ffn_scale': (0.10000000149011612, 0.6),
     'L1_attn_ln_g': (1.0, 0.2),
     'L1_attn_ln_b': (0.0, 0.1)}
    factors = {'L0_attn_ke_w1': 8.0,
     'L0_attn_ke_w2': 8.0,
     'L0_attn_qe_w1': 8.0,
     'L0_attn_qe_w2': 8.0,
     'L0_attn_amp_w': 8.0,
     'L0_ffn_Wd': 8.0,
     'L0_ffn_spline_bases': 8.0,
     'L0_ffn_spline_slopes': 8.0,
     'L0_ffn_Wu': 8.0,
     'L1_attn_W_qkvb': 8.0,
     'L1_attn_W_o': 8.0,
     'L1_ffn_gate_w': 5.231,
     'L1_ffn_w1': 4.878,
     'L1_ffn_w2': 4.846,
     'L1_ffn_w3': 4.877}
    for name, (base, spread) in spreads.items():
        noise = np.random.default_rng([zlib.crc32(name.encode()), seed]).standard_normal(out[name].shape)
        drawn = base * np.exp(spread * noise) if base else spread * noise
        out[name] = jnp.asarray(drawn.astype(out[name].dtype))
    for name, factor in factors.items():
        out[name] = (out[name] * factor).astype(out[name].dtype)
    return out
```

```python
from contextlib import ExitStack

import concourse.bass as bass
from concourse import mybir
from concourse.alu_op_type import AluOpType as ALU

F32 = mybir.dt.float32
BF16 = mybir.dt.bfloat16
I32 = mybir.dt.int32
U8 = mybir.dt.uint8
ACT = mybir.ActivationFunctionType
X = mybir.AxisListType.X

D = 128
NIMG, NPATCH = 32, 36
TI = 11
PI = 3 * NPATCH
NI = TI * PI
NT = 9
N = NT * 128
IMG = 12 * 12
KF = 96
NBLK = (NIMG + 1) * IMG
CH = 396
EPS = 1e-5
PI32 = 3.1415927410125732
BELOW1 = 0.99999994
E0, E1 = 64, 8
GRID = 16
NH, HD = 8, 64
INNER = 512
K0, K1 = E0 + NT - 1, E1 + NT - 1
TILES4 = [(0, 4), (4, 8), (8, 11)]
TILES9 = [(0, 4), (4, 8), (8, 9)]

CONST = [("ident", 128), ("maskimg", PI), ("maskN", 128), ("maskC", 128), ("maskS", 128), ("triS", 128), ("triI", 128),
         ("slot", N), ("tile_end", 8), ("expert1", E0), ("invnorm", 1), ("sin_scale", 1), ("sin_bias", 1), ("kcol", 1),
         ("slotcol", NT), ("keybias", E0), ("prefer", E1), ("ecol", 1), ("one", 1)]
ROWS = ["tok_g", "tok_b", "v_b", "out_b", "l1_g", "l1_b"]
COLS = ["tok_bias", "ke_b1", "qe_b1", "ke_b2", "qe_b2", "amp_b", "ln_g", "ln_b", "gamma", "beta"]


def places():
    at, o = {}, 0
    for n, w in CONST:
        at[n] = (o, o + w)
        o += w
    return at, o


CAT, NCONST = places()


def vit_kernel(nc, A, out, stop=99, dbg=None):
    with ExitStack() as ctx:
        def sb(name, shape, dt=F32):
            return ctx.enter_context(nc.sbuf_tensor(name, shape, dt))

        cst = sb("cst", [128, NCONST])
        C = {n: cst[:, a:b] for n, (a, b) in CAT.items()}
        rows = sb("rows", [128, len(ROWS) * 128])
        R = {n: rows[:, i * 128:(i + 1) * 128] for i, n in enumerate(ROWS)}
        scale_row = sb("scale_row", [128, E0])
        cols = sb("cols", [128, len(COLS)])
        Cc = {n: cols[:, i:i + 1] for i, n in enumerate(COLS)}
        regA = sb("regA", [128, 2 * NBLK])
        blocks = regA[0:KF, :].rearrange("p (k n) -> p k n", k=2)
        tab = regA[:, 0:4096]
        tab_hi = regA[:, 4096:6144].bitcast(BF16)
        tab_lo = regA[0:E0, 6144:8192].bitcast(BF16)
        regW = sb("regW", [128, 2 * E0 * 128])
        wd, wu = regW[:, 0:E0 * 128], regW[:, E0 * 128:]
        W1 = E1 * INNER
        w1, w3, w2 = regW[:, 0:W1], regW[:, W1:2 * W1], regW[:, 2 * W1:3 * W1]
        sw1, sw2 = regW[:, 3 * W1:3 * W1 + INNER], regW[:, 3 * W1 + INNER:3 * W1 + 2 * INNER]
        gate = sb("gate", [128, E1])
        tokw = sb("tokw", [KF, 8 * 256])
        attw = sb("attw", [128, 7 * 128])
        qkvw = sb("qkvw", [128, 3 * 512 + 8])
        wo = sb("wo", [128, 4 * 128])
        B = [sb(f"B{i}", [128, NI]) for i in range(6)]
        HA = sb("HA", [128, TI, 128])
        HB = sb("HB", [128, TI, 128])
        stats = sb("stats", [128, TI, 6])
        mv = sb("mv", [128, TI, 2])
        rstd = sb("rstd", [128, TI])
        mhalf = sb("mhalf", [128, TI])
        zb = sb("zb", [128, 512], BF16)
        oneb = sb("oneb", [128, 128], BF16)
        trib = sb("trib", [128, 128], BF16)
        ecolb = sb("ecolb", [128, 1], BF16)
        sgT = sb("sgT", [128, N], BF16)
        tsum = sb("tsum", [128, E0])
        csum = sb("csum", [128, 8])
        tsig8 = sb("tsig8", [128, E0], BF16)
        csigb = sb("csigb", [128, E0], BF16)
        key = sb("key", [128, NT, E0])
        kmax = sb("kmax", [128, NT])
        wtop = sb("wtop", [128, NT])
        oh = sb("oh", [128, NT, 2, E0], BF16)
        rk = sb("rk", [128, NT, E0])
        small = sb("small", [128, 16])
        srow = sb("srow", [128, E0])
        pos = sb("pos", [128, NT])
        ohs = sb("ohs", [128, N], BF16)
        k64 = sb("k64", [128, 6, E0])
        erow = sb("erow", [128, K0])
        offs = sb("offs", [128, 2, K0], I32)
        xm = sb("xm", [128, 4, 128])
        scl = sb("scl", [128, NT])
        masks = sb("masks", [128, 2, N], U8)
        def heads(t):
            return t[:, 0:NH * 128].rearrange("p (h f) -> p h f", h=NH)

        feat = regA[:, 0:4096].rearrange("p (v h f) -> p v h f", v=2, h=16)
        featT = regA[:, 4096:8192].rearrange("p (h v f) -> p h v f", h=NH, v=2)
        vals = regA[:, 8192:8704].rearrange("p (h e) -> p h e", h=NH)
        outs = regA[:, 8704:9216].rearrange("p (h e) -> p h e", h=NH)
        relus = regW[:, 13312:13312 + 16 * 130].rearrange("p (h f) -> p h f", h=16)
        rhs_v = regW[:, 15392:15904].rearrange("p (h e) -> p h e", h=NH)
        delta = B[0][:, 0:NH * 65].rearrange("p (h e) -> p h e", h=NH)
        resid = B[0][:, 520:520 + 512].rearrange("p (h e) -> p h e", h=NH)
        nt, ct, smm, nn, n2 = (heads(B[i]) for i in range(1, 6))
        ww, n2t = heads(sb("ww", [128, NH * 128])), heads(sb("n2t", [128, NH * 128]))
        sums = sb("sums", [128, 16])
        hsc = sb("hsc", [128, 6, NH])
        gs = regA[:, 0:4 * N]
        sg = regA[:, 4608:5632].rearrange("p (u i) -> p u i", u=2)
        gg = regA[:, 5632:6656].rearrange("p (u i) -> p u i", u=2)
        gT = regA[:, 6656:7680].rearrange("p (u i) -> p u i", u=2)
        ps = ctx.enter_context(nc.psum_tensor("ps", [128, 4096], F32))

        def bank(b, n=512, p=128):
            return ps[0:p, b * 512:b * 512 + n]

        S = {}

        def sems(*names):
            for n in names:
                S[n] = ctx.enter_context(nc.semaphore(n))

        sems("in_const", "in_tok", "in_blocks0", "in_blocks1", "in_blocks2", "in_wd", "in_wu", "in_att", "in_tab", "in_qkv", "in_ffn", "stored")
        sems("dve_step", "act_step", "pool_step", "consts_made", "var_ready", "rstd_ready")
        sems("tok_ps", "tok_own", "tok_used", "h0_ready", "job_ps", "job_used", "z0_ready", "phase_held", "kq_ready", "score_ready",
             "retr_ready", "h1_ready", "h1b_ready", "z1_ready", "dve_h1b", "tab_rest", "y_final", "sgT_ready", "sig_ready", "key_ps", "key_used")
        sems("oh_ready", "rank_ps", "cnt_ready", "start_ps", "route_cols", "rows_ps", "pair_cols", "pairs_ps", "pairs_ready",
             "perm_made", "perm_used", "sorted_ps", "sorted_ready", "xm_ready", "xm_used", 
             "accs_copied", "hT_ps", "hn_ready", "posrow_ready")
        sems("tab_split", "tab_ps", "tab_used", "mask_ready", "mask_used", "hs_ready", "h2_ready", "h2T_ready", "rows_used")
        sems("xst_ready", "qkv_ps", "relu_done", "vb_done", "prod_done", "ft_ps", "ft_done", "gram_ps", "nt_done", "cs_done",
             "n_ps", "n_done", "w_done", "n2_ps", "n2_done", "a_ps", "a_done", "n4_done", "x_ps", "x8_done", "e_ps",
             "d_done", "t_ps", "q_done", "o_ps", "o_done", "ot_ps", "ot_done", "y_ps", "y_done", "l1_step", "xT_ps", "xT_done", "rv_done")
        sems("h3_ready", "h3T_ready", "gate_ps", "s1_ps", "s1_used", "sh_ps", "up_ps", "silu_done", "up_used", "g_done",
             "gT_ps", "gT_done", "y1_ps", "h3T_ps", "top_ready", "wtop_exp", "es_copied")
        block = ctx.enter_context(nc.Block())
        count = {}

        def post(ins, name):
            ins.then_inc(S[name], 1)
            count[name] = count.get(name, 0) + 1

        def done(eng, ins, name):
            post(ins, name)
            eng.wait_ge(S[name], count[name])

        J = {}
        jn = 0
        for what in ["tokT", "h0T", "w1k", "w1q", "amp", "w2k", "w2q", "v", "score", "retr", "rnT", "att", "h1T", "h1B", "z1T"]:
            J[what] = jn
            jn += 3

        def job_bank(n):
            return ((n + 6) % 8) * 512

        PER = dict(xst_ready=1, xT_ps=1, xT_done=1, qkv_ps=1, relu_done=1, vb_done=1, prod_done=1, ft_ps=8, ft_done=8, gram_ps=2,
                   nt_done=2, cs_done=2, n_ps=2, n_done=2, w_done=2, n2_ps=2, n2_done=2, a_ps=2, a_done=2, n4_done=2, x_ps=2,
                   x8_done=2, e_ps=8, d_done=8, t_ps=6, q_done=6, o_ps=2, o_done=2, ot_ps=1, ot_done=1, y_ps=1, y_done=1, rv_done=1)
        BANKS = [(0, 1, 4, 6), (2, 3, 5, 7)]

        @block.sync
        def _(sp):
            def load(dst, src, name):
                sp.dma_start(dst, src).then_inc(S[name], 16)

            load(tokw[:], A["tokw"], "in_tok")
            for c in range(3):
                a, b = 11 * IMG * c, 11 * IMG * (c + 1)
                load(blocks[:, :, a:b], A["blocks"][:, :, a:b], f"in_blocks{c}")
            load(rows[:], A["rows"].partition_broadcast(128), "in_const")
            load(cst[:], A["consts"], "in_const")
            load(cols[:], A["cols"], "in_const")
            load(scale_row[:], A["scale"].partition_broadcast(128), "in_const")
            load(attw[:], A["attw"], "in_att")
            load(wd, A["wd"], "in_wd")
            load(wu, A["wu"], "in_wu")
            load(qkvw[:], A["qkvw"], "in_qkv")
            load(wo[:], A["wo"], "in_qkv")
            load(gate[:], A["gate"], "in_qkv")
            sp.wait_ge(S["tok_ps"], 3)
            load(tab[0:E0, :], A["tab"], "in_tab")
            load(tab[E0:128, :], A["tab"], "in_tab")
            if stop > 3:
                sp.wait_ge(S["xm_used"], 4 + 2 * K0)
                for dst, n in ((w1, "w1"), (w3, "w3"), (w2, "w2"), (sw1, "sw1"), (sw2, "sw2")):
                    load(dst, A[n], "in_ffn")
            if stop < 5:
                for n, v in (("in_wd", 16), ("in_wu", 16), ("in_att", 16), ("in_tab", 32), ("in_qkv", 48)):
                    sp.wait_ge(S[n], v)
            if stop == 1:
                sp.wait_ge(S["h0_ready"], 1)
                sp.dma_start(dbg[0:PI, :], HA[0:PI, :, :].rearrange("p a b -> p (a b)")).then_inc(S["stored"], 16)
            elif stop == 2:
                sp.wait_ge(S["h1b_ready"], 3)
                sp.dma_start(dbg[:, 0:N], HB[:, 0:NT, :].rearrange("p a b -> p (a b)")).then_inc(S["stored"], 16)
            elif stop == 3:
                sp.wait_ge(S["h2_ready"], 1)
                sp.dma_start(dbg[:, 0:N], HA[:, 0:NT, :].rearrange("p a b -> p (a b)")).then_inc(S["stored"], 16)
            elif stop == 4:
                sp.wait_ge(S["h3_ready"], 1)
                sp.dma_start(dbg[:, 0:N], HB[:, 0:NT, :].rearrange("p a b -> p (a b)")).then_inc(S["stored"], 16)
            else:
                sp.wait_ge(S["y_final"], 1)
                sp.dma_start(out, HA[:, 0:NT, :]).then_inc(S["stored"], 16)
            sp.wait_ge(S["stored"], 16)

        @block.tensor
        def _(pe):
            I = C["ident"]

            pe.wait_ge(S["in_tok"], 16)
            for c in range(3):
                pe.wait_ge(S[f"in_blocks{c}"], 16)
                n = 0
                for y in range(2):
                    for x in range(2):
                        for k in range(2):
                            v = blocks[:, k, c * 11 * IMG:(c + 1) * 11 * IMG]
                            v = v.rearrange("p (m y j x) -> p y x m j", y=2, x=2, j=6)[:, y, x]
                            for i in range(2):
                                o = (2 * c + i) * 512
                                last = nc.tensor.matmul(ps[:, o:o + CH], tokw[:, n * 256 + i * 128:n * 256 + i * 128 + 128], v,
                                                        start=(n == 0), stop=(n == 7))
                            n += 1
                post(last, "tok_ps")

            def job(n):
                if n >= 8:
                    pe.wait_ge(S["job_used"], n - 7)
                return job_bank(n)

            def tiles_T(what, src, p, groups, w):
                for g, (a, b) in enumerate(groups):
                    o = job(J[what] + g)
                    for t in range(a, b):
                        last = nc.tensor.transpose(ps[:, o + (t - a) * w:o + (t - a) * w + w], src[0:p, t, :], I[0:p, 0:p])
                    post(last, "job_ps")

            def columns(what, w, src, ready):
                for g in range(3):
                    o = job(J[what] + g)
                    pe.wait_ge(S["job_used"], ready + g + 1)
                    post(nc.tensor.matmul(ps[:, o:o + CH], w, src[:, g * CH:(g + 1) * CH], start=True, stop=True), "job_ps")

            def att_w(i):
                return attw[:, i * 128:(i + 1) * 128]

            pe.wait_ge(S["in_const"], 64)
            pe.wait_ge(S["tok_used"], 3)
            for g, (a, b) in enumerate(TILES4):
                o = job(J["tokT"] + g)
                for t in range(a, b):
                    last = nc.tensor.transpose(ps[0:PI, o + (t - a) * 128:o + (t - a) * 128 + 128],
                                               B[1][:, t * PI:(t + 1) * PI], I)
                post(last, "job_ps")
            if stop == 1:
                return
            pe.wait_ge(S["h0_ready"], 1)
            tiles_T("h0T", HA, PI, TILES4, PI)
            pe.wait_ge(S["in_att"], 16)
            columns("w1k", att_w(0), B[0], J["h0T"])
            columns("w1q", att_w(1), B[0], J["h0T"])
            columns("amp", att_w(4), B[0], J["h0T"])
            columns("w2k", att_w(2), B[1], J["w1k"])
            columns("w2q", att_w(3), B[2], J["w1q"])
            for g, (a, b) in enumerate(TILES4):
                o = job(J["v"] + g)
                for t in range(a, b):
                    last = nc.tensor.matmul(ps[0:PI, o + (t - a) * 128:o + (t - a) * 128 + 128],
                                            B[0][:, t * PI:(t + 1) * PI], att_w(5), start=True, stop=True)
                post(last, "job_ps")
            pe.wait_ge(S["kq_ready"], 2)
            for g, (a, b) in enumerate(TILES4):
                o = job(J["score"] + g)
                for t in range(a, b):
                    last = nc.tensor.matmul(ps[0:PI, o + (t - a) * PI:o + (t - a) * PI + PI],
                                            B[3][:, t * PI:(t + 1) * PI], B[4][:, t * PI:(t + 1) * PI],
                                            start=True, stop=True)
                post(last, "job_ps")
            for g, (a, b) in enumerate(TILES4):
                o = job(J["retr"] + g)
                pe.wait_ge(S["score_ready"], g + 1)
                if g == 0:
                    pe.wait_ge(S["z0_ready"], 1)
                for t in range(a, b):
                    last = nc.tensor.matmul(ps[0:PI, o + (t - a) * 128:o + (t - a) * 128 + 128],
                                            B[5][0:PI, t * PI:(t + 1) * PI], HB[0:PI, t, :], start=True, stop=True)
                post(last, "job_ps")
            pe.wait_ge(S["retr_ready"], 1)
            tiles_T("rnT", HB, PI, TILES4, PI)
            for g, (a, b) in enumerate(TILES4):
                o = job(J["att"] + g)
                if g == 0:
                    pe.wait_ge(S["job_used"], J["rnT"] + 3)
                for t in range(a, b):
                    last = nc.tensor.matmul(ps[0:PI, o + (t - a) * 128:o + (t - a) * 128 + 128],
                                            B[1][:, t * PI:(t + 1) * PI], att_w(6), start=True, stop=True)
                post(last, "job_ps")
            pe.wait_ge(S["h1_ready"], 1)
            tiles_T("h1T", HA, PI, TILES4, PI)
            for g, (a, b) in enumerate(TILES9):
                o = job(J["h1B"] + g)
                if g == 0:
                    pe.wait_ge(S["job_used"], J["h1T"] + 3)
                for t in range(a, b):
                    last = nc.tensor.transpose(ps[:, o + (t - a) * 128:o + (t - a) * 128 + 128],
                                               B[0][:, t * 128:(t + 1) * 128], I)
                post(last, "job_ps")
            if stop == 2:
                return
            pe.wait_ge(S["z1_ready"], 1)
            tiles_T("z1T", HA, 128, TILES9, 128)

            pe.wait_ge(S["sig_ready"], 1)
            pe.wait_ge(S["job_used"], J["z1T"] + 3)
            for t in range(NT):
                for i, w in enumerate((tsig8, csigb)):
                    last = nc.tensor.matmul(ps[:, t * E0:(t + 1) * E0], sgT[:, t * 128:(t + 1) * 128], w[:],
                                            start=(i == 0), stop=(i == 1))
            post(last, "key_ps")

            def route(E, K, r, dup):
                pe.wait_ge(S["oh_ready"], r + 1)
                for j in range(NT):
                    for i in range(j + 1):
                        nc.tensor.matmul(ps[:, j * E:(j + 1) * E], trib[:] if i == j else oneb[:], oh[:, i, 0, 0:E],
                                         start=(i == 0), stop=(i == j))
                M = dup * E
                for i in range(NT):
                    last = nc.tensor.matmul(ps[0:M, 1024:1025], oh[:, i, 0:dup, 0:E], oneb[:, 0:1],
                                            start=(i == 0), stop=(i == NT - 1))
                post(last, "rank_ps")
                pe.wait_ge(S["cnt_ready"], r + 1)
                cnt = small[0:E, 0:1]
                tri = C["triS"][0:E, 0:E]
                for d in range(dup):
                    nc.tensor.matmul(ps[d * E:d * E + E, 1536:1537], tri, cnt, start=True, stop=True)
                post(nc.tensor.matmul(ps[:, 2048:2048 + E], cnt.to_broadcast([E, 128]), tri, start=True, stop=True), "start_ps")
                pe.wait_ge(S["route_cols"], r + 1)
                o = 2560
                pairs, first = small[0:E, 6:7], small[0:E, 3:4]
                nc.tensor.matmul(ps[0:K, o:o + E], pairs.to_broadcast([E, K]), C["triI"][0:E, 0:E], start=True, stop=True)
                nc.tensor.matmul(ps[0:K, o + 64:o + 64 + E], pairs.to_broadcast([E, K]), tri, start=True, stop=True)
                nc.tensor.matmul(ps[0:K, o + 128:o + 128 + E], first.to_broadcast([E, K]), I[0:E, 0:E], start=True, stop=True)
                for g, (a, b) in enumerate(TILES9):
                    last = nc.tensor.matmul(ps[:, g * 512:g * 512 + (b - a) * 128], ecolb[0:E, 0:1].to_broadcast([E, 128]),
                                     ohs[0:E, a * 128:b * 128], start=True, stop=True)
                post(last, "rows_ps")
                pe.wait_ge(S["pair_cols"], r + 1)
                for c in range(3):
                    last = nc.tensor.matmul(ps[:, 3072 + c * 128:3072 + c * 128 + K],
                                            small[0:K, 8 + c:9 + c].to_broadcast([K, 128]), I[0:K, 0:K],
                                            start=True, stop=True)
                post(last, "pairs_ps")
                pe.wait_ge(S["pairs_ready"], r + 1)
                for j in range(NT):
                    last = nc.tensor.matmul(ps[:, 1536 + j * 128:1536 + (j + 1) * 128], pos[:, j:j + 1].to_broadcast([128, 128]),
                                            I, start=True, stop=True)
                post(last, "rows_ps")

            def sort(src, r):
                for j in range(NT):
                    n = r * 18 + j
                    if j == 0:
                        pe.wait_ge(S["posrow_ready"], r + 1)
                    pe.wait_ge(S["perm_made"], n + 1)
                    for g in range(3):
                        last = nc.tensor.matmul(ps[:, 1536 + g * 512:1536 + g * 512 + 384], src[:, j, :],
                                                B[1 + j % 2][:, g * 384:(g + 1) * 384], start=(j == 0), stop=(j == NT - 1))
                    post(last, "perm_used")

            def zero_acc():
                for b, (s, e) in enumerate(TILES9):
                    nc.tensor.matmul(bank(5 + b, (e - s) * 128), zb[:, 0:128], zb[:, 0:(e - s) * 128], start=True, stop=False,
                                     skip_group_check=True)

            def unsort(src, r):
                zero_acc()
                for s_ in range(NT):
                    n = r * 18 + 9 + s_
                    pe.wait_ge(S["perm_made"], n + 1)
                    for i in range(NT):
                        last = nc.tensor.matmul(ps[:, 2560 + i * 128:2560 + (i + 1) * 128],
                                                B[1 + n % 2][:, i * 128:(i + 1) * 128], src[:, s_, :],
                                                start=False, stop=(s_ == NT - 1), skip_group_check=True)
                    post(last, "perm_used")

            def pair_products(w, K, n0):
                zero_acc()
                with pe.Fori(0, K // 4) as quad:
                    k = quad * 4
                    for u in range(4):
                        et = pe.value_load(offs[0:1, 0, bass.ds(k + u, 1)], min_val=0, max_val=(E0 - 1) * 128)
                        tt = pe.value_load(offs[0:1, 1, bass.ds(k + u, 1)], min_val=0, max_val=(NT - 1) * 128)
                        pe.wait_ge(S["xm_ready"], k + (n0 + u + 1))
                        nc.tensor.matmul(ps[:, bass.ds(tt + 2560, 128)], xm[:, u, :], w[:, bass.ds(et, 128)],
                                         start=False, stop=False, skip_group_check=True).then_inc(S["xm_used"], 1)

            route(E0, K0, 0, 2)
            sort(HA, 0)
            pe.wait_ge(S["in_wd"], 16)
            pe.wait_ge(S["pairs_ready"], 1)
            pe.wait_ge(S["sorted_ready"], 1)
            pair_products(wd, K0, 0)
            if stop == 2.5:
                return
            pe.wait_ge(S["accs_copied"], 1)
            for t in range(NT):
                last = nc.tensor.transpose(ps[:, 1536 + t * 128:1536 + (t + 1) * 128], HA[:, t, :], I)
            post(last, "hT_ps")
            pe.wait_ge(S["tab_split"], 1)
            pe.wait_ge(S["hn_ready"], 1)
            n = 0
            for g in range(GRID):
                for c in range(3):
                    if n >= 2:
                        pe.wait_ge(S["tab_used"], n - 1)
                    for v in range(2):
                        o = 1536 + (n % 2) * 1024 + v * 512
                        w = (g * 2 + v) * 128
                        nc.tensor.matmul(ps[:, o:o + 384], tab_hi[:, w:w + 128], ohs[:, c * 384:(c + 1) * 384],
                                         start=True, stop=False)
                        last = nc.tensor.matmul(ps[:, o:o + 384], tab_lo[:, w:w + 128], ohs[0:E0, c * 384:(c + 1) * 384],
                                                start=False, stop=True)
                    post(last, "tab_ps")
                    n += 1
            pe.wait_ge(S["hs_ready"], 1)
            pe.wait_ge(S["in_wu"], 16)
            pair_products(wu, K0, K0)
            pe.wait_ge(S["accs_copied"], 2)
            unsort(HA, 0)
            if stop == 3:
                return

            def l1_tile(j):
                def w(name, c):
                    pe.wait_ge(S[name], j * PER[name] + c)

                w("xst_ready", 1)
                w("y_done", 0)
                nc.tensor.transpose(ps[:, 1664:1792], xm[:, 0, :], I).then_inc(S["xT_ps"], 1)
                w("xT_done", 1)
                for i in range(3):
                    nc.tensor.matmul(bank(i), xm[:, 1, :], qkvw[:, i * 512:(i + 1) * 512], start=True, stop=True)
                nc.tensor.matmul(bank(3, NH), xm[:, 1, :], qkvw[:, 1536:1536 + NH], start=True, stop=True).then_inc(S["qkv_ps"], 1)
                w("prod_done", 1)
                for h in range(NH):
                    if h >= 4:
                        w("ft_done", h - 3)
                    for v in range(2):
                        for i, src in enumerate((8 + h, h)):
                            o = (4 + h % 4) * 512 + (v * 2 + i) * 128
                            last = nc.tensor.transpose(ps[:, o:o + 128], feat[:, v, src, :], I)
                    last.then_inc(S["ft_ps"], 1)

                def half(h, per_head):
                    for i in range(4):
                        last = per_head(4 * h + i, i)
                    return last

                def mm(o, lhsT, rhs, n=128):
                    return nc.tensor.matmul(ps[:, o:o + n], lhsT, rhs, start=True, stop=True)

                for h in range(2):
                    w("ft_done", 4 * h + 4)
                    if h:
                        w("vb_done", 1)

                    def gram(hd, i):
                        o = BANKS[h][0] * 512 + i * 256
                        for v in range(2):
                            last = nc.tensor.matmul(ps[:, o:o + 256], featT[:, hd, v, 0:128], featT[:, hd, v, :],
                                                    start=(v == 0), stop=(v == 1))
                        return last
                    half(h, gram).then_inc(S["gram_ps"], 1)
                for h in range(2):
                    a, b, c, d = (x * 512 for x in BANKS[h])
                    w("nt_done", h + 1)
                    w("ft_done", 8)
                    half(h, lambda hd, i: nc.tensor.transpose(ps[:, c + i * 128:c + i * 128 + 128], nt[:, hd, :], I)).then_inc(S["n_ps"], 1)
                for h in range(2):
                    a, b, c, d = (x * 512 for x in BANKS[h])
                    w("n_done", h + 1)
                    w("cs_done", h + 1)
                    half(h, lambda hd, i: mm(a + i * 128, nn[:, hd, :], nt[:, hd, :]))
                    half(h, lambda hd, i: mm(b + i * 128, nt[:, hd, :], nn[:, hd, :])).then_inc(S["n2_ps"], 1)
                for h in range(2):
                    a, b, c, d = (x * 512 for x in BANKS[h])
                    w("n2_done", h + 1)
                    w("w_done", h + 1)
                    half(h, lambda hd, i: mm(c + i * 128, n2[:, hd, :], ww[:, hd, :]))
                    half(h, lambda hd, i: mm(d + i * 128, n2t[:, hd, :], n2[:, hd, :])).then_inc(S["a_ps"], 1)
                for h in range(2):
                    a, b, c, d = (x * 512 for x in BANKS[h])
                    w("a_done", h + 1)
                    w("n4_done", h + 1)
                    half(h, lambda hd, i: mm(a + i * 128, n2t[:, hd, :], ww[:, hd, :])).then_inc(S["x_ps"], 1)
                for h in range(2):
                    a, b, c, d = (x * 512 for x in BANKS[h])
                    w("x8_done", h + 1)
                    w("rv_done", 1)
                    half(h, lambda hd, i: mm(b + i * 64, nn[:, hd, :], rhs_v[:, hd, :], 64)).then_inc(S["e_ps"], 1)
                for r in range(3):
                    for h in range(2):
                        a, b, c, d = (x * 512 for x in BANKS[h])
                        w("d_done", 2 * r + h + 1)
                        half(h, lambda hd, i: mm(c + i * 64, ct[:, hd, :], delta[:, hd, 0:64], 64)).then_inc(S["t_ps"], 1)
                    for h in range(2):
                        a, b, c, d = (x * 512 for x in BANKS[h])
                        w("q_done", 2 * r + h + 1)
                        half(h, lambda hd, i: mm(d + i * 64, nn[:, hd, :], resid[:, hd, :], 64)).then_inc(S["e_ps"], 1)
                for h in range(2):
                    a, b, c, d = (x * 512 for x in BANKS[h])
                    w("d_done", 6 + h + 1)
                    half(h, lambda hd, i: mm(a + i * 65, smm[:, hd, :], delta[:, hd, :], 65)).then_inc(S["o_ps"], 1)
                w("o_done", 2)
                for i in range(4):
                    last = nc.tensor.transpose(ps[:, 512 + i * 128:512 + i * 128 + 128],
                                               regA[:, 8704 + i * 128:8704 + i * 128 + 128], I)
                last.then_inc(S["ot_ps"], 1)
                w("ot_done", 1)
                for i in range(4):
                    last = nc.tensor.matmul(ps[:, 3072:3200], B[1][:, i * 128:(i + 1) * 128], wo[:, i * 128:(i + 1) * 128],
                                            start=(i == 0), stop=(i == 3))
                last.then_inc(S["y_ps"], 1)

            pe.wait_ge(S["in_qkv"], 48)
            for j in range(NT):
                l1_tile(j)
            if stop == 4:
                return
            pe.wait_ge(S["h3_ready"], 1)
            for t in range(NT):
                last = nc.tensor.transpose(ps[:, t * 128:t * 128 + 128], HB[:, t, :], I)
            post(last, "h3T_ps")
            pe.wait_ge(S["h3T_ready"], 1)
            for t in range(NT):
                last = nc.tensor.matmul(ps[:, 1536 + t * E1:1536 + (t + 1) * E1], B[0][:, t * 128:(t + 1) * 128], gate[:],
                                        start=True, stop=True)
            post(last, "gate_ps")
            pe.wait_ge(S["in_ffn"], 80)
            n = 0
            for c in range(4):
                for g in range(3):
                    if n >= 2:
                        pe.wait_ge(S["s1_used"], n - 1)
                    o = (6 + n % 2) * 512
                    post(nc.tensor.matmul(ps[:, o:o + 384], sw1[:, c * 128:(c + 1) * 128], B[0][:, g * 384:(g + 1) * 384],
                                          start=True, stop=True), "s1_ps")
                    n += 1
            pe.wait_ge(S["s1_used"], 12)
            route(E1, K1, 1, 1)
            sort(HB, 1)
            pe.wait_ge(S["sorted_ready"], 2)
            zero_acc()
            pe.sem_inc(S["gT_ps"], 1)
            pe.sem_inc(S["y1_ps"], 1)
            with pe.Fori(0, K1 // 4) as quad:
                k = quad * 4

                def up(u):
                    et = pe.value_load(offs[0:1, 0, bass.ds(k + u, 1)], min_val=0, max_val=(E1 - 1) * INNER)
                    o = (u % 2) * 1024
                    pe.wait_ge(S["xm_ready"], k + (2 * K0 + u + 1))
                    if u >= 2:
                        pe.wait_ge(S["g_done"], k + u)
                    else:
                        pe.wait_ge(S["g_done"], k + 1)
                    nc.tensor.matmul(ps[:, o:o + 512], xm[:, u, :], w1[:, bass.ds(et, 512)], start=True, stop=True).then_inc(S["up_ps"], 1)
                    nc.tensor.matmul(ps[:, o + 512:o + 1024], xm[:, u, :], w3[:, bass.ds(et, 512)], start=True, stop=True).then_inc(S["xm_used"], 1)

                def down(u):
                    et = pe.value_load(offs[0:1, 0, bass.ds(k + u, 1)], min_val=0, max_val=(E1 - 1) * INNER)
                    tt = pe.value_load(offs[0:1, 1, bass.ds(k + u, 1)], min_val=0, max_val=(NT - 1) * 128)
                    pe.wait_ge(S["g_done"], k + (u + 2))
                    pe.wait_ge(S["gT_done"], k + (u + 1))
                    for i in range(4):
                        last = nc.tensor.transpose(ps[:, 2048 + i * 128:2048 + (i + 1) * 128], gg[:, u % 2, i * 128:(i + 1) * 128], I)
                    last.then_inc(S["gT_ps"], 1)
                    pe.wait_ge(S["gT_done"], k + (u + 2))
                    for i in range(4):
                        last = nc.tensor.matmul(ps[:, bass.ds(tt + 2560, 128)], gT[:, u % 2, i * 128:(i + 1) * 128],
                                                w2[:, bass.ds(et + i * 128, 128)], start=False, stop=False, skip_group_check=True)
                    last.then_inc(S["y1_ps"], 1)

                up(0)
                up(1)
                down(0)
                up(2)
                down(1)
                up(3)
                down(2)
                down(3)
            for t in range(NT):
                for c in range(4):
                    last = nc.tensor.matmul(ps[:, t * 128:(t + 1) * 128], gs[:, c * N + t * 128:c * N + (t + 1) * 128],
                                            sw2[:, c * 128:(c + 1) * 128], start=(c == 0), stop=(c == 3))
            post(last, "sh_ps")
            pe.wait_ge(S["accs_copied"], 3)
            unsort(HA, 1)

        @block.scalar
        def _(act):
            act.wait_ge(S["in_const"], 64)
            for c in range(3):
                act.wait_ge(S["tok_ps"], c + 1)
                post(nc.scalar.activation(B[1][:, c * CH:(c + 1) * CH], ps[:, 2 * c * 512:2 * c * 512 + CH], ACT.Identity,
                                          bias=Cc["tok_bias"]), "tok_own")

            def consume(n):
                act.wait_ge(S["job_ps"], n + 1)
                return job_bank(n)

            def columns(what, dst, func, **kw):
                for g in range(3):
                    o = consume(J[what] + g)
                    post(nc.scalar.activation(dst[:, g * CH:(g + 1) * CH], ps[:, o:o + CH], func, **kw), "job_used")

            for g, (a, b) in enumerate(TILES4):
                o = consume(J["tokT"] + g)
                v = ps[0:PI, o:o + (b - a) * 128].rearrange("p (t q r e) -> p r t q e", q=4, r=2, e=16)
                nc.scalar.activation(HA[0:PI, a:b, 0:64].rearrange("p t (q e) -> p t q e", e=16), v[:, 1], ACT.Copy)
                post(nc.scalar.activation(HA[0:PI, a:b, 64:128].rearrange("p t (q e) -> p t q e", e=16), v[:, 0], ACT.Copy), "job_used")
            if stop == 1:
                return
            for g, (a, b) in enumerate(TILES4):
                o = consume(J["h0T"] + g)
                post(nc.scalar.activation(B[0][:, a * PI:b * PI], ps[:, o:o + (b - a) * PI], ACT.Copy), "job_used")
            columns("w1k", B[1], ACT.Gelu, bias=Cc["ke_b1"])
            columns("w1q", B[2], ACT.Gelu, bias=Cc["qe_b1"])
            columns("amp", B[5], ACT.Identity, bias=Cc["amp_b"])
            columns("w2k", B[3], ACT.Tanh, bias=Cc["ke_b2"])
            columns("w2q", B[4], ACT.Tanh, bias=Cc["qe_b2"])
            for g, (a, b) in enumerate(TILES4):
                o = consume(J["v"] + g)
                post(nc.scalar.activation(HB[0:PI, a:b, :], ps[0:PI, o:o + (b - a) * 128].rearrange("p (t d) -> p t d", d=128),
                                          ACT.Copy), "job_used")
            act.wait_ge(S["job_used"], J["v"] + 3)
            for i in range(2):
                done(act, nc.scalar.activation(B[3 + i][0:64, :], B[3 + i][0:64, :], ACT.Abs), "act_step")
                act.wait_ge(S["phase_held"], i + 1)
                done(act, nc.scalar.activation(B[3 + i][:], B[3 + i][:], ACT.Sin, bias=C["sin_bias"], scale=C["sin_scale"]), "act_step")
            done(act, nc.scalar.activation(B[1][:], B[5][:], ACT.Abs), "act_step")
            done(act, nc.scalar.activation(B[1][:], B[1][:], ACT.Exp, scale=-1.0), "act_step")
            done(act, nc.scalar.activation(B[1][:], B[1][:], ACT.Ln, bias=C["one"]), "act_step")
            assert count["act_step"] == 7
            for g, (a, b) in enumerate(TILES4):
                o = consume(J["rnT"] + g)
                if g == 0:
                    act.wait_ge(S["job_used"], J["rnT"])
                    act.wait_ge(S["kq_ready"], 2)
                post(nc.scalar.activation(B[1][:, a * PI:b * PI], ps[:, o:o + (b - a) * PI], ACT.Identity,
                                          scale=Cc["ln_g"], bias=Cc["ln_b"]), "job_used")
            view = B[0][:, 0:N].rearrange("p (q b) -> p b q", b=NIMG)
            for g, (a, b) in enumerate(TILES4):
                o = consume(J["h1T"] + g)
                if g == 0:
                    act.wait_ge(S["job_used"], J["h1T"])
                n = min(3 * b, NIMG) - 3 * a
                post(nc.scalar.activation(view[:, 3 * a:3 * a + n, :],
                                          ps[:, o:o + n * NPATCH].rearrange("p (b q) -> p b q", q=NPATCH), ACT.Copy), "job_used")
            for g, (a, b) in enumerate(TILES9):
                o = consume(J["h1B"] + g)
                last = nc.scalar.activation(HB[:, a:b, :], ps[:, o:o + (b - a) * 128].rearrange("p (t d) -> p t d", d=128), ACT.Copy)
                post(last, "h1b_ready")
            act.wait_ge(S["h1b_ready"], 3)
            act.wait_ge(S["dve_h1b"], 1)
            if stop == 2:
                return
            for g, (a, b) in enumerate(TILES9):
                o = consume(J["z1T"] + g)
                post(nc.scalar.activation(sgT[:, a * 128:b * 128], ps[:, o:o + (b - a) * 128], ACT.Sign,
                                          scale=Cc["gamma"], bias=Cc["beta"]), "job_used")

            def posrow(r):
                act.wait_ge(S["rows_ps"], 2 * r + 2)
                post(nc.scalar.activation(B[3][:, 0:N], ps[:, 1536:1536 + N], ACT.Copy), "posrow_ready")

            def rows_out(dst, pairs):
                act.wait_ge(S["xm_used"], 4 + pairs)
                post(nc.scalar.activation(dst[:, 0:NT, :], ps[:, 2560:2560 + N].rearrange("p (t d) -> p t d", d=128), ACT.Copy),
                     "accs_copied")

            posrow(0)
            act.wait_ge(S["perm_used"], 9)
            act.wait_ge(S["pairs_ready"], 1)
            post(nc.scalar.activation(B[4][:, 0:N].rearrange("p (g n) -> p g n", g=3),
                                      ps[:, 1536:3072].rearrange("p (g n) -> p g n", g=3)[:, :, 0:384], ACT.Identity,
                                      scale=Cc["gamma"], bias=Cc["beta"]), "sorted_ready")
            rows_out(HA, K0)
            act.wait_ge(S["hT_ps"], 1)
            done(act, nc.scalar.activation(B[5][:, 0:N], ps[:, 1536:1536 + N], ACT.Sigmoid), "hn_ready")
            rows_out(HA, 2 * K0)
            if stop == 3:
                return

            def l1_tile(j):
                def w(name, c):
                    act.wait_ge(S[name], j * PER[name] + c)

                w("xT_ps", 1)
                nc.scalar.activation(xm[:, 1, :], ps[:, 1664:1792], ACT.Copy).then_inc(S["xT_done"], 1)
                w("qkv_ps", 1)
                w("prod_done", 0)
                qk = ps[:, 0:1024].rearrange("p (h e) -> p h e", h=16)
                nc.scalar.activation(relus[:, :, 2:66], qk, ACT.Relu)
                nc.scalar.activation(relus[:, :, 0:2], qk[:, :, 62:64], ACT.Relu, scale=-1.0)
                nc.scalar.activation(relus[:, :, 66:130], qk, ACT.Relu, scale=-1.0).then_inc(S["relu_done"], 1)
                w("rv_done", 0)
                nc.scalar.activation(vals, ps[:, 1024:1536].rearrange("p (h e) -> p h e", h=NH), ACT.Copy)
                nc.scalar.activation(hsc[:, 0, :], bank(3, NH), ACT.Sigmoid).then_inc(S["vb_done"], 1)
                for h in range(NH):
                    w("ft_ps", h + 1)
                    o = (4 + h % 4) * 512
                    nc.scalar.activation(featT[:, h, :, :], ps[:, o:o + 512].rearrange("p (v f) -> p v f", v=2), ACT.Copy).then_inc(S["ft_done"], 1)

                def evac(dst, o, h):
                    return nc.scalar.activation(dst[:, 4 * h:4 * h + 4, :], ps[:, o:o + 512].rearrange("p (h f) -> p h f", h=4), ACT.Copy)

                for h in range(2):
                    w("n_ps", h + 1)
                    evac(nn, BANKS[h][2] * 512, h).then_inc(S["n_done"], 1)
                for h in range(2):
                    w("n2_ps", h + 1)
                    evac(n2t, BANKS[h][0] * 512, h)
                    evac(n2, BANKS[h][1] * 512, h).then_inc(S["n2_done"], 1)
                for h in range(2):
                    w("a_ps", h + 1)
                    evac(n2t, BANKS[h][3] * 512, h).then_inc(S["n4_done"], 1)
                w("ot_ps", 1)
                nc.scalar.activation(B[1][:, 0:512], ps[:, 512:1024], ACT.Copy).then_inc(S["ot_done"], 1)

            for j in range(NT):
                l1_tile(j)
            if stop == 4:
                return
            act.wait_ge(S["h3T_ps"], 1)
            post(nc.scalar.activation(B[0][:, 0:N], ps[:, 0:N], ACT.Copy), "h3T_ready")
            n = 0
            for c in range(4):
                for g in range(3):
                    act.wait_ge(S["s1_ps"], n + 1)
                    o = (6 + n % 2) * 512
                    post(nc.scalar.activation(gs[:, c * N + g * 384:c * N + (g + 1) * 384], ps[:, o:o + 384], ACT.Gelu), "s1_used")
                    n += 1
            act.wait_ge(S["top_ready"], 1)
            post(nc.scalar.activation(wtop[:], wtop[:], ACT.Exp), "wtop_exp")
            act.wait_ge(S["rows_ps"], 3)
            act.wait_ge(S["pairs_ready"], 2)
            post(nc.scalar.activation(B[5][:, 0:N], ps[:, 0:N], ACT.Copy), "es_copied")
            posrow(1)
            act.wait_ge(S["perm_used"], 27)
            post(nc.scalar.activation(B[4][:, 0:N].rearrange("p (g n) -> p g n", g=3),
                                      ps[:, 1536:3072].rearrange("p (g n) -> p g n", g=3)[:, :, 0:384], ACT.Copy), "sorted_ready")
            act.sem_inc(S["gT_done"], 1)
            with act.Fori(0, K1 // 4) as quad:
                k = quad * 4

                def silu(u):
                    act.wait_ge(S["up_ps"], k + (u + 1))
                    if u >= 2:
                        act.wait_ge(S["g_done"], k + u)
                    else:
                        act.wait_ge(S["g_done"], k + 1)
                    nc.scalar.activation(sg[:, u % 2, :], ps[:, (u % 2) * 1024:(u % 2) * 1024 + 512], ACT.Silu).then_inc(S["silu_done"], 1)

                def turned(u):
                    act.wait_ge(S["gT_ps"], k + (u + 2))
                    if u >= 2:
                        act.wait_ge(S["y1_ps"], k + u)
                    else:
                        act.wait_ge(S["y1_ps"], k + 1)
                    nc.scalar.activation(gT[:, u % 2, :], ps[:, 2048:2560], ACT.Copy).then_inc(S["gT_done"], 1)

                silu(0)
                silu(1)
                turned(0)
                silu(2)
                turned(1)
                silu(3)
                turned(2)
                turned(3)
            act.wait_ge(S["y1_ps"], 1 + K1)
            post(nc.scalar.activation(HA[:, 0:NT, :], ps[:, 2560:2560 + N].rearrange("p (t d) -> p t d", d=128), ACT.Copy), "accs_copied")

        @block.gpsimd
        def _(pool):
            done(pool, nc.gpsimd.memset(mhalf[:], -0.5), "pool_step")
            nc.gpsimd.memset(zb[:], 0.0).then_inc(S["consts_made"], 1)
            nc.gpsimd.memset(oneb[:], 1.0).then_inc(S["consts_made"], 1)

            def inv_sqrt(n, p, t):
                pool.wait_ge(S["var_ready"], n)
                post(nc.gpsimd.tensor_tensor(rstd[0:p, 0:t], rstd[0:p, 0:t], mhalf[0:p, 0:t], ALU.pow), "rstd_ready")

            inv_sqrt(1, PI, TI)
            if stop == 1:
                return
            pool.wait_ge(S["in_tab"], 32)
            done(pool, nc.gpsimd.tensor_copy(tab_hi, tab), "pool_step")
            done(pool, nc.gpsimd.tensor_tensor(tab, tab, tab_hi, ALU.subtract), "pool_step")
            nc.gpsimd.tensor_copy(tab_hi[E0:128, :], tab[E0:128, :])
            done(pool, nc.gpsimd.tensor_copy(tab_lo, tab[0:E0, :]), "pool_step")
            done(pool, nc.gpsimd.tensor_tensor(tab_lo, tab[0:E0, :], tab_lo, ALU.subtract), "tab_split")
            inv_sqrt(2, PI, TI)
            inv_sqrt(3, PI, TI)
            if stop == 2:
                return
            inv_sqrt(4, 128, NT)
            inv_sqrt(5, 128, NT)
            if stop == 3:
                return

            def l1_tile(j):
                for h in range(2):
                    pool.wait_ge(S["nt_done"], j * PER["nt_done"] + h + 1)
                    nc.gpsimd.tensor_tensor(ww[:, 4 * h:4 * h + 4, :], C["ident"].unsqueeze(1).to_broadcast([128, 4, 128]),
                                            nt[:, 4 * h:4 * h + 4, :], ALU.subtract).then_inc(S["w_done"], 1)

            for j in range(NT):
                l1_tile(j)
            inv_sqrt(6, 128, NT)
            inv_sqrt(7, 128, NT)
            if stop > 4:
                inv_sqrt(8, 128, NT)

        @block.vector
        def _(dve):
            def step(ins):
                done(dve, ins, "dve_step")

            def norm(src, dst, p, t, n, stats_done=False):
                if not stats_done:
                    for i in range(t):
                        last = nc.vector.bn_stats(stats[0:p, i, :], src[0:p, i, :])
                    step(last)
                for i in range(t):
                    last = nc.vector.bn_aggr(mv[0:p, i, :], stats[0:p, i, :])
                step(last)
                post(nc.vector.tensor_scalar(rstd[0:p, 0:t], mv[0:p, 0:t, 1], EPS, None, ALU.add), "var_ready")
                dve.wait_ge(S["rstd_ready"], n)
                for i in range(t):
                    last = nc.vector.tensor_scalar(dst[0:p, i, :], src[0:p, i, :], mv[0:p, i, 0:1], rstd[0:p, i:i + 1],
                                                   ALU.subtract, ALU.mult)
                return last

            def over_tiles(row, p, t):
                return row[0:p, :].unsqueeze(1).to_broadcast([p, t, 128])

            def affine(buf, p, t, g, b, name):
                step(nc.vector.tensor_tensor(buf[0:p, 0:t, :], buf[0:p, 0:t, :], over_tiles(g, p, t), ALU.mult))
                done(dve, nc.vector.tensor_tensor(buf[0:p, 0:t, :], buf[0:p, 0:t, :], over_tiles(b, p, t), ALU.add), name)

            dve.wait_ge(S["in_const"], 64)
            nc.vector.tensor_copy(trib[:], C["triS"]).then_inc(S["consts_made"], 1)
            nc.vector.tensor_copy(ecolb[:], C["ecol"]).then_inc(S["consts_made"], 1)
            for c in range(3):
                dve.wait_ge(S["tok_own"], c + 1)
                own = B[1][:, c * CH:(c + 1) * CH]
                far = ps[:, (2 * c + 1) * 512:(2 * c + 1) * 512 + CH]
                for q in range(4):
                    p = slice(32 * q, 32 * q + 16)
                    if q < 2:
                        a, b = own[p].rearrange("p (m j) -> p m j", j=6), far[p].rearrange("p (m j) -> p m j", j=6)
                    else:
                        a, b = own[p].rearrange("p (b i) -> p b i", i=36), far[p].rearrange("p (b i) -> p b i", i=36)
                    s1 = 1 if q < 2 else 6
                    if q % 2 == 0:
                        a, b = a[:, :, :-s1], b[:, :, s1:]
                    else:
                        a, b = a[:, :, s1:], b[:, :, :-s1]
                    last = nc.vector.tensor_tensor(a, b, a, ALU.add)
                post(last, "tok_used")
            dve.wait_ge(S["job_used"], J["tokT"] + 3)
            step(norm(HA, HA, PI, TI, 1))
            affine(HA, PI, TI, R["tok_g"], R["tok_b"], "h0_ready")
            if stop == 1:
                return

            def phase(i):
                dve.wait_ge(S["job_used"], J["w2k"] + 3 * i + 3)
                b = B[3 + i]
                done(dve, nc.vector.tensor_scalar(b[64:128, :], b[64:128, :], BELOW1, -BELOW1, ALU.min, ALU.max), "phase_held")

            phase(0)
            phase(1)
            dve.wait_ge(S["act_step"], 7)
            step(nc.vector.scalar_tensor_tensor(B[1][:], B[5][:], 0.0, B[1][:], ALU.max, ALU.add))
            for i in range(2):
                done(dve, nc.vector.scalar_tensor_tensor(B[3 + i][:], B[1][:], 0.1, B[3 + i][:], ALU.add, ALU.mult), "kq_ready")
            dve.wait_ge(S["job_used"], J["v"] + 3)
            done(dve, nc.vector.tensor_tensor(HB[0:PI, :, :], HB[0:PI, :, :], over_tiles(R["v_b"], PI, TI), ALU.add), "z0_ready")
            for g, (a, b) in enumerate(TILES4):
                n = J["score"] + g
                dve.wait_ge(S["job_ps"], n + 1)
                o = job_bank(n)
                done(dve, nc.vector.tensor_tensor(B[5][0:PI, a * PI:b * PI].rearrange("p (t l) -> p t l", l=PI),
                                                  ps[0:PI, o:o + (b - a) * PI].rearrange("p (t l) -> p t l", l=PI),
                                                  C["maskimg"][0:PI, :].unsqueeze(1).to_broadcast([PI, b - a, PI]), ALU.mult), "score_ready")
                dve.sem_inc(S["job_used"], 1)
            for g, (a, b) in enumerate(TILES4):
                n = J["retr"] + g
                dve.wait_ge(S["job_ps"], n + 1)
                if g == 0:
                    dve.wait_ge(S["job_ps"], J["retr"] + 3)
                o = job_bank(n)
                done(dve, nc.vector.tensor_scalar(HB[0:PI, a:b, :], ps[0:PI, o:o + (b - a) * 128].rearrange("p (t d) -> p t d", d=128),
                                                  C["invnorm"][0:PI, :], None, ALU.mult), "dve_step")
                dve.sem_inc(S["job_used"], 1)
            done(dve, norm(HB, HB, PI, TI, 2), "retr_ready")
            for g, (a, b) in enumerate(TILES4):
                n = J["att"] + g
                dve.wait_ge(S["job_ps"], n + 1)
                o = job_bank(n)
                step(nc.vector.scalar_tensor_tensor(HA[0:PI, a:b, :], HA[0:PI, a:b, :], 2.0,
                                                    ps[0:PI, o:o + (b - a) * 128].rearrange("p (t d) -> p t d", d=128),
                                                    ALU.mult, ALU.add))
                dve.sem_inc(S["job_used"], 1)
            step(nc.vector.tensor_tensor(HA[0:PI, :, :], HA[0:PI, :, :], over_tiles(R["out_b"], PI, TI), ALU.add))
            done(dve, norm(HA, HA, PI, TI, 3), "h1_ready")

            dve.wait_ge(S["h1b_ready"], 3)
            dve.sem_inc(S["job_used"], 3)
            dve.sem_inc(S["dve_h1b"], 1)
            if stop == 2:
                return
            dve.wait_ge(S["job_used"], J["h1T"] + 3)
            done(dve, norm(HB, HA, 128, NT, 4), "z1_ready")
            dve.wait_ge(S["in_wd"], 16)
            step(nc.vector.tensor_reduce(tsum[:], wd.rearrange("p (t h) -> p t h", h=128), X, ALU.add))

            def sign(dst, src, tmp, times):
                step(nc.vector.tensor_scalar(tmp, src, 0.0, times, ALU.is_gt, ALU.mult))
                step(nc.vector.tensor_scalar(src, src, 0.0, times, ALU.is_lt, ALU.mult))
                step(nc.vector.tensor_tensor(dst, tmp, src, ALU.subtract))

            sign(tsig8[:], tsum[:], srow[:], 8.0)
            step(nc.vector.tensor_reduce(csum[:], tsig8[:].rearrange("p (c j) -> p c j", j=8), X, ALU.add))
            sign(small[:, 8:16], csum[:], small[:, 0:8], 8.0 * 4096.0)
            done(dve, nc.vector.tensor_copy(csigb[:].rearrange("p (c j) -> p c j", j=8), small[:, 8:16].unsqueeze(2).to_broadcast([128, 8, 8])), "sig_ready")

            dve.wait_ge(S["key_ps"], 1)
            step(nc.vector.tensor_tensor(key[:], ps[:, 0:NT * E0].rearrange("p (t e) -> p t e", e=E0),
                                         C["keybias"].unsqueeze(1).to_broadcast([128, NT, E0]), ALU.add))
            step(nc.vector.tensor_reduce(kmax[:], key[:], X, ALU.max))
            step(nc.vector.tensor_tensor(oh[:, :, 0, :], key[:], kmax[:].unsqueeze(2).to_broadcast([128, NT, E0]), ALU.is_equal))
            done(dve, nc.vector.tensor_copy(oh[:, :, 1, :], oh[:, :, 0, :]), "oh_ready")
            step(nc.vector.tensor_tensor(key[:], oh[:, :, 0, :], scale_row[:].unsqueeze(1).to_broadcast([128, NT, E0]), ALU.mult))
            step(nc.vector.tensor_reduce(scl[:], key[:], X, ALU.add))

            def route(E, K, r, dup, weight):
                M = dup * E
                dve.wait_ge(S["rank_ps"], r + 1)
                done(dve, nc.vector.tensor_copy(small[0:M, 0:1], ps[0:M, 1024:1025]), "cnt_ready")
                dve.wait_ge(S["start_ps"], r + 1)
                step(nc.vector.tensor_copy(small[0:M, 1:2], ps[0:M, 1536:1537]))
                step(nc.vector.tensor_tensor(small[0:M, 2:3], small[0:M, 1:2], small[0:M, 0:1], ALU.add))
                step(nc.vector.tensor_copy(srow[:, 0:E], ps[:, 2048:2048 + E]))
                step(nc.vector.tensor_tensor(rk[:, :, 0:E], ps[:, 0:NT * E].rearrange("p (t e) -> p t e", e=E),
                                             srow[:, 0:E].unsqueeze(1).to_broadcast([128, NT, E]), ALU.add))
                step(nc.vector.tensor_tensor(rk[:, :, 0:E], rk[:, :, 0:E], oh[:, :, 0, 0:E], ALU.mult))
                step(nc.vector.tensor_reduce(pos[:], rk[:, :, 0:E], X, ALU.add))
                step(nc.vector.tensor_scalar(k64[0:E, 0, 0:8], C["tile_end"][0:E, :], small[0:E, 1:2], None, ALU.is_le, ALU.add,
                                             accum_out=small[0:E, 3:4]))
                step(nc.vector.tensor_scalar(k64[0:E, 0, 0:8], C["tile_end"][0:E, :], small[0:E, 2:3], None, ALU.is_lt, ALU.add,
                                             accum_out=small[0:E, 4:5]))
                step(nc.vector.tensor_scalar(small[0:E, 5:6], small[0:E, 0:1], 0.0, None, ALU.is_gt))
                step(nc.vector.tensor_scalar(small[0:E, 6:7], small[0:E, 4:5], small[0:E, 3:4], 1.0, ALU.subtract, ALU.add))
                step(nc.vector.tensor_tensor(small[0:E, 6:7], small[0:E, 6:7], small[0:E, 5:6], ALU.mult))
                step(nc.vector.tensor_scalar(ohs[0:M, :], C["slot"][0:M, :], small[0:M, 1:2], None, ALU.is_ge))
                done(dve, nc.vector.scalar_tensor_tensor(ohs[0:M, :], C["slot"][0:M, :], small[0:M, 2:3], ohs[0:M, :],
                                                         ALU.is_lt, ALU.mult), "route_cols")
                dve.wait_ge(S["rows_ps"], 2 * r + 1)
                kc = C["kcol"][0:K, :]
                o = 2560
                step(nc.vector.tensor_scalar(k64[0:K, 0, 0:E], ps[0:K, o:o + E], kc, None, ALU.is_le))
                step(nc.vector.tensor_copy(k64[0:K, 1, 0:E], ps[0:K, o + 64:o + 64 + E]))
                step(nc.vector.scalar_tensor_tensor(k64[0:K, 0, 0:E], k64[0:K, 1, 0:E], kc, k64[0:K, 0, 0:E], ALU.is_le, ALU.subtract))
                step(nc.vector.tensor_tensor(k64[0:K, 1, 0:E], ps[0:K, o + 128:o + 128 + E], k64[0:K, 1, 0:E], ALU.subtract))
                step(nc.vector.scalar_tensor_tensor(k64[0:K, 2, 0:E], k64[0:K, 1, 0:E], kc, k64[0:K, 0, 0:E], ALU.add, ALU.mult,
                                                    accum_out=small[0:K, 11:12]))
                step(nc.vector.scalar_tensor_tensor(k64[0:K, 3, 0:E], C["expert1"][0:K, 0:E], 1.0, k64[0:K, 0, 0:E], ALU.mult, ALU.mult,
                                                    accum_out=small[0:K, 12:13]))
                step(nc.vector.tensor_scalar(small[0:K, 8:9], small[0:K, 12:13], 1.0, None, ALU.subtract))
                step(nc.vector.tensor_scalar(small[0:K, 9:10], small[0:K, 8:9], 0.0, float(weight), ALU.max, ALU.mult))
                done(dve, nc.vector.tensor_scalar(small[0:K, 10:11], small[0:K, 11:12], 128.0, None, ALU.mult), "pair_cols")
                dve.wait_ge(S["pairs_ps"], r + 1)
                step(nc.vector.tensor_copy(erow[:, 0:K], ps[:, 3072:3072 + K]))
                for c in range(2):
                    last = nc.vector.tensor_copy(offs[0:1, c, 0:K], ps[0:1, 3200 + c * 128:3200 + c * 128 + K])
                done(dve, last, "pairs_ready")

            def perm_to(r):
                for j in range(NT):
                    n = r * 18 + j
                    if n >= 2:
                        dve.wait_ge(S["perm_used"], n - 1)
                    post(nc.vector.tensor_scalar(B[1 + j % 2][:, 0:N], C["slot"], pos[:, j:j + 1], None, ALU.is_equal), "perm_made")

            def perm_from(r):
                for s_ in range(NT):
                    n = r * 18 + 9 + s_
                    dve.wait_ge(S["perm_used"], n - 1)
                    post(nc.vector.tensor_scalar(B[1 + n % 2][:, 0:N], B[3][:, 0:N], C["slotcol"][:, s_:s_ + 1], None,
                                                 ALU.is_equal), "perm_made")

            def masked_pairs(src, K, n0):
                with dve.Fori(0, K // 4) as quad:
                    k = quad * 4
                    for u in range(4):
                        dve.wait_ge(S["xm_used"], k + (n0 + u))
                        tt = dve.value_load(offs[0:1, 1, bass.ds(k + u, 1)], min_val=0, max_val=(NT - 1) * 128)
                        nc.vector.scalar_tensor_tensor(xm[:, u, :], ps[:, bass.ds(tt, 128)], erow[:, bass.ds(k + u, 1)],
                                                       src[:, bass.ds(tt, 128)], ALU.is_equal, ALU.mult).then_inc(S["xm_ready"], 1)

            route(E0, K0, 0, 2, 128)
            perm_to(0)
            dve.wait_ge(S["sorted_ready"], 1)
            dve.sem_inc(S["xm_used"], 4)
            dve.wait_ge(S["pairs_ready"], 1)
            masked_pairs(B[4], K0, 1)
            dve.wait_ge(S["hn_ready"], 1)
            u, lp, cell, fl = B[5][:, 0:N], B[4][:, 0:N], B[0][:, 0:N].bitcast(I32), B[1][:, 0:N]
            step(nc.vector.tensor_scalar(u, u, float(GRID), None, ALU.mult))
            step(nc.vector.tensor_copy(cell, u))
            step(nc.vector.tensor_copy(lp, cell))
            step(nc.vector.tensor_tensor(fl, lp, u, ALU.is_gt))
            step(nc.vector.tensor_tensor(fl, lp, fl, ALU.subtract))
            step(nc.vector.tensor_scalar(fl, fl, float(GRID - 1), None, ALU.min))
            step(nc.vector.tensor_tensor(lp, u, fl, ALU.subtract))
            picked = regA[:, 0:2 * N].rearrange("p (v n) -> p v n", v=2)
            n = 0
            for g in range(GRID):
                m = masks[:, g % 2, :]
                step(nc.vector.tensor_scalar(m, u, float(g), None, ALU.is_ge))
                for c in range(3):
                    dve.wait_ge(S["tab_ps"], n + 1)
                    o = 1536 + (n % 2) * 1024
                    src = ps[:, o:o + 1024].rearrange("p (v n) -> p v n", v=2)[:, :, 0:384]
                    dst = picked[:, :, c * 384:(c + 1) * 384]
                    if g == 0:
                        ins = nc.vector.tensor_copy(dst, src)
                    else:
                        ins = nc.vector.copy_predicated(dst, m[:, c * 384:(c + 1) * 384].unsqueeze(1).to_broadcast([128, 2, 384]), src)
                    done(dve, ins, "tab_used")
                    n += 1
            step(nc.vector.tensor_tensor(lp, lp, picked[:, 1, :], ALU.mult))
            done(dve, nc.vector.tensor_tensor(lp, lp, picked[:, 0, :], ALU.add), "hs_ready")
            masked_pairs(B[4], K0, 1 + K0)
            perm_from(0)
            dve.wait_ge(S["perm_used"], 18)
            for t in range(NT):
                last = nc.vector.tensor_scalar(HA[:, t, :], ps[:, 2560 + t * 128:2560 + (t + 1) * 128], scl[:, t:t + 1], None, ALU.mult)
            step(last)
            step(nc.vector.scalar_tensor_tensor(HA[:, 0:NT, :], HB[:, 0:NT, :], 2.0, HA[:, 0:NT, :], ALU.mult, ALU.add))
            done(dve, norm(HA, HA, 128, NT, 5), "h2_ready")
            if stop == 3:
                return

            L1STEPS = 9

            def l1_tile(j):
                def w(name, c):
                    dve.wait_ge(S[name], j * PER[name] + c)

                steps = [0]

                def own(ins):
                    steps[0] += 1
                    ins.then_inc(S["l1_step"], 1)
                    dve.wait_ge(S["l1_step"], j * L1STEPS + steps[0])

                def per_head(v, h, n):
                    return v[:, 4 * h:4 * h + 4].unsqueeze(2).to_broadcast([128, 4, n])

                nc.vector.tensor_copy(xm[:, 0, :], HA[:, j, :]).then_inc(S["xst_ready"], 1)
                w("relu_done", 1)
                qk = ps[:, 0:1024].rearrange("p (h e) -> p h e", h=16)
                for v in range(2):
                    nc.vector.scalar_tensor_tensor(feat[:, v, :, 0:64], qk, 0.0, relus[:, :, 1 - v:65 - v], ALU.max, ALU.mult)
                    last = nc.vector.scalar_tensor_tensor(feat[:, v, :, 64:128], qk, 0.0, relus[:, :, 65 - v:129 - v], ALU.min, ALU.mult)
                last.then_inc(S["prod_done"], 1)
                w("prod_done", 1)
                for v in range(2):
                    last = nc.vector.tensor_reduce(sums[:] if v == 0 else srow[:, 0:16], feat[:, v], X, ALU.add, apply_absolute_value=True)
                own(last)
                own(nc.vector.tensor_tensor(sums[:], sums[:], srow[:, 0:16], ALU.add))
                sq, sk = sums[:, 0:8], sums[:, 8:16]
                w("vb_done", 1)
                own(nc.vector.reciprocal(hsc[:, 1, :], sk))
                own(nc.vector.tensor_tensor(hsc[:, 2, :], hsc[:, 1, :], hsc[:, 1, :], ALU.mult))
                nc.vector.tensor_scalar(hsc[:, 3, :], sq, 8.0 * EPS, None, ALU.mult)
                nc.vector.tensor_copy(delta[:, :, 64], hsc[:, 1, :])
                own(nc.vector.tensor_tensor(hsc[:, 2, :], hsc[:, 2, :], hsc[:, 0, :], ALU.mult))
                nc.vector.tensor_tensor(rhs_v, vals, sk.unsqueeze(2).to_broadcast([128, NH, 64]), ALU.mult).then_inc(S["rv_done"], 1)
                for h in range(2):
                    w("gram_ps", h + 1)
                    o = BANKS[h][0] * 512
                    g = ps[:, o:o + 1024].rearrange("p (h f) -> p h f", h=4)
                    for i in range(4):
                        last = nc.vector.scalar_tensor_tensor(nt[:, 4 * h + i, :], g[:, i, 0:128], hsc[:, 2, 4 * h + i:4 * h + i + 1],
                                                              C["maskN"], ALU.mult, ALU.mult)
                    last.then_inc(S["nt_done"], 1)
                    nc.vector.tensor_tensor(ct[:, 4 * h:4 * h + 4, :], g[:, :, 0:128], C["maskC"].unsqueeze(1).to_broadcast([128, 4, 128]), ALU.mult)
                    nc.vector.tensor_tensor(smm[:, 4 * h:4 * h + 4, :], g[:, :, 128:256],
                                            C["maskS"].unsqueeze(1).to_broadcast([128, 4, 128]), ALU.mult).then_inc(S["cs_done"], 1)

                def plus_w(dst, b, h):
                    return nc.vector.tensor_tensor(dst[:, 4 * h:4 * h + 4, :], ps[:, b * 512:(b + 1) * 512].rearrange("p (h f) -> p h f", h=4),
                                                   ww[:, 4 * h:4 * h + 4, :], ALU.add)

                for h in range(2):
                    w("a_ps", h + 1)
                    plus_w(ww, BANKS[h][2], h).then_inc(S["a_done"], 1)
                for h in range(2):
                    w("x_ps", h + 1)
                    if h == 0:
                        w("a_done", 2)
                    plus_w(nn, BANKS[h][0], h).then_inc(S["x8_done"], 1)

                def scaled(n, b, h):
                    w("e_ps", n + 1)
                    e = ps[:, b * 512:b * 512 + 256].rearrange("p (h e) -> p h e", h=4)
                    nc.vector.tensor_tensor(delta[:, 4 * h:4 * h + 4, 0:64], e, per_head(hsc[:, 2, :], h, 64), ALU.mult).then_inc(S["d_done"], 1)

                for h in range(2):
                    scaled(h, BANKS[h][1], h)
                for r in range(3):
                    for h in range(2):
                        w("t_ps", 2 * r + h + 1)
                        if r == 0 and h == 0:
                            w("rv_done", 1)
                        t = ps[:, BANKS[h][2] * 512:BANKS[h][2] * 512 + 256].rearrange("p (h e) -> p h e", h=4)
                        nc.vector.tensor_tensor(resid[:, 4 * h:4 * h + 4, :], rhs_v[:, 4 * h:4 * h + 4, :], t, ALU.subtract).then_inc(S["q_done"], 1)
                    for h in range(2):
                        scaled(2 + 2 * r + h, BANKS[h][3], h)
                for h in range(2):
                    w("o_ps", h + 1)
                    o = ps[:, BANKS[h][0] * 512:BANKS[h][0] * 512 + 260].rearrange("p (h e) -> p h e", h=4)
                    hs_ = slice(4 * h, 4 * h + 4)
                    own(nc.vector.scalar_tensor_tensor(hsc[:, 4, hs_], o[:, :, 64], 8.0, hsc[:, 3, hs_], ALU.mult, ALU.add))
                    own(nc.vector.reciprocal(hsc[:, 5, hs_], hsc[:, 4, hs_]))
                    nc.vector.tensor_tensor(outs[:, hs_, :], o[:, :, 0:64], per_head(hsc[:, 5, :], h, 64), ALU.mult).then_inc(S["o_done"], 1)
                w("y_ps", 1)
                nc.vector.tensor_tensor(HB[:, j, :], ps[:, 3072:3200], HA[:, j, :], ALU.add).then_inc(S["y_done"], 1)
                assert steps[0] == L1STEPS, steps

            for j in range(NT):
                l1_tile(j)
            dve.wait_ge(S["y_done"], NT)
            step(norm(HB, HB, 128, NT, 6))
            affine(HB, 128, NT, R["l1_g"], R["l1_b"], "dve_step")
            step(nc.vector.tensor_tensor(HB[:, 0:NT, :], HB[:, 0:NT, :], HA[:, 0:NT, :], ALU.add))
            done(dve, norm(HB, HB, 128, NT, 7), "h3_ready")
            if stop == 4:
                return
            dve.wait_ge(S["gate_ps"], 1)
            lg = key[:, :, 0:E1]
            step(nc.vector.tensor_copy(lg, ps[:, 1536:1536 + NT * E1].rearrange("p (t e) -> p t e", e=E1)))
            step(nc.vector.tensor_reduce(kmax[:], lg, X, ALU.max))
            done(dve, nc.vector.tensor_tensor(wtop[:], kmax[:], kmax[:], ALU.subtract), "top_ready")
            step(nc.vector.tensor_tensor(lg, lg, kmax[:].unsqueeze(2).to_broadcast([128, NT, E1]), ALU.is_equal))
            step(nc.vector.tensor_tensor(lg, lg, C["prefer"].unsqueeze(1).to_broadcast([128, NT, E1]), ALU.mult))
            step(nc.vector.tensor_reduce(kmax[:], lg, X, ALU.max))
            done(dve, nc.vector.tensor_tensor(oh[:, :, 0, 0:E1], lg, kmax[:].unsqueeze(2).to_broadcast([128, NT, E1]), ALU.is_equal), "oh_ready")
            dve.wait_ge(S["wtop_exp"], 1)
            step(nc.vector.reciprocal(scl[:], wtop[:]))
            step(nc.vector.tensor_tensor(scl[:], scl[:], wtop[:], ALU.mult))
            route(E1, K1, 1, 1, INNER)
            perm_to(1)
            dve.wait_ge(S["sorted_ready"], 2)
            dve.wait_ge(S["es_copied"], 1)
            dve.sem_inc(S["g_done"], 1)
            with dve.Fori(0, K1 // 4) as quad:
                k = quad * 4
                for u in range(4):
                    dve.wait_ge(S["xm_used"], k + (2 * K0 + 1 + u))
                    tt = dve.value_load(offs[0:1, 1, bass.ds(k + u, 1)], min_val=0, max_val=(NT - 1) * 128)
                    nc.vector.scalar_tensor_tensor(xm[:, u, :], B[5][:, bass.ds(tt, 128)], erow[:, bass.ds(k + u, 1)],
                                                   B[4][:, bass.ds(tt, 128)], ALU.is_equal, ALU.mult).then_inc(S["xm_ready"], 1)
                for u in range(4):
                    dve.wait_ge(S["silu_done"], k + (u + 1))
                    dve.wait_ge(S["xm_used"], k + (2 * K0 + 4 + u + 1))
                    if u >= 2:
                        dve.wait_ge(S["gT_ps"], k + u)
                    else:
                        dve.wait_ge(S["gT_ps"], k + 1)
                    nc.vector.tensor_tensor(gg[:, u % 2, :], ps[:, (u % 2) * 1024 + 512:(u % 2) * 1024 + 1024], sg[:, u % 2, :], ALU.mult).then_inc(S["g_done"], 1)
            perm_from(1)
            dve.wait_ge(S["perm_used"], 36)
            for t in range(NT):
                last = nc.vector.tensor_scalar(HA[:, t, :], ps[:, 2560 + t * 128:2560 + (t + 1) * 128], scl[:, t:t + 1], None, ALU.mult)
            step(last)
            dve.wait_ge(S["sh_ps"], 1)
            step(nc.vector.tensor_tensor(HA[:, 0:NT, :], ps[:, 0:N].rearrange("p (t d) -> p t d", d=128), HA[:, 0:NT, :], ALU.add))
            step(nc.vector.tensor_tensor(HA[:, 0:NT, :], HA[:, 0:NT, :], HB[:, 0:NT, :], ALU.add))
            done(dve, norm(HA, HA, 128, NT, 8), "y_final")


def pack(a):
    import numpy as np
    f = np.float32
    o = {}
    x = a["x"].reshape(NIMG, 3, 12, 8, 12, 2, 4)
    v = np.zeros((3, 8, 4, 2, NIMG + 1, 12, 12), f)
    v[:, :, :, :, :NIMG] = x.transpose(1, 3, 6, 5, 0, 2, 4)
    o["blocks"] = v.reshape(KF, 2, NBLK)

    def part(w, hy, hx, k):
        w = w.reshape(-1, 3, 2, 8, 2, 2, 4)
        return w[:, :, hy, :, hx, k, :].transpose(1, 2, 3, 0).reshape(KF, -1)

    wm, wx, wy = a["L0_tok_W_main"], a["L0_tok_W_sx"], a["L0_tok_W_sy"]
    tokw = np.zeros((KF, 8, 2, 4, 2, 16), f)
    n = 0
    for hy in range(2):
        for hx in range(2):
            for k in range(2):
                own, far = tokw[:, n, 0], tokw[:, n, 1]
                own[:, :, 1] = part(wm, hy, hx, k).reshape(KF, 4, 16)
                own[:, 1 - hx, 0] = part(wx, hy, 1 - hx, k)
                own[:, 3 - hy, 0] = part(wy, 1 - hy, hx, k)
                far[:, hx, 0] = part(wx, hy, 1 - hx, k)
                far[:, 2 + hy, 0] = part(wy, 1 - hy, hx, k)
                n += 1
    tokw = tokw.reshape(KF, -1)
    o["tokw"] = tokw
    bm, bx, by = (a[n].reshape(-1, 16) for n in ("L0_tok_b_main", "L0_tok_b_sx", "L0_tok_b_sy"))
    bs = np.concatenate([bx, bx, by, by])
    rows = {"tok_g": a["L0_tok_ln_g"], "tok_b": a["L0_tok_ln_b"], "v_b": a["L0_attn_v_b"], "out_b": a["L0_attn_out_b"],
            "l1_g": a["L1_attn_ln_g"], "l1_b": a["L1_attn_ln_b"]}
    o["rows"] = np.concatenate([rows[n] for n in ROWS])
    two = lambda v: np.concatenate([v, v], axis=-1)
    cols = {"tok_bias": np.stack([bs, bm], axis=1).reshape(-1), "ke_b1": a["L0_attn_ke_b1"], "qe_b1": a["L0_attn_qe_b1"], "ke_b2": two(a["L0_attn_ke_b2"]),
            "qe_b2": two(a["L0_attn_qe_b2"]), "amp_b": two(a["L0_attn_amp_b"]), "ln_g": a["L0_attn_ln_g"],
            "ln_b": a["L0_attn_ln_b"], "gamma": a["L0_ffn_gamma"], "beta": a["L0_ffn_beta"]}
    o["cols"] = np.stack([cols[n] for n in COLS], axis=1)
    o["scale"] = a["L0_ffn_scale"]
    o["attw"] = np.concatenate([a["L0_attn_ke_w1"], a["L0_attn_qe_w1"], two(a["L0_attn_ke_w2"]), two(a["L0_attn_qe_w2"]),
                                two(a["L0_attn_amp_w"]), a["L0_attn_v_w"], a["L0_attn_out_w"]], axis=1)
    o["wd"] = a["L0_ffn_Wd"].transpose(2, 0, 1).reshape(128, -1)
    o["wu"] = a["L0_ffn_Wu"].transpose(2, 0, 1).reshape(128, -1)
    tab = np.stack([a["L0_ffn_spline_bases"], a["L0_ffn_spline_slopes"]], axis=0)
    o["tab"] = tab.transpose(1, 3, 0, 2).reshape(E0, -1)
    w = a["L1_attn_W_qkvb"].reshape(NH, 3 * HD + 1, 128)
    o["qkvw"] = np.concatenate([w[:, i * HD:(i + 1) * HD].reshape(NH * HD, 128) for i in range(3)] + [w[:, 3 * HD]], axis=0).T
    o["wo"] = a["L1_attn_W_o"].T.reshape(4, 128, 128).transpose(1, 0, 2).reshape(128, -1)
    o["gate"] = a["L1_ffn_gate_w"].T
    o["w1"] = a["L1_ffn_w1"].transpose(2, 0, 1).reshape(128, -1)
    o["w3"] = a["L1_ffn_w3"].transpose(2, 0, 1).reshape(128, -1)
    o["w2"] = a["L1_ffn_w2"].reshape(E1, 128, 4, 128).transpose(3, 0, 2, 1).reshape(128, -1)
    o["sw1"] = a["L1_ffn_sw1"].T
    o["sw2"] = a["L1_ffn_sw2"].reshape(128, 4, 128).transpose(2, 1, 0).reshape(128, -1)

    c = {}
    i, j = np.arange(128)[:, None], np.arange(128)[None, :]
    c["ident"] = i == j
    c["maskimg"] = ((i // NPATCH == j // NPATCH) & (i <= j) & (i < PI))[:, :PI]
    c["maskN"] = (i // 8 == j // 8) & (i < j)
    c["maskC"] = (i // 32 == j // 32) & (i // 8 < j // 8)
    c["maskS"] = (i // 32 == j // 32) & (i <= j)
    c["triS"] = i < j
    c["triI"] = i <= j
    c["slot"] = np.broadcast_to(np.arange(N), (128, N))
    c["tile_end"] = np.broadcast_to(np.arange(1, 9) * 128, (128, 8))
    c["expert1"] = np.broadcast_to(np.arange(1, E0 + 1), (128, E0))
    c["invnorm"] = 1.0 / np.sqrt((np.arange(128) % NPATCH + 1) * 64.0)[:, None]
    c["sin_scale"] = np.where(i < 64, -PI32, PI32)
    c["sin_bias"] = np.where(i < 64, PI32 / 2, 0.0)
    c["kcol"] = i
    c["ecol"] = i
    c["one"] = i * 0 + 1
    c["slotcol"] = np.arange(NT)[None, :] * 128 + i
    e = np.arange(E0)
    c["keybias"] = np.broadcast_to(-4096.0 * (e // 8) - e % 8, (128, E0))
    c["prefer"] = np.broadcast_to(8.0 - np.arange(E1), (128, E1))
    o["consts"] = np.concatenate([np.asarray(c[n], f) for n, _ in CONST], axis=1)
    return {k: np.ascontiguousarray(v, f) for k, v in o.items()}


def kernel(**inputs):
    import numpy as np
    from concourse import bacc
    from concourse.bass_utils import run_bass_kernel_spmd

    packed = pack({k: np.asarray(v) for k, v in inputs.items()})
    nc = bacc.Bacc("TRN2", target_bir_lowering=False, num_devices=1)
    A = {k: nc.dram_tensor(f"in_{k}", v.shape, F32, kind="ExternalInput").ap() for k, v in packed.items()}
    out = nc.dram_tensor("out", (128, NT, 128), F32, kind="ExternalOutput").ap()
    vit_kernel(nc, A, out)
    got = run_bass_kernel_spmd(nc, [{f"in_{k}": v for k, v in packed.items()}], core_ids=[0]).results[0]["out"]
    return np.ascontiguousarray(got.reshape(4, NIMG, NT, D).transpose(1, 2, 0, 3).reshape(NIMG, NPATCH, D))
```

```python
from contextlib import ExitStack

import concourse.bass as bass
from concourse import mybir
from concourse.alu_op_type import AluOpType as ALU

F32 = mybir.dt.float32
BF16 = mybir.dt.bfloat16
I32 = mybir.dt.int32
U8 = mybir.dt.uint8
ACT = mybir.ActivationFunctionType
X = mybir.AxisListType.X

D = 128
NIMG, NPATCH = 32, 36
TI = 11
PI = 3 * NPATCH
NI = TI * PI
NT = 9
N = NT * 128
IMG = 12 * 12
KF = 96
NBLK = (NIMG + 1) * IMG
CH = 396
EPS = 1e-5
PI32 = 3.1415927410125732
BELOW1 = 0.99999994
E0, E1 = 64, 8
GRID = 16
NH, HD = 8, 64
INNER = 512
NOV = NT - 1
GRP = 4
TILES4 = [(0, 4), (4, 8), (8, 11)]
TILES9 = [(0, 4), (4, 8), (8, 9)]

CONST = [("ident", 128), ("maskimg", PI), ("maskN", 128), ("maskC", 128), ("maskS", 128), ("triS", 128), ("triI", 128),
         ("slot", N), ("tile_end", 8), ("expert1", E0), ("invnorm", 1), ("sin_scale", 1), ("sin_bias", 1), ("kcol", 1), ("k128", 1),
         ("slotcol", NT), ("keybias", E0), ("prefer", E1), ("one", 1)]
ROWS = ["tok_g", "tok_b", "v_b", "out_b", "l1_g", "l1_b"]
COLS = ["tok_bias", "ke_b1", "qe_b1", "ke_b2", "qe_b2", "amp_b", "ln_g", "ln_b", "gamma", "beta"]


def places():
    at, o = {}, 0
    for n, w in CONST:
        at[n] = (o, o + w)
        o += w
    return at, o


CAT, NCONST = places()


def vit_kernel(nc, A, out, stop=99, dbg=None):
    with ExitStack() as ctx:
        def sb(name, shape, dt=F32):
            return ctx.enter_context(nc.sbuf_tensor(name, shape, dt))

        cst = sb("cst", [128, NCONST])
        C = {n: cst[:, a:b] for n, (a, b) in CAT.items()}
        rows = sb("rows", [128, len(ROWS) * 128])
        R = {n: rows[:, i * 128:(i + 1) * 128] for i, n in enumerate(ROWS)}
        scale_row = sb("scale_row", [128, E0])
        cols = sb("cols", [128, len(COLS)])
        Cc = {n: cols[:, i:i + 1] for i, n in enumerate(COLS)}
        regA = sb("regA", [128, 2 * NBLK])
        blocks = regA[0:KF, :].rearrange("p (k n) -> p k n", k=2)
        tab = regA[:, 0:4096]
        tab_hi = regA[:, 4096:6144].bitcast(BF16)
        tab_lo = regA[0:E0, 6144:8192].bitcast(BF16)
        regW = sb("regW", [128, 2 * E0 * 128])
        wd, wu = regW[:, 0:E0 * 128], regW[:, E0 * 128:]
        W1 = E1 * INNER
        w1, w3, w2 = regW[:, 0:W1], regW[:, W1:2 * W1], regW[:, 2 * W1:3 * W1]
        sw1, sw2 = regW[:, 3 * W1:3 * W1 + INNER], regW[:, 3 * W1 + INNER:3 * W1 + 2 * INNER]
        gate = sb("gate", [128, E1])
        tokw = sb("tokw", [KF, 8 * 256])
        attw = sb("attw", [128, 7 * 128])
        qkvw = sb("qkvw", [128, 3 * 512 + 8])
        wo = sb("wo", [128, 4 * 128])
        B = [sb(f"B{i}", [128, NI if i < 4 else N + 128]) for i in range(6)]
        HA = sb("HA", [128, TI, 128])
        HB = sb("HB", [128, TI, 128])
        stats = sb("stats", [128, TI, 6])
        mv = sb("mv", [128, TI, 2])
        rstd = sb("rstd", [128, TI])
        mhalf = sb("mhalf", [128, TI])
        zb = sb("zb", [128, 512], BF16)
        oneb = sb("oneb", [128, 128], BF16)
        trib = sb("trib", [128, 128], BF16)
        sgT = sb("sgT", [128, N], BF16)
        tsum = sb("tsum", [128, E0])
        csum = sb("csum", [128, 8])
        tsig8 = sb("tsig8", [128, E0], BF16)
        csigb = sb("csigb", [128, E0], BF16)
        key = sb("key", [128, NT, E0])
        kmax = sb("kmax", [128, NT])
        wtop = sb("wtop", [128, NT])
        oh = sb("oh", [128, NT, 2, E0], BF16)
        rk = sb("rk", [128, NT, E0])
        small = sb("small", [128, 16])
        srow = sb("srow", [128, E0])
        pos = sb("pos", [128, NT])
        ohs = sb("ohs", [128, N], BF16)
        k64 = sb("k64", [128, 6, E0])
        offs = sb("offs", [128, E0 + NOV], I32)
        ovx = sb("ovx", [128, NOV], I32)
        xm = sb("xm", [128, 4, 128])
        scl = sb("scl", [128, NT])
        masks = sb("masks", [128, 2, N], U8)
        def heads(t):
            return t[:, 0:NH * 128].rearrange("p (h f) -> p h f", h=NH)

        feat = regA[:, 0:4096].rearrange("p (v h f) -> p v h f", v=2, h=16)
        featT = regA[:, 4096:8192].rearrange("p (h v f) -> p h v f", h=NH, v=2)
        vals = regA[:, 8192:8704].rearrange("p (h e) -> p h e", h=NH)
        outs = regA[:, 8704:9216].rearrange("p (h e) -> p h e", h=NH)
        relus = regW[:, 13312:13312 + 16 * 130].rearrange("p (h f) -> p h f", h=16)
        rhs_v = regW[:, 15392:15904].rearrange("p (h e) -> p h e", h=NH)
        delta = B[0][:, 0:NH * 65].rearrange("p (h e) -> p h e", h=NH)
        resid = B[0][:, 520:520 + 512].rearrange("p (h e) -> p h e", h=NH)
        nt, ct, smm, nn, n2 = (heads(B[i]) for i in range(1, 6))
        ww, n2t = heads(sb("ww", [128, NH * 128])), heads(sb("n2t", [128, NH * 128]))
        ov_wd, ov_wu = (t.rearrange("p h f -> p (h f)") for t in (ww, n2t))
        sums = sb("sums", [128, 16])
        hsc = sb("hsc", [128, 6, NH])
        gs = regA[:, 0:4 * N]
        sg = regA[:, 4608:5632].rearrange("p (u i) -> p u i", u=2)
        gg = regA[:, 5632:6656].rearrange("p (u i) -> p u i", u=2)
        ov1 = regW[:, 13312:16384].rearrange("p (u w i) -> p u w i", u=2, w=3)
        ps = ctx.enter_context(nc.psum_tensor("ps", [128, 4096], F32))

        def bank(b, n=512, p=128):
            return ps[0:p, b * 512:b * 512 + n]

        S = {}

        def sems(*names):
            for n in names:
                S[n] = ctx.enter_context(nc.semaphore(n))

        sems("in_const", "in_tok", "in_blocks0", "in_blocks1", "in_blocks2", "in_wd", "in_wu", "in_att", "in_tab", "in_qkv", "in_ffn", "stored")
        sems("dve_step", "act_step", "pool_step", "consts_made", "pads_zero", "var_ready", "rstd_ready")
        sems("tok_ps", "tok_own", "tok_used", "h0_ready", "job_ps", "job_used", "z0_ready", "phase_held", "kq_ready", "score_ready",
             "retr_ready", "h1_ready", "h1b_ready", "z1_ready", "dve_h1b", "tab_rest", "y_final", "sgT_ready", "sig_ready", "key_ps", "key_used")
        sems("oh_ready", "rank_ps", "cnt_ready", "start_ps", "route_cols", "rows_ps", "pair_cols", "pairs_ps", "pairs_ready",
             "perm_made", "perm_used", "sorted_ps", "sorted_ready", "win_ps", "win_copied", "ov0_ready", "yT_ps",
             "accs_copied", "hn_ready", "posrow_ready")
        sems("tab_split", "tab_ps", "tab_used", "mask_ready", "mask_used", "hs_ready", "h2_ready", "h2T_ready", "rows_used")
        sems("xst_ready", "qkv_ps", "relu_done", "vb_done", "prod_done", "ft_ps", "ft_done", "gram_ps", "nt_done", "cs_done",
             "n_ps", "n_done", "w_done", "n2_ps", "n2_done", "a_ps", "a_done", "n4_done", "x_ps", "x8_done", "e_ps",
             "d_done", "t_ps", "q_done", "o_ps", "o_done", "ot_ps", "ot_done", "y_ps", "y_done", "l1_step", "xT_ps", "xT_done", "rv_done")
        sems("h3_ready", "h3T_ready", "gate_ps", "s1_ps", "s1_used", "sh_ps", "up_ps", "silu_done", "up_used", "g_done",
             "y1_ps", "y1_copied", "ov1_ready", "ffn_wd_used", "h3T_ps", "top_ready", "wtop_exp", "es_copied")
        block = ctx.enter_context(nc.Block())
        count = {}
        WG = (E0 + NOV) // GRP

        def window_starts(eng, a, n):
            return nc.values_load_multi_w_load_instructions(
                offs[0:1, a:a + n], engines=[eng.engine], min_val=0, max_val=N,
                skip_runtime_bounds_check_because="slots, from counts of the N tokens, or N for the padding")[1]

        def late_weights(eng, a, n, top):
            return nc.values_load_multi_w_load_instructions(
                ovx[0:1, a:a + n], engines=[eng.engine], min_val=0, max_val=top,
                skip_runtime_bounds_check_because="an expert's number times its width, zero for unused windows")[1]

        def post(ins, name):
            ins.then_inc(S[name], 1)
            count[name] = count.get(name, 0) + 1

        def done(eng, ins, name):
            post(ins, name)
            eng.wait_ge(S[name], count[name])

        J = {}
        jn = 0
        for what in ["tokT", "h0T", "w1k", "w1q", "amp", "w2k", "w2q", "v", "score", "retr", "rnT", "att", "h1T", "h1B", "z1T"]:
            J[what] = jn
            jn += 3

        def job_bank(n):
            return ((n + 6) % 8) * 512

        PER = dict(xst_ready=1, xT_ps=1, xT_done=1, qkv_ps=1, relu_done=1, vb_done=1, prod_done=1, ft_ps=8, ft_done=8, gram_ps=2,
                   nt_done=2, cs_done=2, n_ps=2, n_done=2, w_done=2, n2_ps=2, n2_done=2, a_ps=2, a_done=2, n4_done=2, x_ps=2,
                   x8_done=2, e_ps=8, d_done=8, t_ps=6, q_done=6, o_ps=2, o_done=2, ot_ps=1, ot_done=1, y_ps=1, y_done=1, rv_done=1)
        BANKS = [(0, 1, 4, 6), (2, 3, 5, 7)]

        @block.sync
        def _(sp):
            def load(dst, src, name):
                sp.dma_start(dst, src).then_inc(S[name], 16)

            load(tokw[:], A["tokw"], "in_tok")
            for c in range(3):
                a, b = 11 * IMG * c, 11 * IMG * (c + 1)
                load(blocks[:, :, a:b], A["blocks"][:, :, a:b], f"in_blocks{c}")
            load(rows[:], A["rows"].partition_broadcast(128), "in_const")
            load(cst[:], A["consts"], "in_const")
            load(cols[:], A["cols"], "in_const")
            load(scale_row[:], A["scale"].partition_broadcast(128), "in_const")
            load(attw[:], A["attw"], "in_att")
            load(wd, A["wd"], "in_wd")
            load(wu, A["wu"], "in_wu")
            load(qkvw[:], A["qkvw"], "in_qkv")
            load(wo[:], A["wo"], "in_qkv")
            load(gate[:], A["gate"], "in_qkv")
            sp.wait_ge(S["tok_ps"], 3)
            load(tab[0:E0, :], A["tab"], "in_tab")
            load(tab[E0:128, :], A["tab"], "in_tab")
            if stop > 3:
                sp.wait_ge(S["win_ps"], 2 * WG)
                for dst, n in ((w1, "w1"), (w3, "w3"), (w2, "w2"), (sw1, "sw1"), (sw2, "sw2")):
                    load(dst, A[n], "in_ffn")
            if stop < 5:
                for n, v in (("in_wd", 16), ("in_wu", 16), ("in_att", 16), ("in_tab", 32), ("in_qkv", 48)):
                    sp.wait_ge(S[n], v)
            if stop == 1:
                sp.wait_ge(S["h0_ready"], 1)
                sp.dma_start(dbg[0:PI, :], HA[0:PI, :, :].rearrange("p a b -> p (a b)")).then_inc(S["stored"], 16)
            elif stop == 2:
                sp.wait_ge(S["h1b_ready"], 3)
                sp.dma_start(dbg[:, 0:N], HB[:, 0:NT, :].rearrange("p a b -> p (a b)")).then_inc(S["stored"], 16)
            elif stop == 3:
                sp.wait_ge(S["h2_ready"], 1)
                sp.dma_start(dbg[:, 0:N], HA[:, 0:NT, :].rearrange("p a b -> p (a b)")).then_inc(S["stored"], 16)
            elif stop == 4:
                sp.wait_ge(S["h3_ready"], 1)
                sp.dma_start(dbg[:, 0:N], HB[:, 0:NT, :].rearrange("p a b -> p (a b)")).then_inc(S["stored"], 16)
            else:
                sp.wait_ge(S["y_final"], 1)
                sp.dma_start(out, HA[:, 0:NT, :]).then_inc(S["stored"], 16)
            sp.wait_ge(S["stored"], 16)

        @block.tensor
        def _(pe):
            I = C["ident"]

            pe.wait_ge(S["in_tok"], 16)
            for c in range(3):
                pe.wait_ge(S[f"in_blocks{c}"], 16)
                n = 0
                for y in range(2):
                    for x in range(2):
                        for k in range(2):
                            v = blocks[:, k, c * 11 * IMG:(c + 1) * 11 * IMG]
                            v = v.rearrange("p (m y j x) -> p y x m j", y=2, x=2, j=6)[:, y, x]
                            for i in range(2):
                                o = (2 * c + i) * 512
                                last = nc.tensor.matmul(ps[:, o:o + CH], tokw[:, n * 256 + i * 128:n * 256 + i * 128 + 128], v,
                                                        start=(n == 0), stop=(n == 7))
                            n += 1
                post(last, "tok_ps")

            def job(n):
                if n >= 8:
                    pe.wait_ge(S["job_used"], n - 7)
                return job_bank(n)

            def tiles_T(what, src, p, groups, w):
                for g, (a, b) in enumerate(groups):
                    o = job(J[what] + g)
                    for t in range(a, b):
                        last = nc.tensor.transpose(ps[:, o + (t - a) * w:o + (t - a) * w + w], src[0:p, t, :], I[0:p, 0:p])
                    post(last, "job_ps")

            def columns(what, w, src, ready):
                for g in range(3):
                    o = job(J[what] + g)
                    pe.wait_ge(S["job_used"], ready + g + 1)
                    post(nc.tensor.matmul(ps[:, o:o + CH], w, src[:, g * CH:(g + 1) * CH], start=True, stop=True), "job_ps")

            def att_w(i):
                return attw[:, i * 128:(i + 1) * 128]

            pe.wait_ge(S["in_const"], 64)
            pe.wait_ge(S["tok_used"], 3)
            for g, (a, b) in enumerate(TILES4):
                o = job(J["tokT"] + g)
                for t in range(a, b):
                    last = nc.tensor.transpose(ps[0:PI, o + (t - a) * 128:o + (t - a) * 128 + 128],
                                               B[1][:, t * PI:(t + 1) * PI], I)
                post(last, "job_ps")
            if stop == 1:
                return
            pe.wait_ge(S["h0_ready"], 1)
            tiles_T("h0T", HA, PI, TILES4, PI)
            pe.wait_ge(S["in_att"], 16)
            columns("w1k", att_w(0), B[0], J["h0T"])
            columns("w1q", att_w(1), B[0], J["h0T"])
            columns("amp", att_w(4), B[0], J["h0T"])
            columns("w2k", att_w(2), B[1], J["w1k"])
            columns("w2q", att_w(3), B[2], J["w1q"])
            for g, (a, b) in enumerate(TILES4):
                o = job(J["v"] + g)
                for t in range(a, b):
                    last = nc.tensor.matmul(ps[0:PI, o + (t - a) * 128:o + (t - a) * 128 + 128],
                                            B[0][:, t * PI:(t + 1) * PI], att_w(5), start=True, stop=True)
                post(last, "job_ps")
            pe.wait_ge(S["kq_ready"], 2)
            for g, (a, b) in enumerate(TILES4):
                o = job(J["score"] + g)
                for t in range(a, b):
                    last = nc.tensor.matmul(ps[0:PI, o + (t - a) * PI:o + (t - a) * PI + PI],
                                            B[3][:, t * PI:(t + 1) * PI], B[4][:, t * PI:(t + 1) * PI],
                                            start=True, stop=True)
                post(last, "job_ps")
            for g, (a, b) in enumerate(TILES4):
                o = job(J["retr"] + g)
                pe.wait_ge(S["score_ready"], g + 1)
                if g == 0:
                    pe.wait_ge(S["z0_ready"], 1)
                for t in range(a, b):
                    last = nc.tensor.matmul(ps[0:PI, o + (t - a) * 128:o + (t - a) * 128 + 128],
                                            B[5][0:PI, t * PI:(t + 1) * PI], HB[0:PI, t, :], start=True, stop=True)
                post(last, "job_ps")
            pe.wait_ge(S["retr_ready"], 1)
            tiles_T("rnT", HB, PI, TILES4, PI)
            for g, (a, b) in enumerate(TILES4):
                o = job(J["att"] + g)
                if g == 0:
                    pe.wait_ge(S["job_used"], J["rnT"] + 3)
                for t in range(a, b):
                    last = nc.tensor.matmul(ps[0:PI, o + (t - a) * 128:o + (t - a) * 128 + 128],
                                            B[1][:, t * PI:(t + 1) * PI], att_w(6), start=True, stop=True)
                post(last, "job_ps")
            pe.wait_ge(S["h1_ready"], 1)
            tiles_T("h1T", HA, PI, TILES4, PI)
            for g, (a, b) in enumerate(TILES9):
                o = job(J["h1B"] + g)
                if g == 0:
                    pe.wait_ge(S["job_used"], J["h1T"] + 3)
                for t in range(a, b):
                    last = nc.tensor.transpose(ps[:, o + (t - a) * 128:o + (t - a) * 128 + 128],
                                               B[0][:, t * 128:(t + 1) * 128], I)
                post(last, "job_ps")
            if stop == 2:
                return
            pe.wait_ge(S["z1_ready"], 1)
            tiles_T("z1T", HA, 128, TILES9, 128)

            pe.wait_ge(S["sig_ready"], 1)
            pe.wait_ge(S["job_used"], J["z1T"] + 3)
            for t in range(NT):
                for i, w in enumerate((tsig8, csigb)):
                    last = nc.tensor.matmul(ps[:, t * E0:(t + 1) * E0], sgT[:, t * 128:(t + 1) * 128], w[:],
                                            start=(i == 0), stop=(i == 1))
            post(last, "key_ps")

            def route(E, r, dup):
                pe.wait_ge(S["oh_ready"], r + 1)
                for j in range(NT):
                    for i in range(j + 1):
                        nc.tensor.matmul(ps[:, j * E:(j + 1) * E], trib[:] if i == j else oneb[:], oh[:, i, 0, 0:E],
                                         start=(i == 0), stop=(i == j))
                M = dup * E
                for i in range(NT):
                    last = nc.tensor.matmul(ps[0:M, 1024:1025], oh[:, i, 0:dup, 0:E], oneb[:, 0:1],
                                            start=(i == 0), stop=(i == NT - 1))
                post(last, "rank_ps")
                pe.wait_ge(S["cnt_ready"], r + 1)
                cnt = small[0:E, 0:1]
                tri = C["triS"][0:E, 0:E]
                for d in range(dup):
                    nc.tensor.matmul(ps[d * E:d * E + E, 1536:1537], tri, cnt, start=True, stop=True)
                post(nc.tensor.matmul(ps[:, 2048:2048 + E], cnt.to_broadcast([E, 128]), tri, start=True, stop=True), "start_ps")
                pe.wait_ge(S["route_cols"], r + 1)
                o = 2560
                late, late128, last_slot = small[0:E, 3:4], small[0:E, 4:5], small[0:E, 5:6]
                nc.tensor.matmul(ps[0:NOV, o:o + E], late.to_broadcast([E, NOV]), C["triI"][0:E, 0:E], start=True, stop=True)
                nc.tensor.matmul(ps[0:NOV, o + 64:o + 64 + E], late.to_broadcast([E, NOV]), tri, start=True, stop=True)
                nc.tensor.matmul(ps[0:NOV, o + 128:o + 128 + E], last_slot.to_broadcast([E, NOV]), I[0:E, 0:E], start=True, stop=False)
                post(nc.tensor.matmul(ps[0:NOV, o + 128:o + 128 + E], late128.to_broadcast([E, NOV]), tri, start=False, stop=True), "rows_ps")
                pe.wait_ge(S["pair_cols"], r + 1)
                for c in range(2):
                    last = nc.tensor.matmul(ps[0:1, 3072 + c * 128:3072 + c * 128 + NOV], small[0:NOV, 9 + c:10 + c], I[0:NOV, 0:NOV],
                                            start=True, stop=True)
                post(last, "pairs_ps")
                pe.wait_ge(S["pairs_ready"], r + 1)
                for j in range(NT):
                    last = nc.tensor.matmul(ps[:, 1536 + j * 128:1536 + (j + 1) * 128], pos[:, j:j + 1].to_broadcast([128, 128]),
                                            I, start=True, stop=True)
                post(last, "rows_ps")

            def sort(src, r):
                for j in range(NT):
                    n = r * 18 + j
                    if j == 0:
                        pe.wait_ge(S["posrow_ready"], r + 1)
                    pe.wait_ge(S["perm_made"], n + 1)
                    for g in range(3):
                        last = nc.tensor.matmul(ps[:, 1536 + g * 512:1536 + g * 512 + 384], src[:, j, :],
                                                B[1 + j % 2][:, g * 384:(g + 1) * 384], start=(j == 0), stop=(j == NT - 1))
                    post(last, "perm_used")

            def zero_acc():
                for b, (s, e) in enumerate(TILES9):
                    nc.tensor.matmul(bank(5 + b, (e - s) * 128), zb[:, 0:128], zb[:, 0:(e - s) * 128], start=True, stop=False,
                                     skip_group_check=True)

            def unsort(src, r):
                zero_acc()
                for s_ in range(NT):
                    n = r * 18 + 9 + s_
                    pe.wait_ge(S["perm_made"], n + 1)
                    for i in range(NT):
                        last = nc.tensor.matmul(ps[:, 2560 + i * 128:2560 + (i + 1) * 128],
                                                B[1 + n % 2][:, i * 128:(i + 1) * 128], src[:, s_, :],
                                                start=False, stop=(s_ == NT - 1), skip_group_check=True)
                    post(last, "perm_used")

            def expert_windows(w, late, p):
                for g in range(WG):
                    at = window_starts(pe, g * GRP, GRP)
                    if g >= 4 or p > 0:
                        pe.wait_ge(S["win_copied"], (p * WG + g - 3) * GRP)
                    if g * GRP == E0:
                        pe.wait_ge(S["ov0_ready"], p + 1)
                    for i in range(GRP):
                        e = g * GRP + i
                        wt = w[:, e * 128:(e + 1) * 128] if e < E0 else late[:, (e - E0) * 128:(e - E0 + 1) * 128]
                        o = (g % 4) * 512 + i * 128
                        last = nc.tensor.matmul(ps[:, o:o + 128], wt, B[4][:, bass.ds(at[i], 128)], start=True, stop=True)
                    post(last, "win_ps")

            def columns_to_rows(r):
                for t in range(NT):
                    last = nc.tensor.transpose(ps[:, 1536 + t * 128:1536 + (t + 1) * 128], B[5][:, t * 128:(t + 1) * 128], I)
                post(last, "yT_ps")

            route(E0, 0, 2)
            sort(HA, 0)
            pe.wait_ge(S["in_wd"], 16)
            pe.wait_ge(S["sorted_ready"], 1)
            pe.wait_ge(S["pads_zero"], 1)
            expert_windows(wd, ov_wd, 0)
            pe.wait_ge(S["tab_split"], 1)
            pe.wait_ge(S["hn_ready"], 1)
            n = 0
            for g in range(GRID):
                for c in range(3):
                    if n >= 2:
                        pe.wait_ge(S["tab_used"], n - 1)
                    for v in range(2):
                        o = 1536 + (n % 2) * 1024 + v * 512
                        w = (g * 2 + v) * 128
                        nc.tensor.matmul(ps[:, o:o + 384], tab_hi[:, w:w + 128], ohs[:, c * 384:(c + 1) * 384],
                                         start=True, stop=False)
                        last = nc.tensor.matmul(ps[:, o:o + 384], tab_lo[:, w:w + 128], ohs[0:E0, c * 384:(c + 1) * 384],
                                                start=False, stop=True)
                    post(last, "tab_ps")
                    n += 1
            pe.wait_ge(S["hs_ready"], 1)
            pe.wait_ge(S["in_wu"], 16)
            expert_windows(wu, ov_wu, 1)
            pe.wait_ge(S["win_copied"], 2 * WG * GRP)
            columns_to_rows(0)
            pe.wait_ge(S["accs_copied"], 1)
            unsort(HA, 0)
            if stop == 3:
                return

            def l1_tile(j):
                def w(name, c):
                    pe.wait_ge(S[name], j * PER[name] + c)

                w("xst_ready", 1)
                w("y_done", 0)
                nc.tensor.transpose(ps[:, 1664:1792], xm[:, 0, :], I).then_inc(S["xT_ps"], 1)
                w("xT_done", 1)
                for i in range(3):
                    nc.tensor.matmul(bank(i), xm[:, 1, :], qkvw[:, i * 512:(i + 1) * 512], start=True, stop=True)
                nc.tensor.matmul(bank(3, NH), xm[:, 1, :], qkvw[:, 1536:1536 + NH], start=True, stop=True).then_inc(S["qkv_ps"], 1)
                w("prod_done", 1)
                for h in range(NH):
                    if h >= 4:
                        w("ft_done", h - 3)
                    for v in range(2):
                        for i, src in enumerate((8 + h, h)):
                            o = (4 + h % 4) * 512 + (v * 2 + i) * 128
                            last = nc.tensor.transpose(ps[:, o:o + 128], feat[:, v, src, :], I)
                    last.then_inc(S["ft_ps"], 1)

                def half(h, per_head):
                    for i in range(4):
                        last = per_head(4 * h + i, i)
                    return last

                def mm(o, lhsT, rhs, n=128):
                    return nc.tensor.matmul(ps[:, o:o + n], lhsT, rhs, start=True, stop=True)

                for h in range(2):
                    w("ft_done", 4 * h + 4)
                    if h:
                        w("vb_done", 1)

                    def gram(hd, i):
                        o = BANKS[h][0] * 512 + i * 256
                        for v in range(2):
                            last = nc.tensor.matmul(ps[:, o:o + 256], featT[:, hd, v, 0:128], featT[:, hd, v, :],
                                                    start=(v == 0), stop=(v == 1))
                        return last
                    half(h, gram).then_inc(S["gram_ps"], 1)
                for h in range(2):
                    a, b, c, d = (x * 512 for x in BANKS[h])
                    w("nt_done", h + 1)
                    w("ft_done", 8)
                    half(h, lambda hd, i: nc.tensor.transpose(ps[:, c + i * 128:c + i * 128 + 128], nt[:, hd, :], I)).then_inc(S["n_ps"], 1)
                for h in range(2):
                    a, b, c, d = (x * 512 for x in BANKS[h])
                    w("n_done", h + 1)
                    w("cs_done", h + 1)
                    half(h, lambda hd, i: mm(a + i * 128, nn[:, hd, :], nt[:, hd, :]))
                    half(h, lambda hd, i: mm(b + i * 128, nt[:, hd, :], nn[:, hd, :])).then_inc(S["n2_ps"], 1)
                for h in range(2):
                    a, b, c, d = (x * 512 for x in BANKS[h])
                    w("n2_done", h + 1)
                    w("w_done", h + 1)
                    half(h, lambda hd, i: mm(c + i * 128, n2[:, hd, :], ww[:, hd, :]))
                    half(h, lambda hd, i: mm(d + i * 128, n2t[:, hd, :], n2[:, hd, :])).then_inc(S["a_ps"], 1)
                for h in range(2):
                    a, b, c, d = (x * 512 for x in BANKS[h])
                    w("a_done", h + 1)
                    w("n4_done", h + 1)
                    half(h, lambda hd, i: mm(a + i * 128, n2t[:, hd, :], ww[:, hd, :])).then_inc(S["x_ps"], 1)
                for h in range(2):
                    a, b, c, d = (x * 512 for x in BANKS[h])
                    w("x8_done", h + 1)
                    w("rv_done", 1)
                    half(h, lambda hd, i: mm(b + i * 64, nn[:, hd, :], rhs_v[:, hd, :], 64)).then_inc(S["e_ps"], 1)
                for r in range(3):
                    for h in range(2):
                        a, b, c, d = (x * 512 for x in BANKS[h])
                        w("d_done", 2 * r + h + 1)
                        half(h, lambda hd, i: mm(c + i * 64, ct[:, hd, :], delta[:, hd, 0:64], 64)).then_inc(S["t_ps"], 1)
                    for h in range(2):
                        a, b, c, d = (x * 512 for x in BANKS[h])
                        w("q_done", 2 * r + h + 1)
                        half(h, lambda hd, i: mm(d + i * 64, nn[:, hd, :], resid[:, hd, :], 64)).then_inc(S["e_ps"], 1)
                for h in range(2):
                    a, b, c, d = (x * 512 for x in BANKS[h])
                    w("d_done", 6 + h + 1)
                    half(h, lambda hd, i: mm(a + i * 65, smm[:, hd, :], delta[:, hd, :], 65)).then_inc(S["o_ps"], 1)
                w("o_done", 2)
                for i in range(4):
                    last = nc.tensor.transpose(ps[:, 512 + i * 128:512 + i * 128 + 128],
                                               regA[:, 8704 + i * 128:8704 + i * 128 + 128], I)
                last.then_inc(S["ot_ps"], 1)
                w("ot_done", 1)
                for i in range(4):
                    last = nc.tensor.matmul(ps[:, 3072:3200], B[1][:, i * 128:(i + 1) * 128], wo[:, i * 128:(i + 1) * 128],
                                            start=(i == 0), stop=(i == 3))
                last.then_inc(S["y_ps"], 1)

            pe.wait_ge(S["in_qkv"], 48)
            for j in range(NT):
                l1_tile(j)
            if stop == 4:
                return
            pe.wait_ge(S["h3_ready"], 1)
            for t in range(NT):
                last = nc.tensor.transpose(ps[:, t * 128:t * 128 + 128], HB[:, t, :], I)
            post(last, "h3T_ps")
            pe.wait_ge(S["h3T_ready"], 1)
            for t in range(NT):
                last = nc.tensor.matmul(ps[:, 1536 + t * E1:1536 + (t + 1) * E1], B[0][:, t * 128:(t + 1) * 128], gate[:],
                                        start=True, stop=True)
            post(last, "gate_ps")
            pe.wait_ge(S["in_ffn"], 80)
            n = 0
            for c in range(4):
                for g in range(3):
                    if n >= 2:
                        pe.wait_ge(S["s1_used"], n - 1)
                    o = (6 + n % 2) * 512
                    post(nc.tensor.matmul(ps[:, o:o + 384], sw1[:, c * 128:(c + 1) * 128], B[0][:, g * 384:(g + 1) * 384],
                                          start=True, stop=True), "s1_ps")
                    n += 1
            pe.wait_ge(S["s1_used"], 12)
            route(E1, 1, 1)
            sort(HB, 1)
            pe.wait_ge(S["sorted_ready"], 2)

            def up(k):
                if k % 4 == 0:
                    starts[:] = window_starts(pe, k, 4)
                if k >= 2:
                    pe.wait_ge(S["g_done"], k - 1)
                if k >= E1:
                    pe.wait_ge(S["ov1_ready"], k - E1 + 1)
                for v, w in enumerate((w1, w3)):
                    for c in range(4):
                        o = (k % 2) * 1024 + v * 512 + c * 128
                        wt = w[:, k * INNER + c * 128:k * INNER + (c + 1) * 128] if k < E1 else ov1[:, k % 2, v, c * 128:(c + 1) * 128]
                        last = nc.tensor.matmul(ps[:, o:o + 128], wt, B[4][:, bass.ds(starts[k % 4], 128)], start=True, stop=True)
                post(last, "up_ps")

            def down(k):
                pe.wait_ge(S["g_done"], k + 1)
                if k >= 2:
                    pe.wait_ge(S["y1_copied"], k - 1)
                for c in range(4):
                    wt = w2[:, k * INNER + c * 128:k * INNER + (c + 1) * 128] if k < E1 else ov1[:, k % 2, 2, c * 128:(c + 1) * 128]
                    last = nc.tensor.matmul(ps[:, 2048 + (k % 2) * 512:2176 + (k % 2) * 512], wt, gg[:, k % 2, c * 128:(c + 1) * 128],
                                            start=(c == 0), stop=(c == 3))
                post(last, "y1_ps")

            starts = []
            up(0)
            for k in range(1, E1 + NOV):
                up(k)
                down(k - 1)
            down(E1 + NOV - 1)
            pe.wait_ge(S["y1_copied"], E1 + NOV)
            columns_to_rows(1)
            for t in range(NT):
                for c in range(4):
                    last = nc.tensor.matmul(ps[:, t * 128:(t + 1) * 128], gs[:, c * N + t * 128:c * N + (t + 1) * 128],
                                            sw2[:, c * 128:(c + 1) * 128], start=(c == 0), stop=(c == 3))
            post(last, "sh_ps")
            pe.wait_ge(S["accs_copied"], 2)
            unsort(HA, 1)

        @block.scalar
        def _(act):
            act.wait_ge(S["in_const"], 64)
            for c in range(3):
                act.wait_ge(S["tok_ps"], c + 1)
                post(nc.scalar.activation(B[1][:, c * CH:(c + 1) * CH], ps[:, 2 * c * 512:2 * c * 512 + CH], ACT.Identity,
                                          bias=Cc["tok_bias"]), "tok_own")

            def consume(n):
                act.wait_ge(S["job_ps"], n + 1)
                return job_bank(n)

            def columns(what, dst, func, **kw):
                for g in range(3):
                    o = consume(J[what] + g)
                    post(nc.scalar.activation(dst[:, g * CH:(g + 1) * CH], ps[:, o:o + CH], func, **kw), "job_used")

            for g, (a, b) in enumerate(TILES4):
                o = consume(J["tokT"] + g)
                v = ps[0:PI, o:o + (b - a) * 128].rearrange("p (t q r e) -> p r t q e", q=4, r=2, e=16)
                nc.scalar.activation(HA[0:PI, a:b, 0:64].rearrange("p t (q e) -> p t q e", e=16), v[:, 1], ACT.Copy)
                post(nc.scalar.activation(HA[0:PI, a:b, 64:128].rearrange("p t (q e) -> p t q e", e=16), v[:, 0], ACT.Copy), "job_used")
            if stop == 1:
                return
            for g, (a, b) in enumerate(TILES4):
                o = consume(J["h0T"] + g)
                post(nc.scalar.activation(B[0][:, a * PI:b * PI], ps[:, o:o + (b - a) * PI], ACT.Copy), "job_used")
            columns("w1k", B[1], ACT.Gelu, bias=Cc["ke_b1"])
            columns("w1q", B[2], ACT.Gelu, bias=Cc["qe_b1"])
            columns("amp", B[5], ACT.Identity, bias=Cc["amp_b"])
            columns("w2k", B[3], ACT.Tanh, bias=Cc["ke_b2"])
            columns("w2q", B[4], ACT.Tanh, bias=Cc["qe_b2"])
            for g, (a, b) in enumerate(TILES4):
                o = consume(J["v"] + g)
                post(nc.scalar.activation(HB[0:PI, a:b, :], ps[0:PI, o:o + (b - a) * 128].rearrange("p (t d) -> p t d", d=128),
                                          ACT.Copy), "job_used")
            act.wait_ge(S["job_used"], J["v"] + 3)
            for i in range(2):
                done(act, nc.scalar.activation(B[3 + i][0:64, 0:NI], B[3 + i][0:64, 0:NI], ACT.Abs), "act_step")
                act.wait_ge(S["phase_held"], i + 1)
                done(act, nc.scalar.activation(B[3 + i][:, 0:NI], B[3 + i][:, 0:NI], ACT.Sin, bias=C["sin_bias"], scale=C["sin_scale"]), "act_step")
            done(act, nc.scalar.activation(B[1][:], B[5][:, 0:NI], ACT.Abs), "act_step")
            done(act, nc.scalar.activation(B[1][:], B[1][:], ACT.Exp, scale=-1.0), "act_step")
            done(act, nc.scalar.activation(B[1][:], B[1][:], ACT.Ln, bias=C["one"]), "act_step")
            assert count["act_step"] == 7
            for g, (a, b) in enumerate(TILES4):
                o = consume(J["rnT"] + g)
                if g == 0:
                    act.wait_ge(S["job_used"], J["rnT"])
                    act.wait_ge(S["kq_ready"], 2)
                post(nc.scalar.activation(B[1][:, a * PI:b * PI], ps[:, o:o + (b - a) * PI], ACT.Identity,
                                          scale=Cc["ln_g"], bias=Cc["ln_b"]), "job_used")
            view = B[0][:, 0:N].rearrange("p (q b) -> p b q", b=NIMG)
            for g, (a, b) in enumerate(TILES4):
                o = consume(J["h1T"] + g)
                if g == 0:
                    act.wait_ge(S["job_used"], J["h1T"])
                n = min(3 * b, NIMG) - 3 * a
                post(nc.scalar.activation(view[:, 3 * a:3 * a + n, :],
                                          ps[:, o:o + n * NPATCH].rearrange("p (b q) -> p b q", q=NPATCH), ACT.Copy), "job_used")
            for g, (a, b) in enumerate(TILES9):
                o = consume(J["h1B"] + g)
                last = nc.scalar.activation(HB[:, a:b, :], ps[:, o:o + (b - a) * 128].rearrange("p (t d) -> p t d", d=128), ACT.Copy)
                post(last, "h1b_ready")
            act.wait_ge(S["h1b_ready"], 3)
            act.wait_ge(S["dve_h1b"], 1)
            if stop == 2:
                return
            for g, (a, b) in enumerate(TILES9):
                o = consume(J["z1T"] + g)
                post(nc.scalar.activation(sgT[:, a * 128:b * 128], ps[:, o:o + (b - a) * 128], ACT.Sign,
                                          scale=Cc["gamma"], bias=Cc["beta"]), "job_used")

            def posrow(r):
                act.wait_ge(S["rows_ps"], 2 * r + 2)
                post(nc.scalar.activation(B[3][:, 0:N], ps[:, 1536:1536 + N], ACT.Copy), "posrow_ready")

            def copy_windows(p):
                for g in range(WG):
                    at = window_starts(act, g * GRP, GRP)
                    act.wait_ge(S["win_ps"], p * WG + g + 1)
                    for i in range(GRP):
                        o = (g % 4) * 512 + i * 128
                        ins = nc.scalar.activation(B[5][:, bass.ds(at[i], 128)], ps[:, o:o + 128], ACT.Copy)
                        done(act, ins, "win_copied")

            def rows_out(r):
                act.wait_ge(S["yT_ps"], r + 1)
                post(nc.scalar.activation(HA[:, 0:NT, :], ps[:, 1536:1536 + N].rearrange("p (t d) -> p t d", d=128), ACT.Copy),
                     "accs_copied")

            posrow(0)
            act.wait_ge(S["perm_used"], 9)
            act.wait_ge(S["pairs_ready"], 1)
            post(nc.scalar.activation(B[4][:, 0:N].rearrange("p (g n) -> p g n", g=3),
                                      ps[:, 1536:3072].rearrange("p (g n) -> p g n", g=3)[:, :, 0:384], ACT.Identity,
                                      scale=Cc["gamma"], bias=Cc["beta"]), "sorted_ready")
            copy_windows(0)
            done(act, nc.scalar.activation(B[5][:, 0:N], B[5][:, 0:N], ACT.Sigmoid), "hn_ready")
            act.wait_ge(S["hs_ready"], 1)
            copy_windows(1)
            rows_out(0)
            if stop == 3:
                return

            def l1_tile(j):
                def w(name, c):
                    act.wait_ge(S[name], j * PER[name] + c)

                w("xT_ps", 1)
                nc.scalar.activation(xm[:, 1, :], ps[:, 1664:1792], ACT.Copy).then_inc(S["xT_done"], 1)
                w("qkv_ps", 1)
                w("prod_done", 0)
                qk = ps[:, 0:1024].rearrange("p (h e) -> p h e", h=16)
                nc.scalar.activation(relus[:, :, 2:66], qk, ACT.Relu)
                nc.scalar.activation(relus[:, :, 0:2], qk[:, :, 62:64], ACT.Relu, scale=-1.0)
                nc.scalar.activation(relus[:, :, 66:130], qk, ACT.Relu, scale=-1.0).then_inc(S["relu_done"], 1)
                w("rv_done", 0)
                nc.scalar.activation(vals, ps[:, 1024:1536].rearrange("p (h e) -> p h e", h=NH), ACT.Copy)
                nc.scalar.activation(hsc[:, 0, :], bank(3, NH), ACT.Sigmoid).then_inc(S["vb_done"], 1)
                for h in range(NH):
                    w("ft_ps", h + 1)
                    o = (4 + h % 4) * 512
                    nc.scalar.activation(featT[:, h, :, :], ps[:, o:o + 512].rearrange("p (v f) -> p v f", v=2), ACT.Copy).then_inc(S["ft_done"], 1)

                def evac(dst, o, h):
                    return nc.scalar.activation(dst[:, 4 * h:4 * h + 4, :], ps[:, o:o + 512].rearrange("p (h f) -> p h f", h=4), ACT.Copy)

                for h in range(2):
                    w("n_ps", h + 1)
                    evac(nn, BANKS[h][2] * 512, h).then_inc(S["n_done"], 1)
                for h in range(2):
                    w("n2_ps", h + 1)
                    evac(n2t, BANKS[h][0] * 512, h)
                    evac(n2, BANKS[h][1] * 512, h).then_inc(S["n2_done"], 1)
                for h in range(2):
                    w("a_ps", h + 1)
                    evac(n2t, BANKS[h][3] * 512, h).then_inc(S["n4_done"], 1)
                w("ot_ps", 1)
                nc.scalar.activation(B[1][:, 0:512], ps[:, 512:1024], ACT.Copy).then_inc(S["ot_done"], 1)

            for j in range(NT):
                l1_tile(j)
            if stop == 4:
                return
            act.wait_ge(S["h3T_ps"], 1)
            post(nc.scalar.activation(B[0][:, 0:N], ps[:, 0:N], ACT.Copy), "h3T_ready")
            n = 0
            for c in range(4):
                for g in range(3):
                    act.wait_ge(S["s1_ps"], n + 1)
                    o = (6 + n % 2) * 512
                    post(nc.scalar.activation(gs[:, c * N + g * 384:c * N + (g + 1) * 384], ps[:, o:o + 384], ACT.Gelu), "s1_used")
                    n += 1
            act.wait_ge(S["top_ready"], 1)
            post(nc.scalar.activation(wtop[:], wtop[:], ACT.Exp), "wtop_exp")
            posrow(1)
            act.wait_ge(S["perm_used"], 27)
            post(nc.scalar.activation(B[4][:, 0:N].rearrange("p (g n) -> p g n", g=3),
                                      ps[:, 1536:3072].rearrange("p (g n) -> p g n", g=3)[:, :, 0:384], ACT.Copy), "sorted_ready")
            starts = []

            def silu(k):
                act.wait_ge(S["up_ps"], k + 1)
                if k >= 2:
                    act.wait_ge(S["g_done"], k - 1)
                post(nc.scalar.activation(sg[:, k % 2, :], ps[:, (k % 2) * 1024:(k % 2) * 1024 + 512], ACT.Silu), "silu_done")

            def result(k):
                if k % 4 == 0:
                    starts[:] = window_starts(act, k, 4)
                act.wait_ge(S["y1_ps"], k + 1)
                if k:
                    act.wait_ge(S["y1_copied"], k)
                post(nc.scalar.activation(B[5][:, bass.ds(starts[k % 4], 128)], ps[:, 2048 + (k % 2) * 512:2176 + (k % 2) * 512],
                                          ACT.Copy), "y1_copied")

            silu(0)
            for k in range(1, E1 + NOV):
                silu(k)
                result(k - 1)
            result(E1 + NOV - 1)
            rows_out(1)

        @block.gpsimd
        def _(pool):
            done(pool, nc.gpsimd.memset(mhalf[:], -0.5), "pool_step")
            nc.gpsimd.memset(zb[:], 0.0).then_inc(S["consts_made"], 1)
            nc.gpsimd.memset(oneb[:], 1.0).then_inc(S["consts_made"], 1)

            def inv_sqrt(n, p, t):
                pool.wait_ge(S["var_ready"], n)
                post(nc.gpsimd.tensor_tensor(rstd[0:p, 0:t], rstd[0:p, 0:t], mhalf[0:p, 0:t], ALU.pow), "rstd_ready")

            nc.gpsimd.memset(B[4][:, NI:], 0.0).then_inc(S["pads_zero"], 1)
            inv_sqrt(1, PI, TI)
            if stop == 1:
                return
            pool.wait_ge(S["in_tab"], 32)
            done(pool, nc.gpsimd.tensor_copy(tab_hi, tab), "pool_step")
            done(pool, nc.gpsimd.tensor_tensor(tab, tab, tab_hi, ALU.subtract), "pool_step")
            nc.gpsimd.tensor_copy(tab_hi[E0:128, :], tab[E0:128, :])
            done(pool, nc.gpsimd.tensor_copy(tab_lo, tab[0:E0, :]), "pool_step")
            done(pool, nc.gpsimd.tensor_tensor(tab_lo, tab[0:E0, :], tab_lo, ALU.subtract), "tab_split")
            inv_sqrt(2, PI, TI)
            inv_sqrt(3, PI, TI)
            if stop == 2:
                return
            inv_sqrt(4, 128, NT)
            pool.wait_ge(S["in_wd"], 16)
            pool.wait_ge(S["in_wu"], 16)
            pool.wait_ge(S["pairs_ready"], 1)
            at = late_weights(pool, 0, NOV, (E0 - 1) * 128)
            for w, dst in ((wd, ov_wd), (wu, ov_wu)):
                for i in range(NOV):
                    last = nc.gpsimd.tensor_copy(dst[:, i * 128:(i + 1) * 128], w[:, bass.ds(at[i], 128)])
                post(last, "ov0_ready")
            inv_sqrt(5, 128, NT)
            if stop == 3:
                return

            def l1_tile(j):
                for h in range(2):
                    pool.wait_ge(S["nt_done"], j * PER["nt_done"] + h + 1)
                    nc.gpsimd.tensor_tensor(ww[:, 4 * h:4 * h + 4, :], C["ident"].unsqueeze(1).to_broadcast([128, 4, 128]),
                                            nt[:, 4 * h:4 * h + 4, :], ALU.subtract).then_inc(S["w_done"], 1)

            for j in range(NT):
                l1_tile(j)
            inv_sqrt(6, 128, NT)
            inv_sqrt(7, 128, NT)
            if stop > 4:
                pool.wait_ge(S["pairs_ready"], 2)
                at = late_weights(pool, 0, NOV, (E1 - 1) * INNER)
                for k in range(NOV):
                    if k >= 2:
                        pool.wait_ge(S["y1_ps"], E1 + k - 1)
                    for v, w in enumerate((w1, w3, w2)):
                        last = nc.gpsimd.tensor_copy(ov1[:, k % 2, v, :], w[:, bass.ds(at[k], INNER)])
                    post(last, "ov1_ready")
                inv_sqrt(8, 128, NT)

        @block.vector
        def _(dve):
            def step(ins):
                done(dve, ins, "dve_step")

            def norm(src, dst, p, t, n, stats_done=False):
                if not stats_done:
                    for i in range(t):
                        last = nc.vector.bn_stats(stats[0:p, i, :], src[0:p, i, :])
                    step(last)
                for i in range(t):
                    last = nc.vector.bn_aggr(mv[0:p, i, :], stats[0:p, i, :])
                step(last)
                post(nc.vector.tensor_scalar(rstd[0:p, 0:t], mv[0:p, 0:t, 1], EPS, None, ALU.add), "var_ready")
                dve.wait_ge(S["rstd_ready"], n)
                for i in range(t):
                    last = nc.vector.tensor_scalar(dst[0:p, i, :], src[0:p, i, :], mv[0:p, i, 0:1], rstd[0:p, i:i + 1],
                                                   ALU.subtract, ALU.mult)
                return last

            def over_tiles(row, p, t):
                return row[0:p, :].unsqueeze(1).to_broadcast([p, t, 128])

            def affine(buf, p, t, g, b, name):
                step(nc.vector.tensor_tensor(buf[0:p, 0:t, :], buf[0:p, 0:t, :], over_tiles(g, p, t), ALU.mult))
                done(dve, nc.vector.tensor_tensor(buf[0:p, 0:t, :], buf[0:p, 0:t, :], over_tiles(b, p, t), ALU.add), name)

            dve.wait_ge(S["in_const"], 64)
            nc.vector.tensor_copy(trib[:], C["triS"]).then_inc(S["consts_made"], 1)
            for c in range(3):
                dve.wait_ge(S["tok_own"], c + 1)
                own = B[1][:, c * CH:(c + 1) * CH]
                far = ps[:, (2 * c + 1) * 512:(2 * c + 1) * 512 + CH]
                for q in range(4):
                    p = slice(32 * q, 32 * q + 16)
                    if q < 2:
                        a, b = own[p].rearrange("p (m j) -> p m j", j=6), far[p].rearrange("p (m j) -> p m j", j=6)
                    else:
                        a, b = own[p].rearrange("p (b i) -> p b i", i=36), far[p].rearrange("p (b i) -> p b i", i=36)
                    s1 = 1 if q < 2 else 6
                    if q % 2 == 0:
                        a, b = a[:, :, :-s1], b[:, :, s1:]
                    else:
                        a, b = a[:, :, s1:], b[:, :, :-s1]
                    last = nc.vector.tensor_tensor(a, b, a, ALU.add)
                post(last, "tok_used")
            dve.wait_ge(S["job_used"], J["tokT"] + 3)
            step(norm(HA, HA, PI, TI, 1))
            affine(HA, PI, TI, R["tok_g"], R["tok_b"], "h0_ready")
            if stop == 1:
                return

            def phase(i):
                dve.wait_ge(S["job_used"], J["w2k"] + 3 * i + 3)
                b = B[3 + i]
                done(dve, nc.vector.tensor_scalar(b[64:128, 0:NI], b[64:128, 0:NI], BELOW1, -BELOW1, ALU.min, ALU.max), "phase_held")

            phase(0)
            phase(1)
            dve.wait_ge(S["act_step"], 7)
            step(nc.vector.scalar_tensor_tensor(B[1][:], B[5][:, 0:NI], 0.0, B[1][:], ALU.max, ALU.add))
            for i in range(2):
                done(dve, nc.vector.scalar_tensor_tensor(B[3 + i][:, 0:NI], B[1][:], 0.1, B[3 + i][:, 0:NI], ALU.add, ALU.mult), "kq_ready")
            dve.wait_ge(S["job_used"], J["v"] + 3)
            done(dve, nc.vector.tensor_tensor(HB[0:PI, :, :], HB[0:PI, :, :], over_tiles(R["v_b"], PI, TI), ALU.add), "z0_ready")
            for g, (a, b) in enumerate(TILES4):
                n = J["score"] + g
                dve.wait_ge(S["job_ps"], n + 1)
                o = job_bank(n)
                done(dve, nc.vector.tensor_tensor(B[5][0:PI, a * PI:b * PI].rearrange("p (t l) -> p t l", l=PI),
                                                  ps[0:PI, o:o + (b - a) * PI].rearrange("p (t l) -> p t l", l=PI),
                                                  C["maskimg"][0:PI, :].unsqueeze(1).to_broadcast([PI, b - a, PI]), ALU.mult), "score_ready")
                dve.sem_inc(S["job_used"], 1)
            for g, (a, b) in enumerate(TILES4):
                n = J["retr"] + g
                dve.wait_ge(S["job_ps"], n + 1)
                if g == 0:
                    dve.wait_ge(S["job_ps"], J["retr"] + 3)
                o = job_bank(n)
                done(dve, nc.vector.tensor_scalar(HB[0:PI, a:b, :], ps[0:PI, o:o + (b - a) * 128].rearrange("p (t d) -> p t d", d=128),
                                                  C["invnorm"][0:PI, :], None, ALU.mult), "dve_step")
                dve.sem_inc(S["job_used"], 1)
            done(dve, norm(HB, HB, PI, TI, 2), "retr_ready")
            for g, (a, b) in enumerate(TILES4):
                n = J["att"] + g
                dve.wait_ge(S["job_ps"], n + 1)
                o = job_bank(n)
                step(nc.vector.scalar_tensor_tensor(HA[0:PI, a:b, :], HA[0:PI, a:b, :], 2.0,
                                                    ps[0:PI, o:o + (b - a) * 128].rearrange("p (t d) -> p t d", d=128),
                                                    ALU.mult, ALU.add))
                dve.sem_inc(S["job_used"], 1)
            step(nc.vector.tensor_tensor(HA[0:PI, :, :], HA[0:PI, :, :], over_tiles(R["out_b"], PI, TI), ALU.add))
            done(dve, norm(HA, HA, PI, TI, 3), "h1_ready")

            dve.wait_ge(S["h1b_ready"], 3)
            dve.sem_inc(S["job_used"], 3)
            dve.sem_inc(S["dve_h1b"], 1)
            if stop == 2:
                return
            dve.wait_ge(S["job_used"], J["h1T"] + 3)
            done(dve, norm(HB, HA, 128, NT, 4), "z1_ready")
            dve.wait_ge(S["in_wd"], 16)
            step(nc.vector.tensor_reduce(tsum[:], wd.rearrange("p (t h) -> p t h", h=128), X, ALU.add))

            def sign(dst, src, tmp, times):
                step(nc.vector.tensor_scalar(tmp, src, 0.0, times, ALU.is_gt, ALU.mult))
                step(nc.vector.tensor_scalar(src, src, 0.0, times, ALU.is_lt, ALU.mult))
                step(nc.vector.tensor_tensor(dst, tmp, src, ALU.subtract))

            sign(tsig8[:], tsum[:], srow[:], 8.0)
            step(nc.vector.tensor_reduce(csum[:], tsig8[:].rearrange("p (c j) -> p c j", j=8), X, ALU.add))
            sign(small[:, 8:16], csum[:], small[:, 0:8], 8.0 * 4096.0)
            done(dve, nc.vector.tensor_copy(csigb[:].rearrange("p (c j) -> p c j", j=8), small[:, 8:16].unsqueeze(2).to_broadcast([128, 8, 8])), "sig_ready")

            dve.wait_ge(S["key_ps"], 1)
            step(nc.vector.tensor_tensor(key[:], ps[:, 0:NT * E0].rearrange("p (t e) -> p t e", e=E0),
                                         C["keybias"].unsqueeze(1).to_broadcast([128, NT, E0]), ALU.add))
            step(nc.vector.tensor_reduce(kmax[:], key[:], X, ALU.max))
            step(nc.vector.tensor_tensor(oh[:, :, 0, :], key[:], kmax[:].unsqueeze(2).to_broadcast([128, NT, E0]), ALU.is_equal))
            done(dve, nc.vector.tensor_copy(oh[:, :, 1, :], oh[:, :, 0, :]), "oh_ready")
            step(nc.vector.tensor_tensor(key[:], oh[:, :, 0, :], scale_row[:].unsqueeze(1).to_broadcast([128, NT, E0]), ALU.mult))
            step(nc.vector.tensor_reduce(scl[:], key[:], X, ALU.add))

            def route(E, r, dup, weight):
                M = dup * E
                dve.wait_ge(S["rank_ps"], r + 1)
                done(dve, nc.vector.tensor_copy(small[0:M, 0:1], ps[0:M, 1024:1025]), "cnt_ready")
                dve.wait_ge(S["start_ps"], r + 1)
                step(nc.vector.tensor_copy(small[0:M, 1:2], ps[0:M, 1536:1537]))
                step(nc.vector.tensor_tensor(small[0:M, 2:3], small[0:M, 1:2], small[0:M, 0:1], ALU.add))
                step(nc.vector.tensor_copy(srow[:, 0:E], ps[:, 2048:2048 + E]))
                step(nc.vector.tensor_tensor(rk[:, :, 0:E], ps[:, 0:NT * E].rearrange("p (t e) -> p t e", e=E),
                                             srow[:, 0:E].unsqueeze(1).to_broadcast([128, NT, E]), ALU.add))
                step(nc.vector.tensor_tensor(rk[:, :, 0:E], rk[:, :, 0:E], oh[:, :, 0, 0:E], ALU.mult))
                step(nc.vector.tensor_reduce(pos[:], rk[:, :, 0:E], X, ALU.add))
                step(nc.vector.tensor_scalar(k64[0:E, 0, 0:8], C["tile_end"][0:E, :], small[0:E, 0:1], None, ALU.is_lt, ALU.add,
                                             accum_out=small[0:E, 3:4]))
                step(nc.vector.tensor_scalar(small[0:E, 4:5], small[0:E, 3:4], 128.0, None, ALU.mult))
                step(nc.vector.tensor_scalar(small[0:E, 5:6], small[0:E, 2:3], -128.0, None, ALU.add))
                step(nc.vector.tensor_scalar(ohs[0:M, :], C["slot"][0:M, :], small[0:M, 1:2], None, ALU.is_ge))
                done(dve, nc.vector.scalar_tensor_tensor(ohs[0:M, :], C["slot"][0:M, :], small[0:M, 2:3], ohs[0:M, :],
                                                         ALU.is_lt, ALU.mult), "route_cols")
                dve.wait_ge(S["rows_ps"], 2 * r + 1)
                kc = C["kcol"][0:NOV, :]
                o = 2560
                in_k = k64[0:NOV, 0, 0:E]
                step(nc.vector.tensor_scalar(in_k, ps[0:NOV, o:o + E], kc, None, ALU.is_le))
                step(nc.vector.scalar_tensor_tensor(in_k, ps[0:NOV, o + 64:o + 64 + E], kc, in_k, ALU.is_le, ALU.subtract))
                step(nc.vector.scalar_tensor_tensor(k64[0:NOV, 1, 0:E], ps[0:NOV, o + 128:o + 128 + E], C["k128"][0:NOV, :], in_k,
                                                    ALU.subtract, ALU.mult, accum_out=small[0:NOV, 11:12]))
                step(nc.vector.scalar_tensor_tensor(k64[0:NOV, 2, 0:E], C["expert1"][0:NOV, 0:E], 1.0, in_k, ALU.mult, ALU.mult,
                                                    accum_out=small[0:NOV, 12:13]))
                step(nc.vector.tensor_scalar(small[0:NOV, 8:9], small[0:NOV, 12:13], 0.0, float(N), ALU.is_equal, ALU.mult))
                step(nc.vector.tensor_tensor(small[0:NOV, 10:11], small[0:NOV, 11:12], small[0:NOV, 8:9], ALU.add))
                step(nc.vector.tensor_scalar(small[0:NOV, 8:9], small[0:NOV, 12:13], 1.0, 0.0, ALU.subtract, ALU.max))
                done(dve, nc.vector.tensor_scalar(small[0:NOV, 9:10], small[0:NOV, 8:9], float(weight), None, ALU.mult), "pair_cols")
                dve.wait_ge(S["pairs_ps"], r + 1)
                nc.vector.tensor_copy(offs[0:1, 0:E], srow[0:1, 0:E])
                nc.vector.tensor_copy(offs[0:1, E:E + NOV], ps[0:1, 3200:3200 + NOV])
                done(dve, nc.vector.tensor_copy(ovx[0:1, :], ps[0:1, 3072:3072 + NOV]), "pairs_ready")

            def perm_to(r):
                for j in range(NT):
                    n = r * 18 + j
                    if n >= 2:
                        dve.wait_ge(S["perm_used"], n - 1)
                    post(nc.vector.tensor_scalar(B[1 + j % 2][:, 0:N], C["slot"], pos[:, j:j + 1], None, ALU.is_equal), "perm_made")

            def perm_from(r):
                for s_ in range(NT):
                    n = r * 18 + 9 + s_
                    dve.wait_ge(S["perm_used"], n - 1)
                    post(nc.vector.tensor_scalar(B[1 + n % 2][:, 0:N], B[3][:, 0:N], C["slotcol"][:, s_:s_ + 1], None,
                                                 ALU.is_equal), "perm_made")

            route(E0, 0, 2, 128)
            perm_to(0)
            dve.wait_ge(S["hn_ready"], 1)
            u, lp, cell, fl = B[5][:, 0:N], B[4][:, 0:N], B[0][:, 0:N].bitcast(I32), B[1][:, 0:N]
            step(nc.vector.tensor_scalar(u, u, float(GRID), None, ALU.mult))
            step(nc.vector.tensor_copy(cell, u))
            step(nc.vector.tensor_copy(lp, cell))
            step(nc.vector.tensor_tensor(fl, lp, u, ALU.is_gt))
            step(nc.vector.tensor_tensor(fl, lp, fl, ALU.subtract))
            step(nc.vector.tensor_scalar(fl, fl, float(GRID - 1), None, ALU.min))
            step(nc.vector.tensor_tensor(lp, u, fl, ALU.subtract))
            picked = regA[:, 0:2 * N].rearrange("p (v n) -> p v n", v=2)
            n = 0
            for g in range(GRID):
                m = masks[:, g % 2, :]
                step(nc.vector.tensor_scalar(m, u, float(g), None, ALU.is_ge))
                for c in range(3):
                    dve.wait_ge(S["tab_ps"], n + 1)
                    o = 1536 + (n % 2) * 1024
                    src = ps[:, o:o + 1024].rearrange("p (v n) -> p v n", v=2)[:, :, 0:384]
                    dst = picked[:, :, c * 384:(c + 1) * 384]
                    if g == 0:
                        ins = nc.vector.tensor_copy(dst, src)
                    else:
                        ins = nc.vector.copy_predicated(dst, m[:, c * 384:(c + 1) * 384].unsqueeze(1).to_broadcast([128, 2, 384]), src)
                    done(dve, ins, "tab_used")
                    n += 1
            step(nc.vector.tensor_tensor(lp, lp, picked[:, 1, :], ALU.mult))
            done(dve, nc.vector.tensor_tensor(lp, lp, picked[:, 0, :], ALU.add), "hs_ready")
            perm_from(0)
            dve.wait_ge(S["perm_used"], 18)
            for t in range(NT):
                last = nc.vector.tensor_scalar(HA[:, t, :], ps[:, 2560 + t * 128:2560 + (t + 1) * 128], scl[:, t:t + 1], None, ALU.mult)
            step(last)
            step(nc.vector.scalar_tensor_tensor(HA[:, 0:NT, :], HB[:, 0:NT, :], 2.0, HA[:, 0:NT, :], ALU.mult, ALU.add))
            done(dve, norm(HA, HA, 128, NT, 5), "h2_ready")
            if stop == 3:
                return

            L1STEPS = 9

            def l1_tile(j):
                def w(name, c):
                    dve.wait_ge(S[name], j * PER[name] + c)

                steps = [0]

                def own(ins):
                    steps[0] += 1
                    ins.then_inc(S["l1_step"], 1)
                    dve.wait_ge(S["l1_step"], j * L1STEPS + steps[0])

                def per_head(v, h, n):
                    return v[:, 4 * h:4 * h + 4].unsqueeze(2).to_broadcast([128, 4, n])

                nc.vector.tensor_copy(xm[:, 0, :], HA[:, j, :]).then_inc(S["xst_ready"], 1)
                w("relu_done", 1)
                qk = ps[:, 0:1024].rearrange("p (h e) -> p h e", h=16)
                for v in range(2):
                    nc.vector.scalar_tensor_tensor(feat[:, v, :, 0:64], qk, 0.0, relus[:, :, 1 - v:65 - v], ALU.max, ALU.mult)
                    last = nc.vector.scalar_tensor_tensor(feat[:, v, :, 64:128], qk, 0.0, relus[:, :, 65 - v:129 - v], ALU.min, ALU.mult)
                last.then_inc(S["prod_done"], 1)
                w("prod_done", 1)
                for v in range(2):
                    last = nc.vector.tensor_reduce(sums[:] if v == 0 else srow[:, 0:16], feat[:, v], X, ALU.add, apply_absolute_value=True)
                own(last)
                own(nc.vector.tensor_tensor(sums[:], sums[:], srow[:, 0:16], ALU.add))
                sq, sk = sums[:, 0:8], sums[:, 8:16]
                w("vb_done", 1)
                own(nc.vector.reciprocal(hsc[:, 1, :], sk))
                own(nc.vector.tensor_tensor(hsc[:, 2, :], hsc[:, 1, :], hsc[:, 1, :], ALU.mult))
                nc.vector.tensor_scalar(hsc[:, 3, :], sq, 8.0 * EPS, None, ALU.mult)
                nc.vector.tensor_copy(delta[:, :, 64], hsc[:, 1, :])
                own(nc.vector.tensor_tensor(hsc[:, 2, :], hsc[:, 2, :], hsc[:, 0, :], ALU.mult))
                nc.vector.tensor_tensor(rhs_v, vals, sk.unsqueeze(2).to_broadcast([128, NH, 64]), ALU.mult).then_inc(S["rv_done"], 1)
                for h in range(2):
                    w("gram_ps", h + 1)
                    o = BANKS[h][0] * 512
                    g = ps[:, o:o + 1024].rearrange("p (h f) -> p h f", h=4)
                    for i in range(4):
                        last = nc.vector.scalar_tensor_tensor(nt[:, 4 * h + i, :], g[:, i, 0:128], hsc[:, 2, 4 * h + i:4 * h + i + 1],
                                                              C["maskN"], ALU.mult, ALU.mult)
                    last.then_inc(S["nt_done"], 1)
                    nc.vector.tensor_tensor(ct[:, 4 * h:4 * h + 4, :], g[:, :, 0:128], C["maskC"].unsqueeze(1).to_broadcast([128, 4, 128]), ALU.mult)
                    nc.vector.tensor_tensor(smm[:, 4 * h:4 * h + 4, :], g[:, :, 128:256],
                                            C["maskS"].unsqueeze(1).to_broadcast([128, 4, 128]), ALU.mult).then_inc(S["cs_done"], 1)

                def plus_w(dst, b, h):
                    return nc.vector.tensor_tensor(dst[:, 4 * h:4 * h + 4, :], ps[:, b * 512:(b + 1) * 512].rearrange("p (h f) -> p h f", h=4),
                                                   ww[:, 4 * h:4 * h + 4, :], ALU.add)

                for h in range(2):
                    w("a_ps", h + 1)
                    plus_w(ww, BANKS[h][2], h).then_inc(S["a_done"], 1)
                for h in range(2):
                    w("x_ps", h + 1)
                    if h == 0:
                        w("a_done", 2)
                    plus_w(nn, BANKS[h][0], h).then_inc(S["x8_done"], 1)

                def scaled(n, b, h):
                    w("e_ps", n + 1)
                    e = ps[:, b * 512:b * 512 + 256].rearrange("p (h e) -> p h e", h=4)
                    nc.vector.tensor_tensor(delta[:, 4 * h:4 * h + 4, 0:64], e, per_head(hsc[:, 2, :], h, 64), ALU.mult).then_inc(S["d_done"], 1)

                for h in range(2):
                    scaled(h, BANKS[h][1], h)
                for r in range(3):
                    for h in range(2):
                        w("t_ps", 2 * r + h + 1)
                        if r == 0 and h == 0:
                            w("rv_done", 1)
                        t = ps[:, BANKS[h][2] * 512:BANKS[h][2] * 512 + 256].rearrange("p (h e) -> p h e", h=4)
                        nc.vector.tensor_tensor(resid[:, 4 * h:4 * h + 4, :], rhs_v[:, 4 * h:4 * h + 4, :], t, ALU.subtract).then_inc(S["q_done"], 1)
                    for h in range(2):
                        scaled(2 + 2 * r + h, BANKS[h][3], h)
                for h in range(2):
                    w("o_ps", h + 1)
                    o = ps[:, BANKS[h][0] * 512:BANKS[h][0] * 512 + 260].rearrange("p (h e) -> p h e", h=4)
                    hs_ = slice(4 * h, 4 * h + 4)
                    own(nc.vector.scalar_tensor_tensor(hsc[:, 4, hs_], o[:, :, 64], 8.0, hsc[:, 3, hs_], ALU.mult, ALU.add))
                    own(nc.vector.reciprocal(hsc[:, 5, hs_], hsc[:, 4, hs_]))
                    nc.vector.tensor_tensor(outs[:, hs_, :], o[:, :, 0:64], per_head(hsc[:, 5, :], h, 64), ALU.mult).then_inc(S["o_done"], 1)
                w("y_ps", 1)
                nc.vector.tensor_tensor(HB[:, j, :], ps[:, 3072:3200], HA[:, j, :], ALU.add).then_inc(S["y_done"], 1)
                assert steps[0] == L1STEPS, steps

            for j in range(NT):
                l1_tile(j)
            dve.wait_ge(S["y_done"], NT)
            step(norm(HB, HB, 128, NT, 6))
            affine(HB, 128, NT, R["l1_g"], R["l1_b"], "dve_step")
            step(nc.vector.tensor_tensor(HB[:, 0:NT, :], HB[:, 0:NT, :], HA[:, 0:NT, :], ALU.add))
            done(dve, norm(HB, HB, 128, NT, 7), "h3_ready")
            if stop == 4:
                return
            dve.wait_ge(S["gate_ps"], 1)
            lg = key[:, :, 0:E1]
            step(nc.vector.tensor_copy(lg, ps[:, 1536:1536 + NT * E1].rearrange("p (t e) -> p t e", e=E1)))
            step(nc.vector.tensor_reduce(kmax[:], lg, X, ALU.max))
            done(dve, nc.vector.tensor_tensor(wtop[:], kmax[:], kmax[:], ALU.subtract), "top_ready")
            step(nc.vector.tensor_tensor(lg, lg, kmax[:].unsqueeze(2).to_broadcast([128, NT, E1]), ALU.is_equal))
            step(nc.vector.tensor_tensor(lg, lg, C["prefer"].unsqueeze(1).to_broadcast([128, NT, E1]), ALU.mult))
            step(nc.vector.tensor_reduce(kmax[:], lg, X, ALU.max))
            done(dve, nc.vector.tensor_tensor(oh[:, :, 0, 0:E1], lg, kmax[:].unsqueeze(2).to_broadcast([128, NT, E1]), ALU.is_equal), "oh_ready")
            dve.wait_ge(S["wtop_exp"], 1)
            step(nc.vector.reciprocal(scl[:], wtop[:]))
            step(nc.vector.tensor_tensor(scl[:], scl[:], wtop[:], ALU.mult))
            route(E1, 1, 1, INNER)
            perm_to(1)
            for k in range(E1 + NOV):
                dve.wait_ge(S["silu_done"], k + 1)
                if k >= 2:
                    dve.wait_ge(S["y1_ps"], k - 1)
                post(nc.vector.tensor_tensor(gg[:, k % 2, :], ps[:, (k % 2) * 1024 + 512:(k % 2) * 1024 + 1024], sg[:, k % 2, :],
                                             ALU.mult), "g_done")
            perm_from(1)
            dve.wait_ge(S["perm_used"], 36)
            for t in range(NT):
                last = nc.vector.tensor_scalar(HA[:, t, :], ps[:, 2560 + t * 128:2560 + (t + 1) * 128], scl[:, t:t + 1], None, ALU.mult)
            step(last)
            dve.wait_ge(S["sh_ps"], 1)
            step(nc.vector.tensor_tensor(HA[:, 0:NT, :], ps[:, 0:N].rearrange("p (t d) -> p t d", d=128), HA[:, 0:NT, :], ALU.add))
            step(nc.vector.tensor_tensor(HA[:, 0:NT, :], HA[:, 0:NT, :], HB[:, 0:NT, :], ALU.add))
            done(dve, norm(HA, HA, 128, NT, 8), "y_final")


def pack(a):
    import numpy as np
    f = np.float32
    o = {}
    x = a["x"].reshape(NIMG, 3, 12, 8, 12, 2, 4)
    v = np.zeros((3, 8, 4, 2, NIMG + 1, 12, 12), f)
    v[:, :, :, :, :NIMG] = x.transpose(1, 3, 6, 5, 0, 2, 4)
    o["blocks"] = v.reshape(KF, 2, NBLK)

    def part(w, hy, hx, k):
        w = w.reshape(-1, 3, 2, 8, 2, 2, 4)
        return w[:, :, hy, :, hx, k, :].transpose(1, 2, 3, 0).reshape(KF, -1)

    wm, wx, wy = a["L0_tok_W_main"], a["L0_tok_W_sx"], a["L0_tok_W_sy"]
    tokw = np.zeros((KF, 8, 2, 4, 2, 16), f)
    n = 0
    for hy in range(2):
        for hx in range(2):
            for k in range(2):
                own, far = tokw[:, n, 0], tokw[:, n, 1]
                own[:, :, 1] = part(wm, hy, hx, k).reshape(KF, 4, 16)
                own[:, 1 - hx, 0] = part(wx, hy, 1 - hx, k)
                own[:, 3 - hy, 0] = part(wy, 1 - hy, hx, k)
                far[:, hx, 0] = part(wx, hy, 1 - hx, k)
                far[:, 2 + hy, 0] = part(wy, 1 - hy, hx, k)
                n += 1
    tokw = tokw.reshape(KF, -1)
    o["tokw"] = tokw
    bm, bx, by = (a[n].reshape(-1, 16) for n in ("L0_tok_b_main", "L0_tok_b_sx", "L0_tok_b_sy"))
    bs = np.concatenate([bx, bx, by, by])
    rows = {"tok_g": a["L0_tok_ln_g"], "tok_b": a["L0_tok_ln_b"], "v_b": a["L0_attn_v_b"], "out_b": a["L0_attn_out_b"],
            "l1_g": a["L1_attn_ln_g"], "l1_b": a["L1_attn_ln_b"]}
    o["rows"] = np.concatenate([rows[n] for n in ROWS])
    two = lambda v: np.concatenate([v, v], axis=-1)
    cols = {"tok_bias": np.stack([bs, bm], axis=1).reshape(-1), "ke_b1": a["L0_attn_ke_b1"], "qe_b1": a["L0_attn_qe_b1"], "ke_b2": two(a["L0_attn_ke_b2"]),
            "qe_b2": two(a["L0_attn_qe_b2"]), "amp_b": two(a["L0_attn_amp_b"]), "ln_g": a["L0_attn_ln_g"],
            "ln_b": a["L0_attn_ln_b"], "gamma": a["L0_ffn_gamma"], "beta": a["L0_ffn_beta"]}
    o["cols"] = np.stack([cols[n] for n in COLS], axis=1)
    o["scale"] = a["L0_ffn_scale"]
    o["attw"] = np.concatenate([a["L0_attn_ke_w1"], a["L0_attn_qe_w1"], two(a["L0_attn_ke_w2"]), two(a["L0_attn_qe_w2"]),
                                two(a["L0_attn_amp_w"]), a["L0_attn_v_w"], a["L0_attn_out_w"]], axis=1)
    o["wd"] = a["L0_ffn_Wd"].transpose(2, 0, 1).reshape(128, -1)
    o["wu"] = a["L0_ffn_Wu"].transpose(2, 0, 1).reshape(128, -1)
    tab = np.stack([a["L0_ffn_spline_bases"], a["L0_ffn_spline_slopes"]], axis=0)
    o["tab"] = tab.transpose(1, 3, 0, 2).reshape(E0, -1)
    w = a["L1_attn_W_qkvb"].reshape(NH, 3 * HD + 1, 128)
    o["qkvw"] = np.concatenate([w[:, i * HD:(i + 1) * HD].reshape(NH * HD, 128) for i in range(3)] + [w[:, 3 * HD]], axis=0).T
    o["wo"] = a["L1_attn_W_o"].T.reshape(4, 128, 128).transpose(1, 0, 2).reshape(128, -1)
    o["gate"] = a["L1_ffn_gate_w"].T
    o["w1"] = a["L1_ffn_w1"].transpose(2, 0, 1).reshape(128, -1)
    o["w3"] = a["L1_ffn_w3"].transpose(2, 0, 1).reshape(128, -1)
    o["w2"] = a["L1_ffn_w2"].reshape(E1, 128, 4, 128).transpose(3, 0, 2, 1).reshape(128, -1)
    o["sw1"] = a["L1_ffn_sw1"].T
    o["sw2"] = a["L1_ffn_sw2"].reshape(128, 4, 128).transpose(2, 1, 0).reshape(128, -1)

    c = {}
    i, j = np.arange(128)[:, None], np.arange(128)[None, :]
    c["ident"] = i == j
    c["maskimg"] = ((i // NPATCH == j // NPATCH) & (i <= j) & (i < PI))[:, :PI]
    c["maskN"] = (i // 8 == j // 8) & (i < j)
    c["maskC"] = (i // 32 == j // 32) & (i // 8 < j // 8)
    c["maskS"] = (i // 32 == j // 32) & (i <= j)
    c["triS"] = i < j
    c["triI"] = i <= j
    c["slot"] = np.broadcast_to(np.arange(N), (128, N))
    c["tile_end"] = np.broadcast_to(np.arange(1, 9) * 128, (128, 8))
    c["expert1"] = np.broadcast_to(np.arange(1, E0 + 1), (128, E0))
    c["invnorm"] = 1.0 / np.sqrt((np.arange(128) % NPATCH + 1) * 64.0)[:, None]
    c["sin_scale"] = np.where(i < 64, -PI32, PI32)
    c["sin_bias"] = np.where(i < 64, PI32 / 2, 0.0)
    c["kcol"] = i
    c["k128"] = i * 128
    c["one"] = i * 0 + 1
    c["slotcol"] = np.arange(NT)[None, :] * 128 + i
    e = np.arange(E0)
    c["keybias"] = np.broadcast_to(-4096.0 * (e // 8) - e % 8, (128, E0))
    c["prefer"] = np.broadcast_to(8.0 - np.arange(E1), (128, E1))
    o["consts"] = np.concatenate([np.asarray(c[n], f) for n, _ in CONST], axis=1)
    return {k: np.ascontiguousarray(v, f) for k, v in o.items()}


def kernel(**inputs):
    import numpy as np
    from concourse import bacc
    from concourse.bass_utils import run_bass_kernel_spmd

    packed = pack({k: np.asarray(v) for k, v in inputs.items()})
    nc = bacc.Bacc("TRN2", target_bir_lowering=False, num_devices=1)
    A = {k: nc.dram_tensor(f"in_{k}", v.shape, F32, kind="ExternalInput").ap() for k, v in packed.items()}
    out = nc.dram_tensor("out", (128, NT, 128), F32, kind="ExternalOutput").ap()
    vit_kernel(nc, A, out)
    got = run_bass_kernel_spmd(nc, [{f"in_{k}": v for k, v in packed.items()}], core_ids=[0]).results[0]["out"]
    return np.ascontiguousarray(got.reshape(4, NIMG, NT, D).transpose(1, 2, 0, 3).reshape(NIMG, NPATCH, D))
```

```python
from contextlib import ExitStack

import concourse.bass as bass
from concourse import mybir
from concourse.alu_op_type import AluOpType as ALU

F32 = mybir.dt.float32
BF16 = mybir.dt.bfloat16
I32 = mybir.dt.int32
U8 = mybir.dt.uint8
ACT = mybir.ActivationFunctionType
X = mybir.AxisListType.X

D = 128
NIMG, NPATCH = 32, 36
TI = 11
PI = 3 * NPATCH
NI = TI * PI
NT = 9
N = NT * 128
KC = 6
EPS = 1e-5
PI32 = 3.1415927410125732
BELOW1 = 0.99999994
E0, E1 = 64, 8
GRID = 16
NH, HD = 8, 64
INNER = 512
NOV = NT - 1
GRP = 4
TILES4 = [(0, 4), (4, 8), (8, 11)]
TILES9 = [(0, 4), (4, 8), (8, 9)]

CONST = [("ident", 128), ("maskimg", PI), ("maskN", 128), ("maskC", 128), ("maskS", 128), ("triS", 128), ("triI", 128),
         ("slot", N), ("tile_end", 8), ("expert1", E0), ("invnorm", 1), ("sin_scale", 1), ("sin_bias", 1), ("kcol", 1), ("k128", 1),
         ("slotcol", NT), ("keybias", E0), ("prefer", E1), ("one", 1), ("from_cell", GRID)]
ROWS = ["tok_g", "tok_b", "v_b", "out_b", "l1_g", "l1_b"]
COLS = ["tok_bias", "ke_b1", "qe_b1", "ke_b2", "qe_b2", "amp_b", "ln_g", "ln_b", "gamma", "beta"]


def places():
    at, o = {}, 0
    for n, w in CONST:
        at[n] = (o, o + w)
        o += w
    return at, o


CAT, NCONST = places()


def vit_kernel(nc, A, out, stop=99, dbg=None):
    with ExitStack() as ctx:
        def sb(name, shape, dt=F32):
            return ctx.enter_context(nc.sbuf_tensor(name, shape, dt))

        cst = sb("cst", [128, NCONST])
        C = {n: cst[:, a:b] for n, (a, b) in CAT.items()}
        rows = sb("rows", [128, len(ROWS) * 128])
        R = {n: rows[:, i * 128:(i + 1) * 128] for i, n in enumerate(ROWS)}
        scale_row = sb("scale_row", [128, E0])
        cols = sb("cols", [128, len(COLS)])
        Cc = {n: cols[:, i:i + 1] for i, n in enumerate(COLS)}
        regA = sb("regA", [128, 9504])
        patches = regA[:, 0:KC * NI].rearrange("p (k n) -> p k n", k=KC)
        tab = regA[:, 0:4096]
        tab_hi = regA[:, 4096:6144].bitcast(BF16)
        tab_lo = regA[0:E0, 6144:8192].bitcast(BF16)
        regW = sb("regW", [128, 2 * E0 * 128])
        wd, wu = regW[:, 0:E0 * 128], regW[:, E0 * 128:]
        W1 = E1 * INNER
        w1, w3, w2 = regW[:, 0:W1], regW[:, W1:2 * W1], regW[:, 2 * W1:3 * W1]
        sw1, sw2 = regW[:, 3 * W1:3 * W1 + INNER], regW[:, 3 * W1 + INNER:3 * W1 + 2 * INNER]
        gate = sb("gate", [128, E1])
        tokw = sb("tokw", [128, KC * 256])
        attw = sb("attw", [128, 7 * 128])
        qkvw = sb("qkvw", [128, 3 * 512 + 8])
        wo = sb("wo", [128, 4 * 128])
        B = [sb(f"B{i}", [128, NI if i < 4 else N + 128]) for i in range(6)]
        HA = sb("HA", [128, TI, 128])
        HB = sb("HB", [128, TI, 128])
        stats = sb("stats", [128, TI, 6])
        mv = sb("mv", [128, TI, 2])
        rstd = sb("rstd", [128, TI])
        mhalf = sb("mhalf", [128, TI])
        zb = sb("zb", [128, 512], BF16)
        oneb = sb("oneb", [128, 128], BF16)
        trib = sb("trib", [128, 128], BF16)
        sgT = sb("sgT", [128, N], BF16)
        tsum = sb("tsum", [128, E0])
        csum = sb("csum", [128, 8])
        tsig8 = sb("tsig8", [128, E0], BF16)
        csigb = sb("csigb", [128, E0], BF16)
        key = sb("key", [128, NT, E0])
        kmax = sb("kmax", [128, NT])
        wtop = sb("wtop", [128, NT])
        oh = sb("oh", [128, NT, 2, E0], BF16)
        rk = sb("rk", [128, NT, E0])
        small = sb("small", [128, 16])
        srow = sb("srow", [128, E0])
        pos = sb("pos", [128, NT])
        ohs = sb("ohs", [128, N], BF16)
        k64 = sb("k64", [128, 6, E0])
        offs = sb("offs", [128, E0 + NOV], I32)
        ovx = sb("ovx", [128, NOV], I32)
        hb = sb("hb", [128, 2, 128])
        scl = sb("scl", [128, NT])
        masks = sb("masks", [128, 2, N], U8)
        upper = sb("upper", [128, N], U8)
        B5u = regA[:, 8192:8192 + N + 128]
        picked = regA[:, 0:2 * N].rearrange("p (v n) -> p v n", v=2)
        def heads(t):
            return t[:, 0:NH * 128].rearrange("p (h f) -> p h f", h=NH)

        feat = regA[:, 0:4096].rearrange("p (v h f) -> p v h f", v=2, h=16)
        featT = regA[:, 4096:8192].rearrange("p (h v f) -> p h v f", h=NH, v=2)
        vals = regA[:, 8192:8704].rearrange("p (h e) -> p h e", h=NH)
        outs = regA[:, 8704:9216].rearrange("p (h e) -> p h e", h=NH)
        relus = regW[:, 13312:13312 + 16 * 130].rearrange("p (h f) -> p h f", h=16)
        xT = regW[:, 4096:4096 + N]
        rhs_v = [regW[:, a:a + 512].rearrange("p (h e) -> p h e", h=NH) for a in (15392, 5248)]
        delta = B[0][:, 0:NH * 65].rearrange("p (h e) -> p h e", h=NH)
        first = B[0][:, 520:520 + 512].rearrange("p (h e) -> p h e", h=NH)
        grams = regW[:, 5760:6784].rearrange("p (u h f) -> p u h f", u=2, h=2)
        nt, ct, smm, nn, n2 = (heads(B[i]) for i in range(1, 6))
        ww, n2t = heads(sb("ww", [128, NH * 128])), heads(sb("n2t", [128, NH * 128]))
        nt, ct, smm, ww = ([t, heads(regW[:, a:a + 1024])] for t, a in ((nt, 8192), (ct, 9216), (smm, 10240), (ww, 11264)))
        below_T = n2
        outT = n2t.rearrange("p h f -> p (h f)")[:, 0:512]
        ov_wd, ov_wu = (t.rearrange("p h f -> p (h f)") for t in (ww[0], n2t))
        sums = sb("sums", [128, 16])
        hscs = sb("hscs", [128, 2, 6, NH])
        beta = sb("beta", [128, NT, NH])
        gs = regA[:, 0:4 * N]
        sg = regA[:, 4608:5632].rearrange("p (u i) -> p u i", u=2)
        gg = regA[:, 5632:6656].rearrange("p (u i) -> p u i", u=2)
        ov1 = regW[:, 13312:16384].rearrange("p (u w i) -> p u w i", u=2, w=3)
        sh_early = regA[:, 7808:7808 + 6 * 128]
        h3T = regA[:, 6656:6656 + N]
        yrows = B[4][:, 0:N].rearrange("p (t d) -> p t d", d=128)
        unperm = [regW[:, k * N:(k + 1) * N] for k in range(3)] + [regW[:, 5760 + k * N:5760 + (k + 1) * N] for k in range(2)]
        unperm += [B[i][:, 0:N] for i in (1, 2, 0, 5)]
        ps = ctx.enter_context(nc.psum_tensor("ps", [128, 4096], F32))

        def bank(b, n=512, p=128):
            return ps[0:p, b * 512:b * 512 + n]

        S = {}

        def sems(*names):
            for n in names:
                S[n] = ctx.enter_context(nc.semaphore(n))

        sems("in_const", "in_tok", "in_patches0", "in_patches1", "in_patches2", "in_wd", "in_wu", "in_att", "in_tab", "in_qkv", "in_ffn", "in_ffn2", "stored")
        sems("dve_step", "pool_step", "consts_made", "pads_zero", "var_ready", "rstd_ready")
        sems("tok_ps", "tok_own", "tok_used", "h0_ready", "job_ps", "job_act", "job_dve", "z_abs", "ln_ready", "phase_abs", "phase_held", "sines", "kq_ready",
             "retr_ready", "h1_ready", "z1_ready", "tab_rest", "y_final", "sig_ready", "key_ps")
        sems("oh_ready", "rank_ps", "cnt_ready", "start_ps", "route_cols", "rows_ps", "pair_cols", "late_ps", "slots_ready", "pairs_ps", "pairs_ready",
             "perm_made", "perm_used", "unperm_made", "unsort_ps", "unsort_used", "tile_var", "tile_rstd", "hb_ready", "twice_ready", "sorted_ready", "win_ps", "upper_ps", "win_copied", "upper_copied", "upper_ready", "merged", "u_ready", "cell_ready", "first_cells", "ov0_ready", "yT_ps",
             "accs_copied", "hn_ready", "posrow_ready")
        sems("tab_split", "tab_high", "tab_low", "tab_ps", "tab_used", "mask_ready", "hs_ready", "h2_ready")
        sems("qk_ps", "v_ps", "relu_done", "vb_done", "prod_done", "ft_ps", "ft_done", "gram_ps", "nt_done", "beta_ps", "beta_done", "xT_ps", "xT_done",
             "n_ps", "n_done", "w_done", "n2_ps", "n2_done", "a_ps", "a_done", "n4_done", "x_ps", "x8_done", "e_ps", "m_ps", "m_done", "masks_done", "grams_copied", "e_done",
             "d_done", "t_ps", "o_ps", "o_done", "ot_ps", "ot_done", "y_ps", "y_done", "l1_step", "rv_done", "scales_done")
        sems("h3_ready", "h3T_ready", "gate_ps", "s1_ps", "s1_used", "sh_ps", "sh_early_ps", "sh_early_done", "sh_added", "up_ps", "silu_done", "g_done",
             "y1_ps", "y1_copied", "ov_up_ready", "ov_down_ready", "h3T_ps", "top_ready", "wtop_exp")
        block = ctx.enter_context(nc.Block())
        count = {}
        HG = E0 // 2 // GRP
        LG = NOV // GRP

        def window_starts(eng, a, n):
            return nc.values_load_multi_w_load_instructions(
                offs[0:1, a:a + n], engines=[eng.engine], min_val=0, max_val=N,
                skip_runtime_bounds_check_because="slots, from counts of the N tokens, or N for the padding")[1]

        def late_weights(eng, a, n, top):
            return nc.values_load_multi_w_load_instructions(
                ovx[0:1, a:a + n], engines=[eng.engine], min_val=0, max_val=top,
                skip_runtime_bounds_check_because="an expert's number times its width, zero for unused windows")[1]

        def post(ins, name):
            ins.then_inc(S[name], 1)
            count[name] = count.get(name, 0) + 1

        def done(eng, ins, name):
            post(ins, name)
            eng.wait_ge(S[name], count[name])

        JOBS = [("tokT", 0, "act"), ("tokT", 1, "act"), ("h0T", 0, "act"), ("w1k", 0, "act"), ("w1q", 0, "act"), ("tokT", 2, "act"),
                ("amp", 0, "dve"), ("v", 0, "dve"), ("h0T", 1, "act"), ("w1k", 1, "act"), ("w1q", 1, "act"), ("amp", 1, "dve"),
                ("v", 1, "dve"), ("h0T", 2, "act"), ("w1k", 2, "act"), ("w1q", 2, "act"), ("amp", 2, "dve"), ("v", 2, "dve")]
        JOBS += [("w2k", g, "act") for g in range(3)] + [("w2q", g, "act") for g in range(3)]
        JOBS += [("score", 0, "dve"), ("retr", 0, "dve"), ("score", 1, "dve"), ("retr", 1, "dve"), ("rnT", 0, "act"), ("att", 0, "dve"),
                 ("score", 2, "dve"), ("retr", 2, "dve"), ("rnT", 1, "act"), ("att", 1, "dve"), ("rnT", 2, "act"), ("att", 2, "dve")]
        JOBS += [(what, g, "act") for what in ("h1T", "h1B", "z1T") for g in range(3)]
        JOB = {(what, g): n for n, (what, g, _) in enumerate(JOBS)}

        def wait_used(eng, n):
            mine = JOBS[n][2]
            eng.wait_ge(S["job_" + mine], sum(j[2] == mine for j in JOBS[:n + 1]))

        def wait_full(eng, what, g):
            n = JOB[what, g]
            eng.wait_ge(S["job_ps"], n + 1)
            return job_bank(n)

        def job_bank(n):
            return ((n + 6) % 8) * 512

        PER = dict(qk_ps=1, v_ps=1, relu_done=1, vb_done=1, prod_done=1, ft_ps=8, ft_done=8, gram_ps=4,
                   nt_done=4, grams_copied=4, masks_done=4, n_ps=2, n_done=2, w_done=2, n2_ps=2, n2_done=2, a_ps=2, a_done=2,
                   n4_done=2, x_ps=2, x8_done=2, m_ps=2, m_done=2, e_ps=2, e_done=2, t_ps=6, d_done=6, o_ps=2, o_done=2, ot_ps=1,
                   ot_done=1, y_ps=1, y_done=1, rv_done=1, scales_done=1)
        QK_BANK, V_BANK = 5, 7
        FT_BANK = [5, 6, 7, 6, 7, 6, 7, 6]
        GRAM_BANK = [5, 5, 5, 7]
        N_BANK, N2_BANK, A_BANK, X_BANK = [1, 3], [(2, 4), (0, 1)], [(3, 2), (4, 0)], [1, 3]
        M_BANK, E_BANK, T_BANK, O_BANK, OT_BANK, Y_BANK = [2, 4], [0, 1], [3, 2, 4, 0, 1, 3], [2, 4], 1, 0

        SHARED = [(i, *cg) for i, cg in enumerate([(c, g) for c in range(4) for g in range(2)] + [(c, 2) for c in range(4)])]

        UNSORT_BANK = [2, 5]
        XT_BANK = [0, 1, 0]

        def shared_bank(n):
            return (5 if n < 8 else 6) + n % 2

        def wait_tile(eng, j):
            return lambda name, c: eng.wait_ge(S[name], j * PER[name] + c)

        @block.sync
        def _(sp):
            def load(dst, src, name):
                sp.dma_start(dst, src).then_inc(S[name], 16)

            load(tokw[:], A["tokw"], "in_tok")
            for g, (a, b) in enumerate(TILES4):
                load(patches[:, :, a * PI:b * PI], A["patches"][:, :, a * PI:b * PI], f"in_patches{g}")
                if g == 0:
                    load(rows[:], A["rows"].partition_broadcast(128), "in_const")
                    load(cst[:], A["consts"], "in_const")
                    load(cols[:], A["cols"], "in_const")
                    load(scale_row[:], A["scale"].partition_broadcast(128), "in_const")
            load(attw[:], A["attw"], "in_att")
            load(wd, A["wd"], "in_wd")
            load(wu, A["wu"], "in_wu")
            load(qkvw[:], A["qkvw"], "in_qkv")
            load(wo[:], A["wo"], "in_qkv")
            load(gate[:], A["gate"], "in_qkv")
            sp.wait_ge(S["tok_ps"], 6)
            load(tab[0:E0, :], A["tab"], "in_tab")
            load(tab[E0:128, :], A["tab"], "in_tab")
            if stop > 3:
                sp.wait_ge(S["unsort_ps"], NT)
                for dst, n in ((w1, "w1"), (sw1, "sw1"), (sw2, "sw2")):
                    load(dst, A[n], "in_ffn")
                sp.wait_ge(S["y_done"], NT - 1)
                sp.wait_ge(S["v_ps"], NT)
                sp.wait_ge(S["masks_done"], 4 * NT)
                load(w3, A["w3"], "in_ffn2")
                load(w2, A["w2"], "in_ffn2")
            if stop < 5:
                for n, v in (("in_wd", 16), ("in_wu", 16), ("in_att", 16), ("in_tab", 32), ("in_qkv", 48)):
                    sp.wait_ge(S[n], v)
            if stop == 1:
                sp.wait_ge(S["h0_ready"], 3)
                sp.dma_start(dbg[0:PI, :], HA[0:PI, :, :].rearrange("p a b -> p (a b)")).then_inc(S["stored"], 16)
            elif stop == 2:
                wait_used(sp, JOB["h1B", 2])
                sp.dma_start(dbg[:, 0:N], HB[:, 0:NT, :].rearrange("p a b -> p (a b)")).then_inc(S["stored"], 16)
            elif stop == 3:
                sp.wait_ge(S["h2_ready"], NT)
                sp.dma_start(dbg[:, 0:N], HA[:, 0:NT, :].rearrange("p a b -> p (a b)")).then_inc(S["stored"], 16)
            elif stop == 4:
                sp.wait_ge(S["h3_ready"], NT)
                sp.dma_start(dbg[:, 0:N], HB[:, 0:NT, :].rearrange("p a b -> p (a b)")).then_inc(S["stored"], 16)
            else:
                sp.wait_ge(S["y_final"], NT)
                sp.dma_start(out, HA[:, 0:NT, :]).then_inc(S["stored"], 16)
            sp.wait_ge(S["stored"], 16)

        @block.tensor
        def _(pe):
            I = C["ident"]

            def tokenize(g, far):
                a, b = TILES4[g]
                w = (b - a) * PI
                for k in range(KC):
                    last = nc.tensor.matmul(ps[:, (2 * g + far) * 512:(2 * g + far) * 512 + w],
                                            tokw[:, k * 256 + far * 128:k * 256 + far * 128 + 128],
                                            patches[:, k, a * PI:b * PI], start=(k == 0), stop=(k == KC - 1))
                post(last, "tok_ps")

            def job(what, g):
                n = JOB[what, g]
                assert n == count.get("job_ps", 0)
                if n >= 8:
                    wait_used(pe, n - 8)
                elif n >= 6:
                    pe.wait_ge(S["tok_used"], 3)
                elif n >= 2:
                    pe.wait_ge(S["tok_used"], 2)
                return job_bank(n)

            def tiles_T(what, g, src, p, groups, w):
                a, b = groups[g]
                o = job(what, g)
                for t in range(a, b):
                    last = nc.tensor.transpose(ps[:, o + (t - a) * w:o + (t - a) * w + w], src[0:p, t, :], I[0:p, 0:p])
                post(last, "job_ps")

            def columns(what, g, w, src):
                a, b = TILES4[g]
                o = job(what, g)
                post(nc.tensor.matmul(ps[:, o:o + (b - a) * PI], w, src[:, a * PI:b * PI], start=True, stop=True), "job_ps")

            def rows_of(what, g, left, right):
                a, b = TILES4[g]
                o = job(what, g)
                for t in range(a, b):
                    r = right(t)
                    w = r.shape[-1]
                    last = nc.tensor.matmul(ps[0:PI, o + (t - a) * w:o + (t - a + 1) * w], left(t), r, start=True, stop=True)
                post(last, "job_ps")

            def tile_of(buf, p=128):
                return lambda t: buf[0:p, t * PI:(t + 1) * PI]

            def att_w(i):
                return attw[:, i * 128:(i + 1) * 128]

            def tokens_back(g):
                pe.wait_ge(S["tok_used"], g + 1)
                if g == 0:
                    pe.wait_ge(S["in_const"], 64)
                a, b = TILES4[g]
                o = job("tokT", g)
                for t in range(a, b):
                    last = nc.tensor.transpose(ps[0:PI, o + (t - a) * 128:o + (t - a) * 128 + 128],
                                               B[1][:, t * PI:(t + 1) * PI], I)
                post(last, "job_ps")

            def first_layers(g):
                pe.wait_ge(S["h0_ready"], g + 1)
                if g == 0:
                    pe.wait_ge(S["in_att"], 16)
                tiles_T("h0T", g, HA, PI, TILES4, PI)
                wait_used(pe, JOB["h0T", g])
                columns("w1k", g, att_w(0), B[0])
                columns("w1q", g, att_w(1), B[0])

            def amplitudes_values(g):
                columns("amp", g, att_w(4), B[0])
                rows_of("v", g, tile_of(B[0]), lambda t: att_w(5))

            pe.wait_ge(S["in_tok"], 16)
            for g in range(3):
                pe.wait_ge(S[f"in_patches{g}"], 16)
                tokenize(g, 0)
                if g == 1:
                    tokens_back(0)
                tokenize(g, 1)
            tokens_back(1)
            if stop == 1:
                tokens_back(2)
                return
            first_layers(0)
            tokens_back(2)
            amplitudes_values(0)
            first_layers(1)
            amplitudes_values(1)
            first_layers(2)
            amplitudes_values(2)
            for g in range(3):
                wait_used(pe, JOB["w1k", g])
                columns("w2k", g, att_w(2), B[1])
            for g in range(3):
                wait_used(pe, JOB["w1q", g])
                columns("w2q", g, att_w(3), B[2])

            def score(g):
                pe.wait_ge(S["kq_ready"], g + 1)
                rows_of("score", g, tile_of(B[3]), tile_of(B[4]))

            def retrieve(g):
                wait_used(pe, JOB["score", g])
                wait_used(pe, JOB["v", g])
                rows_of("retr", g, tile_of(B[5], PI), lambda t: HB[0:PI, t, :])

            def out_layer(g):
                pe.wait_ge(S["retr_ready"], g + 1)
                tiles_T("rnT", g, HB, PI, TILES4, PI)
                wait_used(pe, JOB["rnT", g])
                rows_of("att", g, tile_of(B[1]), lambda t: att_w(6))

            score(0)
            retrieve(0)
            score(1)
            retrieve(1)
            out_layer(0)
            score(2)
            retrieve(2)
            out_layer(1)
            out_layer(2)
            for g in range(3):
                pe.wait_ge(S["h1_ready"], g + 1)
                tiles_T("h1T", g, HA, PI, TILES4, PI)
            wait_used(pe, JOB["h1T", 2])
            for g in range(3):
                tiles_T("h1B", g, B[0][:, 0:N].rearrange("p (t n) -> p t n", n=128), 128, TILES9, 128)
            if stop == 2:
                return
            for g in range(3):
                pe.wait_ge(S["z1_ready"], g + 1)
                tiles_T("z1T", g, HA, 128, TILES9, 128)

            pe.wait_ge(S["sig_ready"], 1)
            wait_used(pe, JOB["z1T", 2])
            for t in range(NT):
                for i, w in enumerate((tsig8, csigb)):
                    last = nc.tensor.matmul(ps[:, t * E0:(t + 1) * E0], sgT[:, t * 128:(t + 1) * 128], w[:],
                                            start=(i == 0), stop=(i == 1))
            post(last, "key_ps")

            def position_rows(o):
                for j in range(NT):
                    last = nc.tensor.matmul(ps[:, o + j * 128:o + (j + 1) * 128], pos[:, j:j + 1].to_broadcast([128, 128]),
                                            I, start=True, stop=True)
                post(last, "rows_ps")

            def route_and_sort(E, r, dup, src, meanwhile=lambda n: None):
                pe.wait_ge(S["oh_ready"], r + 1)
                for j in range(NT):
                    for i in range(j + 1):
                        nc.tensor.matmul(ps[:, j * E:(j + 1) * E], trib[:] if i == j else oneb[:], oh[:, i, 0, 0:E],
                                         start=(i == 0), stop=(i == j))
                M = dup * E
                for i in range(NT):
                    last = nc.tensor.matmul(ps[0:M, 1024:1025], oh[:, i, 0:dup, 0:E], oneb[:, 0:1],
                                            start=(i == 0), stop=(i == NT - 1))
                post(last, "rank_ps")
                pe.wait_ge(S["cnt_ready"], r + 1)
                cnt = small[0:E, 0:1]
                tri = C["triS"][0:E, 0:E]
                for d in range(dup):
                    nc.tensor.matmul(ps[d * E:d * E + E, 1536:1537], tri, cnt, start=True, stop=True)
                post(nc.tensor.matmul(ps[:, 2048:2048 + E], cnt.to_broadcast([E, 128]), tri, start=True, stop=True), "start_ps")
                meanwhile(4)
                for j in range(NT):
                    if j == 3:
                        pe.wait_ge(S["route_cols"], r + 1)
                        o = 512
                        late, late128, last_slot = small[0:E, 3:4], small[0:E, 4:5], small[0:E, 5:6]
                        nc.tensor.matmul(ps[0:NOV, o:o + E], late.to_broadcast([E, NOV]), C["triI"][0:E, 0:E], start=True, stop=True)
                        nc.tensor.matmul(ps[0:NOV, o + 64:o + 64 + E], late.to_broadcast([E, NOV]), tri, start=True, stop=True)
                        nc.tensor.matmul(ps[0:NOV, o + 128:o + 128 + E], last_slot.to_broadcast([E, NOV]), I[0:E, 0:E],
                                         start=True, stop=False)
                        post(nc.tensor.matmul(ps[0:NOV, o + 128:o + 128 + E], late128.to_broadcast([E, NOV]), tri,
                                              start=False, stop=True), "late_ps")
                    if j == 6:
                        pe.wait_ge(S["pair_cols"], r + 1)
                        for c in range(2):
                            last = nc.tensor.matmul(ps[0:1, 512 + c * 128:512 + c * 128 + NOV], small[0:NOV, 9 + c:10 + c],
                                                    I[0:NOV, 0:NOV], start=True, stop=True)
                        post(last, "pairs_ps")
                    if j == NT - 1 and r == 1:
                        pe.wait_ge(S["pairs_ready"], 2)
                        position_rows(0)
                    n = r * NT + j
                    pe.wait_ge(S["perm_made"], n + 1)
                    for g in range(3):
                        last = nc.tensor.matmul(ps[:, 1536 + g * 512:1536 + g * 512 + 384], src[:, j, :],
                                                B[1 + j % 2][:, g * 384:(g + 1) * 384], start=(j == 0), stop=(j == NT - 1))
                    post(last, "perm_used")

            def unsort(r, i):
                n = r * NT + i
                if i >= 3:
                    pe.wait_ge(S["unsort_used"], n - 2)
                o = (UNSORT_BANK[r] + i % 3) * 512
                for s_ in range(NT):
                    if i == 0:
                        pe.wait_ge(S["unperm_made"], r * NT + s_ + 1)
                    last = nc.tensor.matmul(ps[:, o:o + 128], unperm[s_][:, i * 128:(i + 1) * 128], yrows[:, s_, :],
                                            start=(s_ == 0), stop=(s_ == NT - 1))
                post(last, "unsort_ps")

            def expert_windows(w, late, p):
                for g in range(2 * HG + LG):
                    late_group, up = g >= 2 * HG, g < 2 * HG and g % 2
                    a = g - HG if late_group else g // 2
                    first_window = g * GRP if late_group else up * E0 // 2 + a * GRP
                    at = window_starts(pe, first_window, GRP)
                    if a >= 2 or p > 0:
                        if up:
                            pe.wait_ge(S["upper_copied"], (p * HG + a - 1) * GRP)
                        else:
                            pe.wait_ge(S["win_copied"], (p * (HG + LG) + a - 1) * GRP)
                    if g == 2 * HG:
                        pe.wait_ge(S["ov0_ready"], p + 1)
                    for i in range(GRP):
                        e = first_window + i
                        wt = w[:, e * 128:(e + 1) * 128] if e < E0 else late[:, (e - E0) * 128:(e - E0 + 1) * 128]
                        o = (2 * up + a % 2) * 512 + i * 128
                        last = nc.tensor.matmul(ps[:, o:o + 128], wt, B[4][:, bass.ds(at[i], 128)], start=True, stop=True)
                    post(last, "upper_ps" if up else "win_ps")
                    if p == 1 and g == 5:
                        position_rows(2048)

            def columns_to_rows(r):
                for t in range(NT):
                    last = nc.tensor.transpose(ps[:, 1536 + t * 128:1536 + (t + 1) * 128], B[5][:, t * 128:(t + 1) * 128], I)
                post(last, "yT_ps")

            route_and_sort(E0, 0, 2, HA)
            pe.wait_ge(S["in_wd"], 16)
            pe.wait_ge(S["sorted_ready"], 1)
            pe.wait_ge(S["pads_zero"], 1)
            expert_windows(wd, ov_wd, 0)
            pe.wait_ge(S["tab_split"], 1)
            pe.wait_ge(S["slots_ready"], 1)
            pe.wait_ge(S["hn_ready"], 1)
            n = 0
            for g in range(GRID):
                for c in range(3):
                    if 4 <= n < 7:
                        pe.wait_ge(S["first_cells"], n - 3)
                    if n >= 7:
                        pe.wait_ge(S["tab_used"], n - 6)
                    for v in range(2):
                        o = (n % 4) * 1024 + v * 512
                        w = (g * 2 + v) * 128
                        nc.tensor.matmul(ps[:, o:o + 384], tab_hi[:, w:w + 128], ohs[:, c * 384:(c + 1) * 384],
                                         start=True, stop=False)
                        last = nc.tensor.matmul(ps[:, o:o + 384], tab_lo[:, w:w + 128], ohs[0:E0, c * 384:(c + 1) * 384],
                                                start=False, stop=True)
                    post(last, "tab_ps")
                    n += 1
            pe.wait_ge(S["hs_ready"], 1)
            pe.wait_ge(S["in_wu"], 16)
            expert_windows(wu, ov_wu, 1)
            pe.wait_ge(S["win_copied"], 2 * (HG + LG) * GRP)
            columns_to_rows(0)
            pe.wait_ge(S["accs_copied"], 1)
            for i in range(4):
                unsort(0, i)
            if stop == 3:
                for i in range(4, NT):
                    unsort(0, i)
                return

            def tokens_T(g):
                a, b = TILES9[g]
                pe.wait_ge(S["h2_ready"], b)
                if g == 2:
                    pe.wait_ge(S["xT_done"], 1)
                for t in range(a, b):
                    o = XT_BANK[g] * 512 + (t - a) * 128
                    last = nc.tensor.transpose(ps[:, o:o + 128], HA[:, t, :], I)
                post(last, "xT_ps")

            unsort(0, 4)
            tokens_T(0)
            unsort(0, 5)

            def mm(o, lhsT, rhs, n=128):
                return nc.tensor.matmul(ps[:, o:o + n], lhsT, rhs, start=True, stop=True)

            def per_half(h, head):
                for i in range(4):
                    last = head(4 * h + i, i)
                return last

            def gram_bank_free(j, q):
                wait_tile(pe, j)("nt_done", q + 1)

            def queries_keys(j):
                if j:
                    gram_bank_free(j - 1, 2)
                x = xT[:, j * 128:(j + 1) * 128]
                mm(QK_BANK * 512, x, qkvw[:, 0:512], 512)
                mm(QK_BANK * 512 + 512, x, qkvw[:, 512:1024], 512).then_inc(S["qk_ps"], 1)

            def values(j):
                if j:
                    gram_bank_free(j - 1, 3)
                mm(V_BANK * 512, xT[:, j * 128:(j + 1) * 128], qkvw[:, 1024:1536], 512).then_inc(S["v_ps"], 1)

            def features_T(j, h):
                w = wait_tile(pe, j)
                if h == 0:
                    w("prod_done", 1)
                if h == 2:
                    w("vb_done", 1)
                if h >= 3:
                    w("ft_done", h - 1)
                for v in range(2):
                    for i, src in enumerate((8 + h, h)):
                        o = FT_BANK[h] * 512 + (v * 2 + i) * 128
                        last = nc.tensor.transpose(ps[:, o:o + 128], feat[:, v, src, :], I)
                last.then_inc(S["ft_ps"], 1)

            def gram(j, q):
                w = wait_tile(pe, j)
                w("ft_done", 2 * q + 2)
                if q in (1, 2):
                    gram_bank_free(j, q - 1)
                for i in range(2):
                    o = GRAM_BANK[q] * 512 + i * 256
                    for v in range(2):
                        last = nc.tensor.matmul(ps[:, o:o + 256], featT[:, 2 * q + i, v, 0:128], featT[:, 2 * q + i, v, :],
                                                start=(v == 0), stop=(v == 1))
                last.then_inc(S["gram_ps"], 1)

            def turn_n(j, h):
                wait_tile(pe, j)("nt_done", 2 * h + 2)
                per_half(h, lambda hd, i: nc.tensor.transpose(ps[:, N_BANK[h] * 512 + i * 128:N_BANK[h] * 512 + (i + 1) * 128],
                                                              nt[j % 2][:, hd, :], I)).then_inc(S["n_ps"], 1)

            def square(j, h):
                w = wait_tile(pe, j)
                w("n_done", h + 1)
                if h == 1 and j:
                    w("y_done", 0)
                a, b = N2_BANK[h]
                per_half(h, lambda hd, i: mm(a * 512 + i * 128, nn[:, hd, :], nt[j % 2][:, hd, :]))
                per_half(h, lambda hd, i: mm(b * 512 + i * 128, nt[j % 2][:, hd, :], nn[:, hd, :])).then_inc(S["n2_ps"], 1)

            def second_factor(j, h):
                w = wait_tile(pe, j)
                w("n2_done", h + 1)
                w("w_done", h + 1)
                a, b = A_BANK[h]
                per_half(h, lambda hd, i: mm(a * 512 + i * 128, n2[:, hd, :], ww[j % 2][:, hd, :]))
                per_half(h, lambda hd, i: mm(b * 512 + i * 128, n2t[:, hd, :], n2[:, hd, :])).then_inc(S["a_ps"], 1)

            def third_factor(j, h):
                w = wait_tile(pe, j)
                w("a_done", h + 1)
                w("n4_done", h + 1)
                per_half(h, lambda hd, i: mm(X_BANK[h] * 512 + i * 128, n2t[:, hd, :], ww[j % 2][:, hd, :])).then_inc(S["x_ps"], 1)

            def below(j, h):
                w = wait_tile(pe, j)
                w("x8_done", h + 1)
                w("masks_done", 2 * h + 2)
                per_half(h, lambda hd, i: mm(M_BANK[h] * 512 + i * 128, ct[j % 2][:, hd, :], nn[:, hd, :])).then_inc(S["m_ps"], 1)

            def solve_first(j, h):
                w = wait_tile(pe, j)
                w("x8_done", h + 1)
                w("rv_done", 1)
                per_half(h, lambda hd, i: mm(E_BANK[h] * 512 + i * 64, nn[:, hd, :], rhs_v[j % 2][:, hd, :], 64)).then_inc(S["e_ps"], 1)

            def substitute(j, h, r):
                w = wait_tile(pe, j)
                if r == 0:
                    w("m_done", h + 1)
                    w("e_done", h + 1)
                else:
                    w("d_done", 2 * r + h - 1)
                known = first if r == 0 else delta
                per_half(h, lambda hd, i: mm(T_BANK[2 * r + h] * 512 + i * 64, below_T[:, hd, :], known[:, hd, 0:64], 64)).then_inc(S["t_ps"], 1)

            def outputs(j, h):
                w = wait_tile(pe, j)
                w("scales_done", 1)
                w("masks_done", 2 * h + 2)
                per_half(h, lambda hd, i: mm(O_BANK[h] * 512 + i * 65, smm[j % 2][:, hd, :], delta[:, hd, :], 65)).then_inc(S["o_ps"], 1)

            def outputs_T(j):
                wait_tile(pe, j)("o_done", 2)
                for i in range(4):
                    last = nc.tensor.transpose(ps[:, OT_BANK * 512 + i * 128:OT_BANK * 512 + i * 128 + 128],
                                               regA[:, 8704 + i * 128:8704 + i * 128 + 128], I)
                last.then_inc(S["ot_ps"], 1)

            def project(j):
                wait_tile(pe, j)("ot_done", 1)
                for i in range(4):
                    last = nc.tensor.matmul(ps[:, Y_BANK * 512:Y_BANK * 512 + 128], outT[:, i * 128:(i + 1) * 128],
                                            wo[:, i * 128:(i + 1) * 128], start=(i == 0), stop=(i == 3))
                last.then_inc(S["y_ps"], 1)

            def both(piece, *args):
                for h in range(2):
                    piece(args[0], h, *args[1:])

            pe.wait_ge(S["in_qkv"], 48)

            def run(f, *pieces):
                if f < NT:
                    for piece, *i in pieces:
                        piece(f, *i)

            FIRST7 = ((0, 7), (7, 9))

            def ffn_tokens_T(n):
                a, b = FIRST7[n]
                pe.wait_ge(S["h3_ready"], b)
                for t in range(a, b):
                    last = nc.tensor.transpose(ps[:, 2560 + (t - a) * 128:2560 + (t - a + 1) * 128], HB[:, t, :], I)
                post(last, "h3T_ps")

            def gate_logits(n):
                a, b = FIRST7[n]
                pe.wait_ge(S["h3T_ready"], n + 1)
                for t in range(a, b):
                    last = nc.tensor.matmul(ps[:, 3584 + t * E1:3584 + (t + 1) * E1], h3T[:, t * 128:(t + 1) * 128], gate[:],
                                            start=True, stop=True)
                post(last, "gate_ps")

            shared = iter(SHARED)

            def shared_up(count_):
                for _ in range(count_):
                    n, c, g = next(shared)
                    if n == 0:
                        pe.wait_ge(S["in_ffn"], 48)
                    if n >= 2:
                        pe.wait_ge(S["s1_used"], 8 if n == 8 else n - 1)
                    o = shared_bank(n) * 512
                    post(nc.tensor.matmul(ps[:, o:o + 384], sw1[:, c * 128:(c + 1) * 128], h3T[:, g * 384:(g + 1) * 384],
                                          start=True, stop=True), "s1_ps")

            pe.wait_ge(S["xT_done"], 1)
            queries_keys(0)
            values(0)
            unsort(0, 6)
            unsort(0, 7)
            unsort(0, 8)
            tokens_T(1)
            tokens_T(2)
            features_T(0, 0)
            features_T(0, 1)
            pe.wait_ge(S["xT_done"], 3)
            for t in range(NT):
                last = mm(512 + t * NH, xT[:, t * 128:(t + 1) * 128], qkvw[:, 1536:1536 + NH], NH)
            post(last, "beta_ps")
            for h in range(2, NH):
                features_T(0, h)
                if h in (2, 4, 6):
                    gram(0, h // 2 - 1)
            gram(0, 3)
            queries_keys(1)
            for j in range(NT):
                f = j + 1
                both(turn_n, j)
                run(f, (values,))
                both(square, j)
                both(second_factor, j)
                both(third_factor, j)
                run(f, (features_T, 0), (features_T, 1))
                if f == NT and stop > 4:
                    ffn_tokens_T(0)
                for h in range(2):
                    below(j, h)
                    solve_first(j, h)
                run(f, (features_T, 2), (gram, 0), (features_T, 3), (features_T, 4))
                if f == NT and stop > 4:
                    gate_logits(0)
                    shared_up(1)
                both(substitute, j, 0)
                run(f, (gram, 1), (features_T, 5))
                if f == NT and stop > 4:
                    shared_up(2)
                both(substitute, j, 1)
                run(f, (features_T, 6), (gram, 2))
                if f == NT and stop > 4:
                    shared_up(2)
                both(substitute, j, 2)
                run(f, (features_T, 7), (gram, 3))
                if f == NT and stop > 4:
                    shared_up(3)
                both(outputs, j)
                run(f + 1, (queries_keys,))
                outputs_T(j)
                project(j)
            if stop == 4:
                return
            def shared_down(o, t):
                for c in range(4):
                    last = nc.tensor.matmul(ps[:, o:o + 128], gs[:, c * N + t * 128:c * N + (t + 1) * 128],
                                            sw2[:, c * 128:(c + 1) * 128], start=(c == 0), stop=(c == 3))
                return last

            pe.wait_ge(S["s1_used"], 8)
            for t in range(6):
                last = shared_down(2560 + t * 128, t)
            post(last, "sh_early_ps")
            pe.wait_ge(S["sh_early_done"], 1)
            ffn_tokens_T(1)
            gate_logits(1)
            route_and_sort(E1, 1, 1, HB, shared_up)
            pe.wait_ge(S["in_ffn2"], 32)
            pe.wait_ge(S["sorted_ready"], 2)
            pe.wait_ge(S["posrow_ready"], 2)

            def up(k):
                if k % 4 == 0:
                    starts[:] = window_starts(pe, k, 4)
                if k >= 2:
                    pe.wait_ge(S["g_done"], k - 1)
                if k >= E1:
                    pe.wait_ge(S["ov_up_ready"], k - E1 + 1)
                for v, w in enumerate((w1, w3)):
                    for c in range(4):
                        o = (k % 2) * 1024 + v * 512 + c * 128
                        wt = w[:, k * INNER + c * 128:k * INNER + (c + 1) * 128] if k < E1 else ov1[:, k % 2, v, c * 128:(c + 1) * 128]
                        last = nc.tensor.matmul(ps[:, o:o + 128], wt, B[4][:, bass.ds(starts[k % 4], 128)], start=True, stop=True)
                post(last, "up_ps")

            def down(k):
                pe.wait_ge(S["g_done"], k + 1)
                if k >= 2:
                    pe.wait_ge(S["y1_copied"], k - 1)
                if k >= E1:
                    pe.wait_ge(S["ov_down_ready"], k - E1 + 1)
                for c in range(4):
                    wt = w2[:, k * INNER + c * 128:k * INNER + (c + 1) * 128] if k < E1 else ov1[:, k % 2, 2, c * 128:(c + 1) * 128]
                    last = nc.tensor.matmul(ps[:, 2048 + (k % 2) * 512:2176 + (k % 2) * 512], wt, gg[:, k % 2, c * 128:(c + 1) * 128],
                                            start=(c == 0), stop=(c == 3))
                post(last, "y1_ps")

            starts = []
            up(0)
            for k in range(1, E1 + NOV):
                up(k)
                down(k - 1)
            down(E1 + NOV - 1)
            pe.wait_ge(S["y1_copied"], E1 + NOV)
            columns_to_rows(1)
            for t in range(6, NT):
                last = shared_down((t - 6) * 128, t)
            post(last, "sh_ps")
            pe.wait_ge(S["accs_copied"], 2)
            for i in range(NT):
                unsort(1, i)

        @block.scalar
        def _(act):
            act.wait_ge(S["in_const"], 64)
            def own_channels(g):
                a, b = TILES4[g]
                act.wait_ge(S["tok_ps"], 2 * g + 2)
                post(nc.scalar.activation(B[1][:, a * PI:b * PI], ps[:, 2 * g * 512:2 * g * 512 + (b - a) * PI], ACT.Identity,
                                          bias=Cc["tok_bias"]), "tok_own")

            def tokens_back(g):
                a, b = TILES4[g]
                o = wait_full(act, "tokT", g)
                v = ps[0:PI, o:o + (b - a) * 128].rearrange("p (t q r e) -> p r t q e", q=4, r=2, e=16)
                nc.scalar.activation(HA[0:PI, a:b, 0:64].rearrange("p t (q e) -> p t q e", e=16), v[:, 1], ACT.Copy)
                post(nc.scalar.activation(HA[0:PI, a:b, 64:128].rearrange("p t (q e) -> p t q e", e=16), v[:, 0], ACT.Copy), "job_act")

            def columns(what, g, dst, func, **kw):
                a, b = TILES4[g]
                o = wait_full(act, what, g)
                post(nc.scalar.activation(dst[:, a * PI:b * PI], ps[:, o:o + (b - a) * PI], func, **kw), "job_act")

            def first_layers(g):
                columns("h0T", g, B[0], ACT.Copy)
                columns("w1k", g, B[1], ACT.Gelu, bias=Cc["ke_b1"])
                columns("w1q", g, B[2], ACT.Gelu, bias=Cc["qe_b1"])

            own_channels(0)
            tokens_back(0)
            own_channels(1)
            tokens_back(1)
            own_channels(2)
            if stop == 1:
                tokens_back(2)
                return
            first_layers(0)
            tokens_back(2)
            first_layers(1)
            first_layers(2)
            wait_used(act, JOB["amp", 2])
            act.wait_ge(S["job_ps"], JOB["v", 2] + 1)
            done(act, nc.scalar.activation(B[0][:], B[5][:, 0:NI], ACT.Abs), "z_abs")
            done(act, nc.scalar.activation(B[0][:], B[0][:], ACT.Exp, scale=-1.0), "z_abs")
            post(nc.scalar.activation(B[0][:], B[0][:], ACT.Ln, bias=C["one"]), "ln_ready")
            for what, dst, bias in (("w2k", B[3], "ke_b2"), ("w2q", B[4], "qe_b2")):
                for g in range(3):
                    columns(what, g, dst, ACT.Tanh, bias=Cc[bias])
            wait_used(act, JOB["w2q", 2])
            for i in range(2):
                done(act, nc.scalar.activation(B[3 + i][0:64, 0:NI], B[3 + i][0:64, 0:NI], ACT.Abs), "phase_abs")
            act.wait_ge(S["phase_held"], 2)
            for a, b in TILES4:
                for i in range(2):
                    v = B[3 + i][:, a * PI:b * PI]
                    post(nc.scalar.activation(v, v, ACT.Sin, bias=C["sin_bias"], scale=C["sin_scale"]), "sines")
            act.wait_ge(S["in_tab"], 32)
            nc.scalar.activation(tab_hi, tab, ACT.Copy).then_inc(S["tab_high"], 1)
            for g in range(3):
                columns("rnT", g, B[1], ACT.Identity, scale=Cc["ln_g"], bias=Cc["ln_b"])
            view = B[0][:, 0:N].rearrange("p (q b) -> p b q", b=NIMG)
            for g, (a, b) in enumerate(TILES4):
                o = wait_full(act, "h1T", g)
                n = min(3 * b, NIMG) - 3 * a
                post(nc.scalar.activation(view[:, 3 * a:3 * a + n, :],
                                          ps[:, o:o + n * NPATCH].rearrange("p (b q) -> p b q", q=NPATCH), ACT.Copy), "job_act")
            for g, (a, b) in enumerate(TILES9):
                o = wait_full(act, "h1B", g)
                post(nc.scalar.activation(HB[:, a:b, :], ps[:, o:o + (b - a) * 128].rearrange("p (t d) -> p t d", d=128), ACT.Copy),
                     "job_act")
            if stop == 2:
                return
            for g, (a, b) in enumerate(TILES9):
                o = wait_full(act, "z1T", g)
                post(nc.scalar.activation(sgT[:, a * 128:b * 128], ps[:, o:o + (b - a) * 128], ACT.Sign,
                                          scale=Cc["gamma"], bias=Cc["beta"]), "job_act")
            act.wait_ge(S["tab_rest"], 1)
            nc.scalar.activation(tab_hi[E0:128, :], tab[E0:128, :], ACT.Copy)
            nc.scalar.activation(tab_lo, tab[0:E0, :], ACT.Copy).then_inc(S["tab_low"], 1)

            def posrow(r, o):
                act.wait_ge(S["rows_ps"], r + 1)
                post(nc.scalar.activation(B[3][:, 0:N], ps[:, o:o + N], ACT.Copy), "posrow_ready")

            def copy_windows(p):
                for g in range(HG + LG):
                    if g == HG and p == 1:
                        posrow(0, 2048)
                    if g == HG:
                        act.wait_ge(S["merged"], p + 1)
                    at = window_starts(act, g * GRP if g < HG else E0 + (g - HG) * GRP, GRP)
                    act.wait_ge(S["win_ps"], p * (HG + LG) + g + 1)
                    for i in range(GRP):
                        o = (g % 2) * 512 + i * 128
                        ins = nc.scalar.activation(B[5][:, bass.ds(at[i], 128)], ps[:, o:o + 128], ACT.Copy)
                        done(act, ins, "win_copied")

            def rows_out(r):
                act.wait_ge(S["yT_ps"], r + 1)
                post(nc.scalar.activation(B[4][:, 0:N], ps[:, 1536:1536 + N], ACT.Copy), "accs_copied")

            act.wait_ge(S["perm_used"], NT)
            act.wait_ge(S["pairs_ready"], 1)
            post(nc.scalar.activation(B[4][:, 0:N].rearrange("p (g n) -> p g n", g=3),
                                      ps[:, 1536:3072].rearrange("p (g n) -> p g n", g=3)[:, :, 0:384], ACT.Identity,
                                      scale=Cc["gamma"], bias=Cc["beta"]), "sorted_ready")
            copy_windows(0)
            done(act, nc.scalar.activation(B[5][:, 0:N], B[5][:, 0:N], ACT.Sigmoid), "hn_ready")
            post(nc.scalar.activation(B[2][:, 0:N], B[5][:, 0:N], ACT.Copy, scale=float(GRID)), "u_ready")
            for c in range(3):
                act.wait_ge(S["tab_ps"], c + 1)
                o = c * 1024
                post(nc.scalar.activation(picked[:, :, c * 384:(c + 1) * 384],
                                          ps[:, o:o + 1024].rearrange("p (v n) -> p v n", v=2)[:, :, 0:384], ACT.Copy), "first_cells")
            act.wait_ge(S["cell_ready"], 1)
            for g in range(1, GRID):
                if g >= 3:
                    act.wait_ge(S["tab_used"], 3 * (g - 2))
                post(nc.scalar.activation(masks[:, g % 2, :], B[1][:, 0:N], ACT.Relu, bias=C["from_cell"][:, g:g + 1]), "mask_ready")
            act.wait_ge(S["hs_ready"], 1)
            copy_windows(1)
            rows_out(0)
            post(nc.scalar.activation(HB[:, 0:NT, :], HB[:, 0:NT, :], ACT.Copy, scale=2.0), "twice_ready")
            if stop == 3:
                return

            def relu_parts(j):
                w = wait_tile(act, j)
                w("qk_ps", 1)
                if j:
                    w("prod_done", 0)
                qk = ps[:, QK_BANK * 512:QK_BANK * 512 + 1024].rearrange("p (h e) -> p h e", h=16)
                nc.scalar.activation(relus[:, :, 2:66], qk, ACT.Relu)
                nc.scalar.activation(relus[:, :, 0:2], qk[:, :, 62:64], ACT.Relu, scale=-1.0)
                nc.scalar.activation(relus[:, :, 66:130], qk, ACT.Relu, scale=-1.0).then_inc(S["relu_done"], 1)

            def values(j):
                w = wait_tile(act, j)
                w("v_ps", 1)
                if j:
                    w("rv_done", 0)
                nc.scalar.activation(vals, ps[:, V_BANK * 512:(V_BANK + 1) * 512].rearrange("p (h e) -> p h e", h=NH),
                                     ACT.Copy).then_inc(S["vb_done"], 1)

            def features_T(j, h):
                wait_tile(act, j)("ft_ps", h + 1)
                o = FT_BANK[h] * 512
                nc.scalar.activation(featT[:, h, :, :], ps[:, o:o + 512].rearrange("p (v f) -> p v f", v=2), ACT.Copy).then_inc(S["ft_done"], 1)

            def evac(dst, bank_, h):
                return nc.scalar.activation(dst[:, 4 * h:4 * h + 4, :], bank(bank_).rearrange("p (h f) -> p h f", h=4), ACT.Copy)

            def tokens_T(g):
                a, b = TILES9[g]
                act.wait_ge(S["xT_ps"], g + 1)
                post(nc.scalar.activation(xT[:, a * 128:b * 128], ps[:, XT_BANK[g] * 512:XT_BANK[g] * 512 + (b - a) * 128],
                                          ACT.Copy), "xT_done")

            def copy_grams(j, q):
                w = wait_tile(act, j)
                w("gram_ps", q + 1)
                if q >= 2:
                    w("masks_done", q - 1)
                elif j:
                    wait_tile(act, j - 1)("masks_done", q + 3)
                nc.scalar.activation(grams[:, q % 2], bank(GRAM_BANK[q]).rearrange("p (h f) -> p h f", h=2), ACT.Copy).then_inc(S["grams_copied"], 1)

            def ffn_tokens_T(n):
                a, b = ((0, 7), (7, 9))[n]
                act.wait_ge(S["h3T_ps"], n + 1)
                post(nc.scalar.activation(h3T[:, a * 128:b * 128], ps[:, 2560:2560 + (b - a) * 128], ACT.Copy), "h3T_ready")

            def shared_up(n):
                _, c, g = SHARED[n]
                act.wait_ge(S["s1_ps"], n + 1)
                o = shared_bank(n) * 512
                post(nc.scalar.activation(gs[:, c * N + g * 384:c * N + (g + 1) * 384], ps[:, o:o + 384], ACT.Gelu), "s1_used")

            tokens_T(0)
            relu_parts(0)
            values(0)
            tokens_T(1)
            tokens_T(2)
            act.wait_ge(S["beta_ps"], 1)
            nc.scalar.activation(beta[:], bank(1, NT * NH).rearrange("p (t h) -> p t h", h=NH), ACT.Sigmoid).then_inc(S["beta_done"], 1)
            for h in range(NH):
                features_T(0, h)
                if h in (2, 4, 6):
                    copy_grams(0, h // 2 - 1)
            copy_grams(0, 3)
            relu_parts(1)
            for j in range(NT):
                f = j + 1
                w = wait_tile(act, j)
                for h in range(2):
                    w("n_ps", h + 1)
                    evac(nn, N_BANK[h], h).then_inc(S["n_done"], 1)
                if f < NT:
                    values(f)
                for h in range(2):
                    w("n2_ps", h + 1)
                    evac(n2t, N2_BANK[h][0], h)
                    evac(n2, N2_BANK[h][1], h).then_inc(S["n2_done"], 1)
                for h in range(2):
                    w("a_ps", h + 1)
                    evac(n2t, A_BANK[h][1], h).then_inc(S["n4_done"], 1)
                if f < NT:
                    features_T(f, 0)
                    features_T(f, 1)
                for h in range(2):
                    w("e_ps", h + 1)
                    nc.scalar.activation(first[:, 4 * h:4 * h + 4, :], bank(E_BANK[h], 256).rearrange("p (h e) -> p h e", h=4),
                                         ACT.Copy).then_inc(S["e_done"], 1)
                if f < NT:
                    features_T(f, 2)
                    copy_grams(f, 0)
                    features_T(f, 3)
                    features_T(f, 4)
                    copy_grams(f, 1)
                    features_T(f, 5)
                    features_T(f, 6)
                    copy_grams(f, 2)
                    features_T(f, 7)
                    copy_grams(f, 3)
                if f == NT and stop > 4:
                    ffn_tokens_T(0)
                    for n in range(8):
                        shared_up(n)
                w("ot_ps", 1)
                nc.scalar.activation(outT, bank(OT_BANK), ACT.Copy).then_inc(S["ot_done"], 1)
                if f + 1 < NT:
                    relu_parts(f + 1)
            if stop == 4:
                return
            act.wait_ge(S["sh_early_ps"], 1)
            post(nc.scalar.activation(sh_early, ps[:, 2560:2560 + 768], ACT.Copy), "sh_early_done")
            ffn_tokens_T(1)
            for n in range(8, 12):
                shared_up(n)
            posrow(1, 0)
            act.wait_ge(S["perm_used"], 2 * NT)
            post(nc.scalar.activation(B[4][:, 0:N].rearrange("p (g n) -> p g n", g=3),
                                      ps[:, 1536:3072].rearrange("p (g n) -> p g n", g=3)[:, :, 0:384], ACT.Copy), "sorted_ready")
            starts, places = [], []

            def silu(k):
                act.wait_ge(S["up_ps"], k + 1)
                if k >= 2:
                    act.wait_ge(S["g_done"], k - 1)
                post(nc.scalar.activation(sg[:, k % 2, :], ps[:, (k % 2) * 1024:(k % 2) * 1024 + 512], ACT.Silu), "silu_done")

            def result(k):
                if k % 4 == 0:
                    starts[:] = window_starts(act, k, 4)
                act.wait_ge(S["y1_ps"], k + 1)
                if k:
                    act.wait_ge(S["y1_copied"], k)
                post(nc.scalar.activation(B[5][:, bass.ds(starts[k % 4], 128)], ps[:, 2048 + (k % 2) * 512:2176 + (k % 2) * 512],
                                          ACT.Copy), "y1_copied")

            def late_down(k):
                if k == E1:
                    places[:] = late_weights(act, 0, NOV, (E1 - 1) * INNER)
                post(nc.scalar.activation(ov1[:, k % 2, 2, :], w2[:, bass.ds(places[k - E1], INNER)], ACT.Copy), "ov_down_ready")

            silu(0)
            for k in range(1, E1 + NOV):
                silu(k)
                result(k - 1)
                if E1 <= k + 1 < E1 + NOV:
                    late_down(k + 1)
            result(E1 + NOV - 1)
            rows_out(1)
            act.wait_ge(S["top_ready"], 1)
            post(nc.scalar.activation(wtop[:], wtop[:], ACT.Exp), "wtop_exp")

        @block.gpsimd
        def _(pool):
            done(pool, nc.gpsimd.memset(mhalf[:], -0.5), "pool_step")
            nc.gpsimd.memset(zb[:], 0.0).then_inc(S["consts_made"], 1)
            nc.gpsimd.memset(oneb[:], 1.0).then_inc(S["consts_made"], 1)

            def inv_sqrt(p, a, b):
                n = count.get("rstd_ready", 0) + 1
                pool.wait_ge(S["var_ready"], n)
                post(nc.gpsimd.tensor_tensor(rstd[0:p, a:b], rstd[0:p, a:b], mhalf[0:p, a:b], ALU.pow), "rstd_ready")

            nc.gpsimd.memset(B[4][:, NI:], 0.0).then_inc(S["pads_zero"], 1)
            for a, b in TILES4:
                inv_sqrt(PI, a, b)
            if stop == 1:
                return
            pool.wait_ge(S["tok_ps"], 6)
            nc.gpsimd.memset(B5u, 0.0).then_inc(S["upper_ready"], 1)
            for g in (0, 1, 0, 2, 1, 2):
                inv_sqrt(PI, *TILES4[g])
            if stop == 2:
                return
            for a, b in TILES9:
                inv_sqrt(128, a, b)
            pool.wait_ge(S["tab_high"], 1)
            nc.gpsimd.tensor_tensor(tab, tab, tab_hi, ALU.subtract).then_inc(S["tab_rest"], 1)
            pool.wait_ge(S["tab_low"], 1)
            post(nc.gpsimd.tensor_tensor(tab_lo, tab[0:E0, :], tab_lo, ALU.subtract), "tab_split")
            pool.wait_ge(S["in_wd"], 16)
            pool.wait_ge(S["in_wu"], 16)
            pool.wait_ge(S["pairs_ready"], 1)
            at = late_weights(pool, 0, NOV, (E0 - 1) * 128)
            for w, dst in ((wd, ov_wd), (wu, ov_wu)):
                for i in range(NOV):
                    last = nc.gpsimd.tensor_copy(dst[:, i * 128:(i + 1) * 128], w[:, bass.ds(at[i], 128)])
                post(last, "ov0_ready")

            def tile_inv_sqrt(n, i):
                pool.wait_ge(S["tile_var"], n)
                post(nc.gpsimd.tensor_tensor(rstd[:, i:i + 1], rstd[:, i:i + 1], mhalf[:, 0:1], ALU.pow), "tile_rstd")

            def unsort(n0):
                for i in range(NT):
                    tile_inv_sqrt(n0 + i + 1, i)

            unsort(0)
            if stop == 3:
                return

            def one_minus_n(j, h):
                wait_tile(pool, j)("nt_done", 2 * h + 2)
                nc.gpsimd.tensor_tensor(ww[j % 2][:, 4 * h:4 * h + 4, :], C["ident"].unsqueeze(1).to_broadcast([128, 4, 128]),
                                        nt[j % 2][:, 4 * h:4 * h + 4, :], ALU.subtract).then_inc(S["w_done"], 1)

            def gram_masks(j, q):
                wait_tile(pool, j)("grams_copied", q + 1)
                two = slice(2 * q, 2 * q + 2)
                nc.gpsimd.tensor_tensor(ct[j % 2][:, two, :], grams[:, q % 2, :, 0:128],
                                        C["maskC"].unsqueeze(1).to_broadcast([128, 2, 128]), ALU.mult)
                nc.gpsimd.tensor_tensor(smm[j % 2][:, two, :], grams[:, q % 2, :, 128:256],
                                        C["maskS"].unsqueeze(1).to_broadcast([128, 2, 128]), ALU.mult).then_inc(S["masks_done"], 1)

            for j in range(NT + 2):
                if j >= 2:
                    tile_inv_sqrt(NT + 2 * (j - 2) + 1, j - 2)
                if 2 <= j < NT:
                    wait_tile(pool, j - 2)("o_ps", 2)
                if j < NT:
                    gram_masks(j, 0)
                    gram_masks(j, 1)
                    one_minus_n(j, 0)
                if j >= 2:
                    tile_inv_sqrt(NT + 2 * (j - 2) + 2, j - 2)
                if j < NT:
                    gram_masks(j, 2)
                    one_minus_n(j, 1)
                    gram_masks(j, 3)
                    nc.gpsimd.tensor_tensor(hb[:, j % 2, :], HA[:, j, :], R["l1_b"], ALU.add).then_inc(S["hb_ready"], 1)
            if stop > 4:
                pool.wait_ge(S["sh_early_done"], 1)
                pool.wait_ge(S["perm_used"], 2 * NT)
                post(nc.gpsimd.tensor_tensor(HB[:, 0:6, :], HB[:, 0:6, :], sh_early.rearrange("p (t d) -> p t d", d=128), ALU.add),
                     "sh_added")
                unsort(3 * NT)

        @block.vector
        def _(dve):
            def step(ins):
                done(dve, ins, "dve_step")

            def norm(src, dst, p, a, b):
                for i in range(a, b):
                    last = nc.vector.bn_stats(stats[0:p, i, :], src[0:p, i, :])
                step(last)
                for i in range(a, b):
                    last = nc.vector.bn_aggr(mv[0:p, i, :], stats[0:p, i, :])
                step(last)
                post(nc.vector.tensor_scalar(rstd[0:p, a:b], mv[0:p, a:b, 1], EPS, None, ALU.add), "var_ready")
                dve.wait_ge(S["rstd_ready"], count["var_ready"])
                for i in range(a, b):
                    last = nc.vector.tensor_scalar(dst[0:p, i, :], src[0:p, i, :], mv[0:p, i, 0:1], rstd[0:p, i:i + 1],
                                                   ALU.subtract, ALU.mult)
                return last

            def over_tiles(row, p, t):
                return row[0:p, :].unsqueeze(1).to_broadcast([p, t, 128])

            dve.wait_ge(S["in_const"], 64)
            nc.vector.tensor_copy(trib[:], C["triS"]).then_inc(S["consts_made"], 1)
            def shifted_channels(g):
                a, b = TILES4[g]
                dve.wait_ge(S["tok_own"], g + 1)
                own = B[1][:, a * PI:b * PI]
                far = ps[:, (2 * g + 1) * 512:(2 * g + 1) * 512 + (b - a) * PI]
                for q in range(4):
                    p = slice(32 * q, 32 * q + 16)
                    if q < 2:
                        x, y = own[p].rearrange("p (m j) -> p m j", j=6), far[p].rearrange("p (m j) -> p m j", j=6)
                    else:
                        x, y = own[p].rearrange("p (b i) -> p b i", i=36), far[p].rearrange("p (b i) -> p b i", i=36)
                    s1 = 1 if q < 2 else 6
                    if q % 2 == 0:
                        x, y = x[:, :, :-s1], y[:, :, s1:]
                    else:
                        x, y = x[:, :, s1:], y[:, :, :-s1]
                    last = nc.vector.tensor_tensor(x, y, x, ALU.add)
                post(last, "tok_used")

            def token_norm(g):
                a, b = TILES4[g]
                wait_used(dve, JOB["tokT", g])
                step(norm(HA, HA, PI, a, b))
                h = HA[0:PI, a:b, :]
                step(nc.vector.tensor_tensor(h, h, over_tiles(R["tok_g"], PI, b - a), ALU.mult))
                post(nc.vector.tensor_tensor(h, h, over_tiles(R["tok_b"], PI, b - a), ALU.add), "h0_ready")

            def amplitudes_values(g):
                a, b = TILES4[g]
                o = wait_full(dve, "amp", g)
                post(nc.vector.tensor_scalar(B[5][:, a * PI:b * PI], ps[:, o:o + (b - a) * PI], Cc["amp_b"], None, ALU.add), "job_dve")
                o = wait_full(dve, "v", g)
                post(nc.vector.tensor_tensor(HB[0:PI, a:b, :], ps[0:PI, o:o + (b - a) * 128].rearrange("p (t d) -> p t d", d=128),
                                             over_tiles(R["v_b"], PI, b - a), ALU.add), "job_dve")

            shifted_channels(0)
            token_norm(0)
            shifted_channels(1)
            token_norm(1)
            shifted_channels(2)
            token_norm(2)
            if stop == 1:
                dve.wait_ge(S["h0_ready"], 3)
                return
            for g in range(3):
                amplitudes_values(g)
            dve.wait_ge(S["in_wd"], 16)
            step(nc.vector.tensor_reduce(tsum[:], wd.rearrange("p (t h) -> p t h", h=128), X, ALU.add))

            def sign(dst, src, tmp, times):
                step(nc.vector.tensor_scalar(tmp, src, 0.0, times, ALU.is_gt, ALU.mult))
                step(nc.vector.tensor_scalar(src, src, 0.0, times, ALU.is_lt, ALU.mult))
                step(nc.vector.tensor_tensor(dst, tmp, src, ALU.subtract))

            sign(tsig8[:], tsum[:], srow[:], 8.0)
            step(nc.vector.tensor_reduce(csum[:], tsig8[:].rearrange("p (c j) -> p c j", j=8), X, ALU.add))
            sign(small[:, 8:16], csum[:], small[:, 0:8], 8.0 * 4096.0)
            done(dve, nc.vector.tensor_copy(csigb[:].rearrange("p (c j) -> p c j", j=8), small[:, 8:16].unsqueeze(2).to_broadcast([128, 8, 8])), "sig_ready")

            dve.wait_ge(S["ln_ready"], 1)
            step(nc.vector.scalar_tensor_tensor(B[0][:], B[5][:, 0:NI], 0.0, B[0][:], ALU.max, ALU.add))
            for i in range(2):
                wait_used(dve, JOB["w2q" if i else "w2k", 2])
                held = B[3 + i][64:128, 0:NI]
                post(nc.vector.tensor_scalar(held, held, BELOW1, -BELOW1, ALU.min, ALU.max), "phase_held")

            def keys_queries(g):
                a, b = TILES4[g]
                c = slice(a * PI, b * PI)
                for i in range(2):
                    dve.wait_ge(S["sines"], 2 * g + i + 1)
                    last = nc.vector.scalar_tensor_tensor(B[3 + i][:, c], B[0][:, c], 0.1, B[3 + i][:, c], ALU.add, ALU.mult)
                post(last, "kq_ready")

            def retrieval(g):
                a, b = TILES4[g]
                o = wait_full(dve, "score", g)
                post(nc.vector.tensor_tensor(B[5][0:PI, a * PI:b * PI].rearrange("p (t l) -> p t l", l=PI),
                                             ps[0:PI, o:o + (b - a) * PI].rearrange("p (t l) -> p t l", l=PI),
                                             C["maskimg"][0:PI, :].unsqueeze(1).to_broadcast([PI, b - a, PI]), ALU.mult), "job_dve")
                o = wait_full(dve, "retr", g)
                post(nc.vector.tensor_scalar(HB[0:PI, a:b, :], ps[0:PI, o:o + (b - a) * 128].rearrange("p (t d) -> p t d", d=128),
                                             C["invnorm"][0:PI, :], None, ALU.mult), "job_dve")
                wait_used(dve, JOB["retr", g])
                post(norm(HB, HB, PI, a, b), "retr_ready")

            def attention_out(g):
                a, b = TILES4[g]
                h = HA[0:PI, a:b, :]
                o = wait_full(dve, "att", g)
                post(nc.vector.scalar_tensor_tensor(h, h, 2.0, ps[0:PI, o:o + (b - a) * 128].rearrange("p (t d) -> p t d", d=128),
                                                    ALU.mult, ALU.add), "job_dve")
                wait_used(dve, JOB["att", g])
                step(nc.vector.tensor_tensor(h, h, over_tiles(R["out_b"], PI, b - a), ALU.add))
                post(norm(HA, HA, PI, a, b), "h1_ready")

            keys_queries(0)
            keys_queries(1)
            keys_queries(2)
            retrieval(0)
            retrieval(1)
            attention_out(0)
            retrieval(2)
            attention_out(1)
            attention_out(2)
            if stop == 2:
                return
            wait_used(dve, JOB["h1T", 2])
            for g, (a, b) in enumerate(TILES9):
                wait_used(dve, JOB["h1B", g])
                post(norm(HB, HA, 128, a, b), "z1_ready")
            dve.wait_ge(S["key_ps"], 1)
            step(nc.vector.tensor_tensor(key[:], ps[:, 0:NT * E0].rearrange("p (t e) -> p t e", e=E0),
                                         C["keybias"].unsqueeze(1).to_broadcast([128, NT, E0]), ALU.add))
            step(nc.vector.tensor_reduce(kmax[:], key[:], X, ALU.max))
            step(nc.vector.tensor_tensor(oh[:, :, 0, :], key[:], kmax[:].unsqueeze(2).to_broadcast([128, NT, E0]), ALU.is_equal))
            done(dve, nc.vector.tensor_copy(oh[:, :, 1, :], oh[:, :, 0, :]), "oh_ready")
            step(nc.vector.tensor_tensor(key[:], oh[:, :, 0, :], scale_row[:].unsqueeze(1).to_broadcast([128, NT, E0]), ALU.mult))
            step(nc.vector.tensor_reduce(scl[:], key[:], X, ALU.add))

            def perm_to(r, a, b):
                for j in range(a, b):
                    n = r * NT + j
                    if n >= 2:
                        dve.wait_ge(S["perm_used"], n - 1)
                    post(nc.vector.tensor_scalar(B[1 + j % 2][:, 0:N], C["slot"], pos[:, j:j + 1], None, ALU.is_equal), "perm_made")

            def route(E, r, dup, weight):
                M = dup * E
                dve.wait_ge(S["rank_ps"], r + 1)
                done(dve, nc.vector.tensor_copy(small[0:M, 0:1], ps[0:M, 1024:1025]), "cnt_ready")
                dve.wait_ge(S["start_ps"], r + 1)
                step(nc.vector.tensor_copy(small[0:M, 1:2], ps[0:M, 1536:1537]))
                step(nc.vector.tensor_tensor(small[0:M, 2:3], small[0:M, 1:2], small[0:M, 0:1], ALU.add))
                step(nc.vector.tensor_copy(srow[:, 0:E], ps[:, 2048:2048 + E]))
                step(nc.vector.tensor_tensor(rk[:, :, 0:E], ps[:, 0:NT * E].rearrange("p (t e) -> p t e", e=E),
                                             srow[:, 0:E].unsqueeze(1).to_broadcast([128, NT, E]), ALU.add))
                step(nc.vector.tensor_tensor(rk[:, :, 0:E], rk[:, :, 0:E], oh[:, :, 0, 0:E], ALU.mult))
                step(nc.vector.tensor_reduce(pos[:], rk[:, :, 0:E], X, ALU.add))
                perm_to(r, 0, 3)
                step(nc.vector.tensor_scalar(k64[0:E, 0, 0:8], C["tile_end"][0:E, :], small[0:E, 0:1], None, ALU.is_lt, ALU.add,
                                             accum_out=small[0:E, 3:4]))
                step(nc.vector.tensor_scalar(small[0:E, 4:5], small[0:E, 3:4], 128.0, None, ALU.mult))
                done(dve, nc.vector.tensor_scalar(small[0:E, 5:6], small[0:E, 2:3], -128.0, None, ALU.add), "route_cols")
                perm_to(r, 3, 5)
                dve.wait_ge(S["late_ps"], r + 1)
                kc = C["kcol"][0:NOV, :]
                o = 512
                in_k = k64[0:NOV, 0, 0:E]
                step(nc.vector.tensor_scalar(in_k, ps[0:NOV, o:o + E], kc, None, ALU.is_le))
                step(nc.vector.scalar_tensor_tensor(in_k, ps[0:NOV, o + 64:o + 64 + E], kc, in_k, ALU.is_le, ALU.subtract))
                step(nc.vector.scalar_tensor_tensor(k64[0:NOV, 1, 0:E], ps[0:NOV, o + 128:o + 128 + E], C["k128"][0:NOV, :], in_k,
                                                    ALU.subtract, ALU.mult, accum_out=small[0:NOV, 11:12]))
                step(nc.vector.scalar_tensor_tensor(k64[0:NOV, 2, 0:E], C["expert1"][0:NOV, 0:E], 1.0, in_k, ALU.mult, ALU.mult,
                                                    accum_out=small[0:NOV, 12:13]))
                step(nc.vector.tensor_scalar(small[0:NOV, 8:9], small[0:NOV, 12:13], 0.0, float(N), ALU.is_equal, ALU.mult))
                step(nc.vector.tensor_tensor(small[0:NOV, 10:11], small[0:NOV, 11:12], small[0:NOV, 8:9], ALU.add))
                step(nc.vector.tensor_scalar(small[0:NOV, 8:9], small[0:NOV, 12:13], 1.0, 0.0, ALU.subtract, ALU.max))
                done(dve, nc.vector.tensor_scalar(small[0:NOV, 9:10], small[0:NOV, 8:9], float(weight), None, ALU.mult), "pair_cols")
                perm_to(r, 5, NT)
                dve.wait_ge(S["pairs_ps"], r + 1)
                nc.vector.tensor_copy(offs[0:1, 0:E], srow[0:1, 0:E])
                nc.vector.tensor_copy(offs[0:1, E:E + NOV], ps[0:1, 640:640 + NOV])
                done(dve, nc.vector.tensor_copy(ovx[0:1, :], ps[0:1, 512:512 + NOV]), "pairs_ready")
                if r == 0:
                    step(nc.vector.tensor_scalar(ohs[0:M, :], C["slot"][0:M, :], small[0:M, 1:2], None, ALU.is_ge))
                    done(dve, nc.vector.scalar_tensor_tensor(ohs[0:M, :], C["slot"][0:M, :], small[0:M, 2:3], ohs[0:M, :],
                                                             ALU.is_lt, ALU.mult), "slots_ready")

            def make_unperm(r):
                dve.wait_ge(S["posrow_ready"], r + 1)
                for s_ in range(NT):
                    if s_ == NT - 1:
                        dve.wait_ge(S["yT_ps"], r + 1)
                    post(nc.vector.tensor_scalar(unperm[s_], B[3][:, 0:N], C["slotcol"][:, s_:s_ + 1], None, ALU.is_equal), "unperm_made")

            def tile_stats(buf, i):
                step(nc.vector.bn_stats(stats[:, i, :], buf[:, i, :]))
                step(nc.vector.bn_aggr(mv[:, i, :], stats[:, i, :]))
                post(nc.vector.tensor_scalar(rstd[:, i:i + 1], mv[:, i, 1:2], EPS, None, ALU.add), "tile_var")

            def tile_norm(buf, i, n):
                dve.wait_ge(S["tile_rstd"], n)
                return nc.vector.tensor_scalar(buf[:, i, :], buf[:, i, :], mv[:, i, 0:1], rstd[:, i:i + 1], ALU.subtract, ALU.mult)

            def unsort_and_norm(r, n0, name, between=lambda i: None):
                for i in range(NT):
                    dve.wait_ge(S["unsort_ps"], r * NT + i + 1)
                    o = (UNSORT_BANK[r] + i % 3) * 512
                    done(dve, nc.vector.scalar_tensor_tensor(HA[:, i, :], ps[:, o:o + 128], scl[:, i:i + 1], HB[:, i, :],
                                                             ALU.mult, ALU.add), "unsort_used")
                    tile_stats(HA, i)
                    if i:
                        post(tile_norm(HA, i - 1, n0 + i), name)
                    between(i)
                post(tile_norm(HA, NT - 1, n0 + NT), name)

            route(E0, 0, 2, 128)
            def copy_upper(p):
                for g in range(HG):
                    at = window_starts(dve, E0 // 2 + g * GRP, GRP)
                    dve.wait_ge(S["upper_ps"], p * HG + g + 1)
                    for i in range(GRP):
                        o = (2 + g % 2) * 512 + i * 128
                        done(dve, nc.vector.tensor_copy(B5u[:, bass.ds(at[i], 128)], ps[:, o:o + 128]), "upper_copied")
                dve.wait_ge(S["win_copied"], (p * (HG + LG) + HG) * GRP)
                post(nc.vector.copy_predicated(B[5][:, 0:N], upper[:], B5u[:, 0:N]), "merged")

            step(nc.vector.tensor_scalar(upper[:], C["slot"], srow[:, E0 // 2:E0 // 2 + 1], None, ALU.is_ge))
            dve.wait_ge(S["upper_ready"], 1)
            copy_upper(0)
            dve.wait_ge(S["hn_ready"], 1)
            u, lp, cell, fl = B[2][:, 0:N], B[4][:, 0:N], B[0][:, 0:N].bitcast(I32), B[1][:, 0:N]
            step(nc.vector.tensor_scalar(cell, B[5][:, 0:N], float(GRID), None, ALU.mult))
            step(nc.vector.tensor_copy(lp, cell))
            dve.wait_ge(S["u_ready"], 1)
            step(nc.vector.tensor_tensor(fl, lp, u, ALU.is_gt))
            done(dve, nc.vector.tensor_tensor(fl, lp, fl, ALU.subtract), "cell_ready")
            step(nc.vector.scalar_tensor_tensor(lp, fl, float(GRID - 1), u, ALU.min, ALU.subtract))
            dve.wait_ge(S["first_cells"], 3)
            n = 0
            for g in range(1, GRID):
                m = masks[:, g % 2, :]
                dve.wait_ge(S["mask_ready"], g)
                for c in range(3):
                    dve.wait_ge(S["tab_ps"], n + 4)
                    if n >= 3:
                        dve.wait_ge(S["tab_used"], n - 2)
                    o = ((n + 3) % 4) * 1024
                    src = ps[:, o:o + 1024].rearrange("p (v n) -> p v n", v=2)[:, :, 0:384]
                    dst = picked[:, :, c * 384:(c + 1) * 384]
                    post(nc.vector.copy_predicated(dst, m[:, c * 384:(c + 1) * 384].unsqueeze(1).to_broadcast([128, 2, 384]), src), "tab_used")
                    n += 1
            dve.wait_ge(S["tab_used"], n)
            step(nc.vector.tensor_tensor(lp, lp, picked[:, 1, :], ALU.mult))
            done(dve, nc.vector.tensor_tensor(lp, picked[:, 0, :], lp, ALU.subtract), "hs_ready")
            copy_upper(1)
            dve.wait_ge(S["ov0_ready"], 2)
            make_unperm(0)

            def product(j, k):
                v, low = k // 2, k % 2
                if k == 0:
                    wait_tile(dve, j)("relu_done", 1)
                qk = ps[:, QK_BANK * 512:QK_BANK * 512 + 1024].rearrange("p (h e) -> p h e", h=16)
                o = 64 * low
                ins = nc.vector.scalar_tensor_tensor(feat[:, v, :, o:o + 64], qk, 0.0, relus[:, :, o + 1 - v:o + 65 - v],
                                                     ALU.min if low else ALU.max, ALU.mult)
                if k == 3:
                    ins.then_inc(S["prod_done"], 1)

            def between(i):
                if i >= 5:
                    product(0, i - 5)

            dve.wait_ge(S["twice_ready"], 1)
            unsort_and_norm(0, 0, "h2_ready", between if stop > 3 else lambda i: None)
            if stop == 3:
                dve.wait_ge(S["h2_ready"], NT)
                return

            own_steps = [0]

            def own(ins):
                own_steps[0] += 1
                ins.then_inc(S["l1_step"], 1)
                dve.wait_ge(S["l1_step"], own_steps[0])

            def per_head(v, h, n):
                return v[:, 4 * h:4 * h + 4].unsqueeze(2).to_broadcast([128, 4, n])

            def products(j):
                for k in range(4):
                    product(j, k)

            def feature_sums(j, v):
                if v == 0:
                    wait_tile(dve, j)("prod_done", 1)
                return nc.vector.tensor_reduce(sums[:] if v == 0 else srow[:, 0:16], feat[:, v], X, ALU.add, apply_absolute_value=True)

            def head_scales(j):
                hsc = hscs[:, j % 2]
                own(nc.vector.tensor_tensor(sums[:], sums[:], srow[:, 0:16], ALU.add))
                sq, sk = sums[:, 0:8], sums[:, 8:16]
                own(nc.vector.reciprocal(hsc[:, 1, :], sk))
                own(nc.vector.tensor_tensor(hsc[:, 2, :], hsc[:, 1, :], hsc[:, 1, :], ALU.mult))
                nc.vector.tensor_scalar(hsc[:, 3, :], sq, 8.0 * EPS, None, ALU.mult)
                if j == 0:
                    dve.wait_ge(S["beta_done"], 1)
                own(nc.vector.tensor_tensor(hsc[:, 2, :], hsc[:, 2, :], beta[:, j, :], ALU.mult))
                wait_tile(dve, j)("vb_done", 1)
                nc.vector.tensor_tensor(rhs_v[j % 2], vals, sk.unsqueeze(2).to_broadcast([128, NH, 64]), ALU.mult).then_inc(S["rv_done"], 1)

            def gram(j, q):
                wait_tile(dve, j)("grams_copied", q + 1)
                g = bank(GRAM_BANK[q]).rearrange("p (h f) -> p h f", h=2)
                for i in range(2):
                    hd = 2 * q + i
                    last = nc.vector.scalar_tensor_tensor(nt[j % 2][:, hd, :], g[:, i, 0:128], hscs[:, j % 2, 2, hd:hd + 1],
                                                          C["maskN"], ALU.mult, ALU.mult)
                last.then_inc(S["nt_done"], 1)

            def plus_w(j, dst, bank_, h):
                return nc.vector.tensor_tensor(dst[:, 4 * h:4 * h + 4, :], bank(bank_).rearrange("p (h f) -> p h f", h=4),
                                               ww[j % 2][:, 4 * h:4 * h + 4, :], ALU.add)

            def norm_affine(j):
                own(tile_norm(HB, j, NT + 2 * j + 1))
                own(nc.vector.tensor_tensor(HB[:, j, :], HB[:, j, :], R["l1_g"], ALU.mult))
                dve.wait_ge(S["hb_ready"], j + 1)
                own(nc.vector.tensor_tensor(HB[:, j, :], HB[:, j, :], hb[:, j % 2, :], ALU.add))
                tile_stats(HB, j)

            feature_sums(0, 0)
            own(feature_sums(0, 1))
            head_scales(0)
            for q in range(4):
                gram(0, q)
            for j in range(NT):
                f = j + 1
                w = wait_tile(dve, j)
                hsc = hscs[:, j % 2]
                if f < NT:
                    products(f)
                for h in range(2):
                    w("a_ps", h + 1)
                    plus_w(j, ww[j % 2], A_BANK[h][0], h).then_inc(S["a_done"], 1)
                for h in range(2):
                    w("x_ps", h + 1)
                    if h == 0:
                        w("a_done", 2)
                    plus_w(j, nn, X_BANK[h], h).then_inc(S["x8_done"], 1)
                if f < NT:
                    feature_sums(f, 0)
                nc.vector.tensor_copy(delta[:, :, 64], hsc[:, 1, :])
                for h in range(2):
                    w("m_ps", h + 1)
                    nc.vector.tensor_tensor(below_T[:, 4 * h:4 * h + 4, :], bank(M_BANK[h]).rearrange("p (h f) -> p h f", h=4),
                                            per_head(hsc[:, 2, :], h, 128), ALU.mult).then_inc(S["m_done"], 1)
                if f < NT:
                    own(feature_sums(f, 1))
                    head_scales(f)
                    gram(f, 0)
                for r in range(3):
                    for h in range(2):
                        w("t_ps", 2 * r + h + 1)
                        if r == 0:
                            w("e_done", h + 1)
                        nc.vector.tensor_tensor(delta[:, 4 * h:4 * h + 4, 0:64], first[:, 4 * h:4 * h + 4, :],
                                                bank(T_BANK[2 * r + h], 256).rearrange("p (h e) -> p h e", h=4),
                                                ALU.subtract).then_inc(S["d_done"], 1)
                    if f < NT and r < 2:
                        gram(f, r + 1)
                    if j and r == 0:
                        norm_affine(j - 1)
                    if j and r == 1:
                        post(tile_norm(HB, j - 1, NT + 2 * j), "h3_ready")
                w("d_done", 6)
                nc.vector.tensor_tensor(delta[:, :, 0:64], delta[:, :, 0:64], hsc[:, 2, :].unsqueeze(2).to_broadcast([128, NH, 64]),
                                        ALU.mult).then_inc(S["scales_done"], 1)
                if f < NT:
                    gram(f, 3)
                for h in range(2):
                    w("o_ps", h + 1)
                    o = bank(O_BANK[h], 260).rearrange("p (h e) -> p h e", h=4)
                    hs_ = slice(4 * h, 4 * h + 4)
                    own(nc.vector.scalar_tensor_tensor(hsc[:, 4, hs_], o[:, :, 64], 8.0, hsc[:, 3, hs_], ALU.mult, ALU.add))
                    own(nc.vector.reciprocal(hsc[:, 5, hs_], hsc[:, 4, hs_]))
                    nc.vector.tensor_tensor(outs[:, hs_, :], o[:, :, 0:64], per_head(hsc[:, 5, :], h, 64), ALU.mult).then_inc(S["o_done"], 1)
                w("y_ps", 1)
                nc.vector.tensor_tensor(HB[:, j, :], bank(Y_BANK, 128), HA[:, j, :], ALU.add).then_inc(S["y_done"], 1)
                w("y_done", 1)
                tile_stats(HB, j)

            norm_affine(NT - 1)
            done(dve, tile_norm(HB, NT - 1, 3 * NT), "h3_ready")
            if stop == 4:
                return
            dve.wait_ge(S["gate_ps"], 2)
            lg = key[:, :, 0:E1]
            step(nc.vector.tensor_copy(lg, ps[:, 3584:3584 + NT * E1].rearrange("p (t e) -> p t e", e=E1)))
            step(nc.vector.tensor_reduce(kmax[:], lg, X, ALU.max))
            done(dve, nc.vector.tensor_tensor(wtop[:], kmax[:], kmax[:], ALU.subtract), "top_ready")
            step(nc.vector.tensor_tensor(lg, lg, kmax[:].unsqueeze(2).to_broadcast([128, NT, E1]), ALU.is_equal))
            step(nc.vector.tensor_tensor(lg, lg, C["prefer"].unsqueeze(1).to_broadcast([128, NT, E1]), ALU.mult))
            step(nc.vector.tensor_reduce(kmax[:], lg, X, ALU.max))
            done(dve, nc.vector.tensor_tensor(oh[:, :, 0, 0:E1], lg, kmax[:].unsqueeze(2).to_broadcast([128, NT, E1]), ALU.is_equal), "oh_ready")
            route(E1, 1, 1, INNER)
            dve.wait_ge(S["in_ffn"], 48)
            dve.wait_ge(S["in_ffn2"], 32)
            places = late_weights(dve, 0, NOV, (E1 - 1) * INNER)
            for k in range(E1 + NOV):
                if E1 <= k + 1 < E1 + NOV:
                    dve.wait_ge(S["up_ps"], k)
                    for v, w in enumerate((w1, w3)):
                        last = nc.vector.tensor_copy(ov1[:, (k + 1) % 2, v, :], w[:, bass.ds(places[k + 1 - E1], INNER)])
                    post(last, "ov_up_ready")
                dve.wait_ge(S["silu_done"], k + 1)
                if k >= 2:
                    dve.wait_ge(S["y1_ps"], k - 1)
                post(nc.vector.tensor_tensor(gg[:, k % 2, :], ps[:, (k % 2) * 1024 + 512:(k % 2) * 1024 + 1024], sg[:, k % 2, :],
                                             ALU.mult), "g_done")
            make_unperm(1)
            dve.wait_ge(S["wtop_exp"], 1)
            step(nc.vector.reciprocal(scl[:], wtop[:]))
            step(nc.vector.tensor_tensor(scl[:], scl[:], wtop[:], ALU.mult))
            dve.wait_ge(S["sh_ps"], 1)
            step(nc.vector.tensor_tensor(HB[:, 6:NT, :], ps[:, 0:384].rearrange("p (t d) -> p t d", d=128), HB[:, 6:NT, :], ALU.add))
            dve.wait_ge(S["sh_added"], 1)
            unsort_and_norm(1, 3 * NT, "y_final")


def pack(a):
    import numpy as np
    f = np.float32
    o = {}
    def patch_pixels(v):
        v = v.reshape(-1, 3, 2, 8, 2, 8).transpose(0, 2, 4, 1, 3, 5)
        return v.reshape(len(v), 768)

    def chunks(v):
        return v.T.reshape(KC, 128, -1).transpose(1, 0, 2)

    x = a["x"].reshape(NIMG, 3, 6, 16, 6, 16).transpose(0, 2, 4, 1, 3, 5).reshape(-1, 3, 16, 16)
    v = np.zeros((NI, 768), f)
    v[:NIMG * NPATCH] = patch_pixels(x)
    o["patches"] = chunks(v)

    wm, wx, wy = (a[n].reshape(-1, 3, 16, 16) for n in ("L0_tok_W_main", "L0_tok_W_sx", "L0_tok_W_sy"))
    w = np.zeros((2, 4, 2, 16, 3, 16, 16), f)
    w[0, :, 1] = wm.reshape(4, 16, 3, 16, 16)
    w[0, 0, 0, ..., 8:] = wx[..., :8]
    w[1, 0, 0, ..., :8] = wx[..., 8:]
    w[0, 1, 0, ..., :8] = wx[..., 8:]
    w[1, 1, 0, ..., 8:] = wx[..., :8]
    w[0, 2, 0, :, :, 8:] = wy[:, :, :8]
    w[1, 2, 0, :, :, :8] = wy[:, :, 8:]
    w[0, 3, 0, :, :, :8] = wy[:, :, 8:]
    w[1, 3, 0, :, :, 8:] = wy[:, :, :8]
    o["tokw"] = chunks(patch_pixels(w)).reshape(128, -1)
    bm, bx, by = (a[n].reshape(-1, 16) for n in ("L0_tok_b_main", "L0_tok_b_sx", "L0_tok_b_sy"))
    bs = np.concatenate([bx, bx, by, by])
    rows = {"tok_g": a["L0_tok_ln_g"], "tok_b": a["L0_tok_ln_b"], "v_b": a["L0_attn_v_b"], "out_b": a["L0_attn_out_b"],
            "l1_g": a["L1_attn_ln_g"], "l1_b": a["L1_attn_ln_b"]}
    o["rows"] = np.concatenate([rows[n] for n in ROWS])
    two = lambda v: np.concatenate([v, v], axis=-1)
    cols = {"tok_bias": np.stack([bs, bm], axis=1).reshape(-1), "ke_b1": a["L0_attn_ke_b1"], "qe_b1": a["L0_attn_qe_b1"], "ke_b2": two(a["L0_attn_ke_b2"]),
            "qe_b2": two(a["L0_attn_qe_b2"]), "amp_b": two(a["L0_attn_amp_b"]), "ln_g": a["L0_attn_ln_g"],
            "ln_b": a["L0_attn_ln_b"], "gamma": a["L0_ffn_gamma"], "beta": a["L0_ffn_beta"]}
    o["cols"] = np.stack([cols[n] for n in COLS], axis=1)
    o["scale"] = a["L0_ffn_scale"]
    o["attw"] = np.concatenate([a["L0_attn_ke_w1"], a["L0_attn_qe_w1"], two(a["L0_attn_ke_w2"]), two(a["L0_attn_qe_w2"]),
                                two(a["L0_attn_amp_w"]), a["L0_attn_v_w"], a["L0_attn_out_w"]], axis=1)
    o["wd"] = a["L0_ffn_Wd"].transpose(2, 0, 1).reshape(128, -1)
    o["wu"] = a["L0_ffn_Wu"].transpose(2, 0, 1).reshape(128, -1)
    tab = np.stack([a["L0_ffn_spline_bases"], a["L0_ffn_spline_slopes"]], axis=0)
    o["tab"] = tab.transpose(1, 3, 0, 2).reshape(E0, -1)
    w = a["L1_attn_W_qkvb"].reshape(NH, 3 * HD + 1, 128)
    o["qkvw"] = np.concatenate([w[:, i * HD:(i + 1) * HD].reshape(NH * HD, 128) for i in range(3)] + [w[:, 3 * HD]], axis=0).T
    o["wo"] = a["L1_attn_W_o"].T.reshape(4, 128, 128).transpose(1, 0, 2).reshape(128, -1)
    o["gate"] = a["L1_ffn_gate_w"].T
    o["w1"] = a["L1_ffn_w1"].transpose(2, 0, 1).reshape(128, -1)
    o["w3"] = a["L1_ffn_w3"].transpose(2, 0, 1).reshape(128, -1)
    o["w2"] = a["L1_ffn_w2"].reshape(E1, 128, 4, 128).transpose(3, 0, 2, 1).reshape(128, -1)
    o["sw1"] = a["L1_ffn_sw1"].T
    o["sw2"] = a["L1_ffn_sw2"].reshape(128, 4, 128).transpose(2, 1, 0).reshape(128, -1)

    c = {}
    i, j = np.arange(128)[:, None], np.arange(128)[None, :]
    c["ident"] = i == j
    c["maskimg"] = ((i // NPATCH == j // NPATCH) & (i <= j) & (i < PI))[:, :PI]
    c["maskN"] = (i // 8 == j // 8) & (i < j)
    c["maskC"] = (i // 32 == j // 32) & (i // 8 > j // 8)
    c["maskS"] = (i // 32 == j // 32) & (i <= j)
    c["triS"] = i < j
    c["triI"] = i <= j
    c["slot"] = np.broadcast_to(np.arange(N), (128, N))
    c["tile_end"] = np.broadcast_to(np.arange(1, 9) * 128, (128, 8))
    c["expert1"] = np.broadcast_to(np.arange(1, E0 + 1), (128, E0))
    c["invnorm"] = 1.0 / np.sqrt((np.arange(128) % NPATCH + 1) * 64.0)[:, None]
    c["sin_scale"] = np.where(i < 64, -PI32, PI32)
    c["sin_bias"] = np.where(i < 64, PI32 / 2, 0.0)
    c["kcol"] = i
    c["from_cell"] = np.broadcast_to(1.0 - np.arange(GRID), (128, GRID))
    c["k128"] = i * 128
    c["one"] = i * 0 + 1
    c["slotcol"] = np.arange(NT)[None, :] * 128 + i
    e = np.arange(E0)
    c["keybias"] = np.broadcast_to(-4096.0 * (e // 8) - e % 8, (128, E0))
    c["prefer"] = np.broadcast_to(8.0 - np.arange(E1), (128, E1))
    o["consts"] = np.concatenate([np.asarray(c[n], f) for n, _ in CONST], axis=1)
    return {k: np.ascontiguousarray(v, f) for k, v in o.items()}


def kernel(**inputs):
    import numpy as np
    from concourse import bacc
    from concourse.bass_utils import run_bass_kernel_spmd

    packed = pack({k: np.asarray(v) for k, v in inputs.items()})
    nc = bacc.Bacc("TRN2", target_bir_lowering=False, num_devices=1)
    A = {k: nc.dram_tensor(f"in_{k}", v.shape, F32, kind="ExternalInput").ap() for k, v in packed.items()}
    out = nc.dram_tensor("out", (128, NT, 128), F32, kind="ExternalOutput").ap()
    vit_kernel(nc, A, out)
    got = run_bass_kernel_spmd(nc, [{f"in_{k}": v for k, v in packed.items()}], core_ids=[0]).results[0]["out"]
    return np.ascontiguousarray(got.reshape(4, NIMG, NT, D).transpose(1, 2, 0, 3).reshape(NIMG, NPATCH, D))
```
